# Optimizing a Trainium2 kernel written in Bass

```python
import numpy as np
import jax
import jax.numpy as jnp

def _softmax(x, axis=-1):
    return jax.nn.softmax(x, axis=axis)

def _gelu(x):
    return jax.nn.gelu(x, approximate=True)

def _silu(x):
    return jax.nn.silu(x)

def _sigmoid(x):
    return jax.nn.sigmoid(x)

def _layernorm(x, axis=-1, eps=1e-05):
    m = jnp.mean(x, axis=axis, keepdims=True)
    v = jnp.var(x, axis=axis, keepdims=True)
    return (x - m) / jnp.sqrt(v + eps)

def _scatter_add(tgt, idx, src, axis=0):
    return tgt.at[idx].add(src)

def _segment_sum(src, seg, n):
    return jax.ops.segment_sum(src, seg, n)
kernel_name = 'mk_audio_tower_d1_tok_audfeat2048_r4_1ef639'

def setup_inputs(seed: int=0):
    np.random.seed(seed)
    _w = jnp.asarray

    def _rec_inputs():
        import jax
        import jax.numpy as jnp
        _rk = jax.random.key(seed)
        x = -0.000392918 + 0.999932 * jax.random.normal(jax.random.fold_in(_rk, 1), (64, 375, 64), jnp.float32)
        return x
    x = _rec_inputs()

    def _L0_tok_setup():
        import jax, jax.numpy as jnp
        import numpy as np
        TIN = 16
        FEAT = 64
        IN_DIM = TIN * FEAT
        HDIM = 512
        EPS = 1e-06

        def layer_norm(x, gamma, beta, eps):
            mu = jnp.mean(x, axis=-1, keepdims=True)
            var = jnp.mean(jnp.square(x - mu), axis=-1, keepdims=True)
            return (x - mu) * jax.lax.rsqrt(var + eps) * gamma + beta
        key = jax.random.key(seed)
        ks = jax.random.split(key, 4)
        x = jax.random.normal(ks[0], (64, 1024, FEAT), dtype=jnp.float32)
        W = jax.random.normal(ks[1], (IN_DIM, HDIM), dtype=jnp.float32) / np.sqrt(IN_DIM)
        b = jnp.zeros((HDIM,), dtype=jnp.float32)
        g1 = jnp.ones((IN_DIM,), dtype=jnp.float32)
        b1 = jnp.zeros((IN_DIM,), dtype=jnp.float32)
        g2 = jnp.ones((HDIM,), dtype=jnp.float32)
        b2 = jnp.zeros((HDIM,), dtype=jnp.float32)
        return {'x': x, 'W': W, 'b': b, 'g1': g1, 'b1': b1, 'g2': g2, 'b2': b2}
    _L0_tok_all = _L0_tok_setup()
    _L0_tok_in = {k: v for k, v in _L0_tok_all.items() if k in ('W', 'b', 'g1', 'b1', 'g2', 'b2')}
    del _L0_tok_all

    def _L0_attn_setup():
        import jax, jax.numpy as jnp
        import numpy as np
        D, NC, DS = (512, 2, 16)
        B, L = (2, 128)

        def _rmsnorm(x, w):
            eps = jnp.asarray(jnp.finfo(x.dtype).eps, x.dtype)
            ms = jnp.mean(jnp.square(x), axis=-1, keepdims=True)
            return x * jax.lax.rsqrt(ms + eps) * w

        def _reference_tuple_inner(x, W_in, W_out, A_theta, B_real, B_imag, C_real, C_imag, norm_w):
            b, l, _ = x.shape
            xi = (x @ W_in.T).reshape(b, l, NC, D)[..., None]
            ct = jnp.cos(A_theta)
            st = jnp.sin(A_theta)
            rs = jnp.zeros((b, l, NC, D, DS), dtype=x.dtype)
            is_ = jnp.zeros_like(rs)
            bxr = B_real * xi
            bxi = B_imag * xi
            nr = ct * rs - st * is_ + bxr
            ni = st * rs + ct * is_ + bxi
            y = jnp.sum(C_real * nr - C_imag * ni, axis=-1)
            out = y.reshape(b, l, NC * D) @ W_out.T
            return (x + _rmsnorm(out, norm_w), nr, ni)
        key = jax.random.key(seed)
        ks = jax.random.split(key, 9)
        x = jax.random.normal(ks[0], (B, L, D), dtype=jnp.float32)
        W_in = jax.random.normal(ks[1], (NC * D, D), dtype=jnp.float32) * 0.02
        W_out = jax.random.normal(ks[2], (D, NC * D), dtype=jnp.float32) * 0.02
        A_theta = jax.random.normal(ks[3], (NC, D, DS), dtype=jnp.float32) * 0.1
        B_real = jax.random.normal(ks[4], (NC, D, DS), dtype=jnp.float32) * 0.1
        B_imag = jax.random.normal(ks[5], (NC, D, DS), dtype=jnp.float32) * 0.1
        C_real = jax.random.normal(ks[6], (NC, D, DS), dtype=jnp.float32) * 0.1
        C_imag = jax.random.normal(ks[7], (NC, D, DS), dtype=jnp.float32) * 0.1
        norm_w = jnp.ones((D,), dtype=jnp.float32)
        return {'x': x, 'W_in': W_in, 'W_out': W_out, 'A_theta': A_theta, 'B_real': B_real, 'B_imag': B_imag, 'C_real': C_real, 'C_imag': C_imag, 'norm_w': norm_w}
    _L0_attn_all = _L0_attn_setup()
    _L0_attn_in = {k: v for k, v in _L0_attn_all.items() if k in ('W_in', 'W_out', 'A_theta', 'B_real', 'B_imag', 'C_real', 'C_imag', 'norm_w')}
    del _L0_attn_all

    def _L0_ffn_setup():
        import jax, jax.numpy as jnp
        import numpy as np
        B, S, H = (2, 256, 512)
        I = 256
        E = 32
        Z = 32
        K = 8
        SCALE = 1.5
        CAP = 256
        EPS = 1e-20

        def _moe_forward(x, w_cls, bias, w_gate_up, w_down):
            T = x.shape[0] * x.shape[1]
            xf = x.reshape(T, H)
            logits = xf.astype(jnp.float32) @ w_cls.T
            scores = jax.nn.softmax(logits, axis=-1)
            _, topk_idx = jax.lax.top_k(scores + bias[None, :], K)
            w = jnp.take_along_axis(scores, topk_idx, axis=-1)
            w = w / (w.sum(-1, keepdims=True) + EPS) * SCALE
            routed = topk_idx < E
            w_r = jnp.where(routed, w, 0.0)
            w_z = jnp.where(routed, 0.0, w)
            N = T * K
            flat_ids = jnp.where(routed, topk_idx, E).reshape(-1)
            x_exp = jnp.repeat(xf, K, axis=0)
            order = jnp.argsort(flat_ids)
            ids_s = flat_ids[order]
            counts = jax.ops.segment_sum(jnp.ones(N, jnp.int32), flat_ids, num_segments=E + 1)
            starts = jnp.cumsum(counts) - counts
            pos = jnp.arange(N) - starts[ids_s]
            buf = jnp.zeros((E, CAP, H), xf.dtype).at[ids_s, pos].set(x_exp[order], mode='drop')
            gu = jnp.einsum('ech,ehf->ecf', buf, w_gate_up)
            g, u = jnp.split(gu, 2, axis=-1)
            act = jax.nn.silu(g) * u
            y = jnp.einsum('eci,eih->ech', act, w_down)
            valid = (ids_s < E) & (pos < CAP)
            y_tok = jnp.where(valid[:, None], y[jnp.clip(ids_s, 0, E - 1), jnp.clip(pos, 0, CAP - 1)], 0.0)
            y_exp = jnp.zeros((N, H), xf.dtype).at[order].set(y_tok).reshape(T, K, H)
            routed_out = jnp.einsum('tk,tkh->th', w_r, y_exp)
            out = routed_out * (1.0 + w_z.sum(-1, keepdims=True))
            return out.reshape(x.shape)
        key = jax.random.key(seed)
        ks = jax.random.split(key, 5)
        x = jax.random.normal(ks[0], (B, S, H), jnp.float32)
        w_cls = jax.random.normal(ks[1], (E + Z, H), jnp.float32) / np.float32(np.sqrt(H))
        bias = jax.random.normal(ks[2], (E + Z,), jnp.float32) * 0.02
        w_gate_up = jax.random.normal(ks[3], (E, H, 2 * I), jnp.float32) * 0.02
        w_down = jax.random.normal(ks[4], (E, I, H), jnp.float32) * 0.02
        return {'x': x, 'w_cls': w_cls, 'bias': bias, 'w_gate_up': w_gate_up, 'w_down': w_down}
    _L0_ffn_all = _L0_ffn_setup()
    _L0_ffn_in = {k: v for k, v in _L0_ffn_all.items() if k in ('w_cls', 'bias', 'w_gate_up', 'w_down')}
    del _L0_ffn_all
    return {'x': x, 'L0_tok_W': _L0_tok_in['W'], 'L0_tok_b': _L0_tok_in['b'], 'L0_tok_g1': _L0_tok_in['g1'], 'L0_tok_b1': _L0_tok_in['b1'], 'L0_tok_g2': _L0_tok_in['g2'], 'L0_tok_b2': _L0_tok_in['b2'], 'L0_attn_W_in': _L0_attn_in['W_in'], 'L0_attn_W_out': _L0_attn_in['W_out'], 'L0_attn_A_theta': _L0_attn_in['A_theta'], 'L0_attn_B_real': _L0_attn_in['B_real'], 'L0_attn_B_imag': _L0_attn_in['B_imag'], 'L0_attn_C_real': _L0_attn_in['C_real'], 'L0_attn_C_imag': _L0_attn_in['C_imag'], 'L0_attn_norm_w': _L0_attn_in['norm_w'], 'L0_ffn_w_cls': _L0_ffn_in['w_cls'], 'L0_ffn_bias': _L0_ffn_in['bias'], 'L0_ffn_w_gate_up': _L0_ffn_in['w_gate_up'], 'L0_ffn_w_down': _L0_ffn_in['w_down']}

def reference(x, L0_tok_W, L0_tok_b, L0_tok_g1, L0_tok_b1, L0_tok_g2, L0_tok_b2, L0_attn_W_in, L0_attn_W_out, L0_attn_A_theta, L0_attn_B_real, L0_attn_B_imag, L0_attn_C_real, L0_attn_C_imag, L0_attn_norm_w, L0_ffn_w_cls, L0_ffn_bias, L0_ffn_w_gate_up, L0_ffn_w_down):
    import jax
    import jax.numpy as jnp

    def _L0_tok_ref(x, W, b, g1, b1, g2, b2):
        import jax, jax.numpy as jnp
        import numpy as np
        TIN = 16
        FEAT = 64
        IN_DIM = TIN * FEAT
        HDIM = 512
        EPS = 1e-06

        def layer_norm(x, gamma, beta, eps):
            mu = jnp.mean(x, axis=-1, keepdims=True)
            var = jnp.mean(jnp.square(x - mu), axis=-1, keepdims=True)
            return (x - mu) * jax.lax.rsqrt(var + eps) * gamma + beta
        bsz, T, F = x.shape
        n_patch = T // TIN
        x = x[:, :n_patch * TIN, :].reshape(bsz, n_patch, TIN * F)
        x = layer_norm(x, g1, b1, EPS)
        x = jnp.einsum('bpd,dh->bph', x, W) + b
        return layer_norm(x, g2, b2, EPS)

    def _L0_attn_ref(x, W_in, W_out, A_theta, B_real, B_imag, C_real, C_imag, norm_w):
        import jax, jax.numpy as jnp
        import numpy as np
        D, NC, DS = (512, 2, 16)
        B, L = (2, 128)

        def _rmsnorm(x, w):
            eps = jnp.asarray(jnp.finfo(x.dtype).eps, x.dtype)
            ms = jnp.mean(jnp.square(x), axis=-1, keepdims=True)
            return x * jax.lax.rsqrt(ms + eps) * w

        def _reference_tuple_inner(x, W_in, W_out, A_theta, B_real, B_imag, C_real, C_imag, norm_w):
            b, l, _ = x.shape
            xi = (x @ W_in.T).reshape(b, l, NC, D)[..., None]
            ct = jnp.cos(A_theta)
            st = jnp.sin(A_theta)
            rs = jnp.zeros((b, l, NC, D, DS), dtype=x.dtype)
            is_ = jnp.zeros_like(rs)
            bxr = B_real * xi
            bxi = B_imag * xi
            nr = ct * rs - st * is_ + bxr
            ni = st * rs + ct * is_ + bxi
            y = jnp.sum(C_real * nr - C_imag * ni, axis=-1)
            out = y.reshape(b, l, NC * D) @ W_out.T
            return (x + _rmsnorm(out, norm_w), nr, ni)
        return _reference_tuple_inner(x, W_in, W_out, A_theta, B_real, B_imag, C_real, C_imag, norm_w)[0]

    def _L0_ffn_ref(x, w_cls, bias, w_gate_up, w_down):
        import jax, jax.numpy as jnp
        import numpy as np
        B, S, H = (2, 256, 512)
        I = 256
        E = 32
        Z = 32
        K = 8
        SCALE = 1.5
        CAP = 256
        EPS = 1e-20

        def _moe_forward(x, w_cls, bias, w_gate_up, w_down):
            T = x.shape[0] * x.shape[1]
            xf = x.reshape(T, H)
            logits = xf.astype(jnp.float32) @ w_cls.T
            scores = jax.nn.softmax(logits, axis=-1)
            _, topk_idx = jax.lax.top_k(scores + bias[None, :], K)
            w = jnp.take_along_axis(scores, topk_idx, axis=-1)
            w = w / (w.sum(-1, keepdims=True) + EPS) * SCALE
            routed = topk_idx < E
            w_r = jnp.where(routed, w, 0.0)
            w_z = jnp.where(routed, 0.0, w)
            N = T * K
            flat_ids = jnp.where(routed, topk_idx, E).reshape(-1)
            x_exp = jnp.repeat(xf, K, axis=0)
            order = jnp.argsort(flat_ids)
            ids_s = flat_ids[order]
            counts = jax.ops.segment_sum(jnp.ones(N, jnp.int32), flat_ids, num_segments=E + 1)
            starts = jnp.cumsum(counts) - counts
            pos = jnp.arange(N) - starts[ids_s]
            buf = jnp.zeros((E, CAP, H), xf.dtype).at[ids_s, pos].set(x_exp[order], mode='drop')
            gu = jnp.einsum('ech,ehf->ecf', buf, w_gate_up)
            g, u = jnp.split(gu, 2, axis=-1)
            act = jax.nn.silu(g) * u
            y = jnp.einsum('eci,eih->ech', act, w_down)
            valid = (ids_s < E) & (pos < CAP)
            y_tok = jnp.where(valid[:, None], y[jnp.clip(ids_s, 0, E - 1), jnp.clip(pos, 0, CAP - 1)], 0.0)
            y_exp = jnp.zeros((N, H), xf.dtype).at[order].set(y_tok).reshape(T, K, H)
            routed_out = jnp.einsum('tk,tkh->th', w_r, y_exp)
            out = routed_out * (1.0 + w_z.sum(-1, keepdims=True))
            return out.reshape(x.shape)
        return _moe_forward(x, w_cls, bias, w_gate_up, w_down)
    h = _L0_tok_ref(x, L0_tok_W, L0_tok_b, L0_tok_g1, L0_tok_b1, L0_tok_g2, L0_tok_b2)
    h = h + _L0_attn_ref(_layernorm(h, axis=-1), L0_attn_W_in, L0_attn_W_out, L0_attn_A_theta, L0_attn_B_real, L0_attn_B_imag, L0_attn_C_real, L0_attn_C_imag, L0_attn_norm_w)
    h = h + _L0_ffn_ref(_layernorm(h, axis=-1), L0_ffn_w_cls, L0_ffn_bias, L0_ffn_w_gate_up, L0_ffn_w_down)
    return h

_drawn_inputs = setup_inputs


def setup_inputs(seed=0):
    import zlib

    import numpy as np

    out = dict(_drawn_inputs(seed))
    spreads = {'L0_tok_b': (0.0, 0.1),
     'L0_tok_g1': (1.0, 0.2),
     'L0_tok_b1': (0.0, 0.1),
     'L0_tok_g2': (1.0, 0.2),
     'L0_tok_b2': (0.0, 0.1),
     'L0_attn_norm_w': (1.0, 0.2)}
    factors = {'L0_ffn_w_cls': 5.613,
     'L0_ffn_bias': 8.0,
     'L0_ffn_w_gate_up': 5.346,
     'L0_ffn_w_down': 5.338}
    for name, (base, spread) in spreads.items():
        noise = np.random.default_rng([zlib.crc32(name.encode()), seed]).standard_normal(out[name].shape)
        drawn = base * np.exp(spread * noise) if base else spread * noise
        out[name] = jnp.asarray(drawn.astype(out[name].dtype))
    for name, factor in factors.items():
        out[name] = (out[name] * factor).astype(out[name].dtype)
    return out
```

```python
from contextlib import ExitStack

import concourse.bass as bass
from concourse import mybir

F32 = mybir.dt.float32
BF16 = mybir.dt.bfloat16
F16 = mybir.dt.float16
I32 = mybir.dt.int32
U32 = mybir.dt.uint32
ALU = mybir.AluOpType
ACT = mybir.ActivationFunctionType
AX = mybir.AxisListType

P = 128
PI = 3.1415925


class Step:

    def __init__(self, i, off, unroll):
        self.i, self.off, self.unroll = i, off, unroll

    def __add__(self, k):
        return Step(self.i, self.off + k, self.unroll)

    @property
    def n(self):
        return self.off if isinstance(self.i, int) else self.i * self.unroll + self.off

    def slot(self, ring):
        return self.off % ring

    def turn(self, ring):
        here = self.off // ring
        return here if isinstance(self.i, int) else self.i * (self.unroll // ring) + here


def wait(eng, sem, value):
    if not isinstance(value, int) or value > 0:
        eng.wait_ge(sem, value)


class Links:

    def __init__(self, eng, sem, before):
        self.eng, self.sem, self.before, self.n = eng, sem, before, 0

    def __call__(self, instruction):
        self.n += 1
        instruction.then_inc(self.sem, 1)
        self.eng.wait_ge(self.sem, self.before + self.n)


def audio_tower(nc, x, W, b, g1, b1, g2, b2, W_in, W_out, A_theta, B_real, B_imag, C_real, C_imag,
                norm_w, w_cls, route_bias, w_gate_up, w_down, out):
    BATCH, TIME, FEAT = x.shape
    DIN, D = W.shape
    TIN = DIN // FEAT
    NPATCH = TIME // TIN
    T = BATCH * NPATCH
    BPT = P // NPATCH
    R = BPT * NPATCH
    TILES = -(-BATCH // BPT)
    BLAST = BATCH - (TILES - 1) * BPT
    RLAST = BLAST * NPATCH
    KX = DIN // P
    KD = D // P
    NS = W_in.shape[0]
    KS = NS // P
    DS = A_theta.shape[2]
    NE2 = w_cls.shape[0]
    E = w_gate_up.shape[0]
    I = w_down.shape[1]
    KI = I // P
    CAP = 256
    HALVES = CAP // P
    LO = 16
    HI = CAP // LO
    EG = P // HI
    GROUPS = E // EG
    SCALE = 1.5
    ROW = D + E
    RING = 4

    x_rows = x[:, 0:NPATCH * TIN, :].rearrange("b (n t) f -> b n (t f)", t=TIN)
    xf_d = nc.dram_tensor("token_rows", (T, ROW), F32).ap()
    acc_d = nc.dram_tensor("sums", (T + P, D), F32).ap()
    tbl_d = nc.dram_tensor("slot_table", (E * CAP,), F32).ap()
    out_d = out.rearrange("b n d -> (b n) d")

    ctx = ExitStack()
    with ctx:
        def sb(name, shape, dt=F32):
            return ctx.enter_context(nc.sbuf_tensor(name, shape, dt))

        def sem(name):
            return ctx.enter_context(nc.semaphore(name))

        bank = [ctx.enter_context(nc.psum_tensor(f"bank{i}", [P, 512], F32)) for i in range(8)]
        p_xT = [bank[0], bank[1]]
        p_tok, p_xnT, p_attn, p_xfT, p_logits, p_table = bank[2:8]
        p_pos = p_xfT[:, KD * R:KD * R + E]
        p_woT = [p_logits, p_table]
        p_m = [p_attn, p_xfT]
        p_gu, p_xeT, p_y, p_actT = [bank[0], bank[1]], [bank[2], bank[3]], [bank[4], bank[6]], [bank[5], bank[7]]

        ident = sb("ident", [P, P])
        before = sb("before", [P, P], BF16)
        ones = sb("ones", [P, P], BF16)
        same_i, same_expert = sb("same_i", [P, EG], I32), sb("same_expert", [P, EG])
        iota_lo = sb("iota_lo", [P, GROUPS, LO, EG], F16)
        iota_hi1 = sb("iota_hi1", [P, GROUPS, HI, EG], F16)
        iota_e = sb("iota_e", [1, E])
        iota_e1 = sb("iota_e1", [1, E])
        ones_e = sb("ones_e", [1, E])
        token_id = sb("token_id", [P, 1])
        spare_row = sb("spare_row", [P, 1])
        zero_row = sb("zero_row", [P, D])
        zero_16 = sb("zero_16", [P, D], F16)
        w_tok = sb("w_tok", [P, KX, D])
        g1_all, b1_all = sb("g1_all", [P, DIN]), sb("b1_all", [P, DIN])
        b_all, g2_all, b2_all = sb("b_all", [P, D]), sb("g2_all", [P, D]), sb("b2_all", [P, D])
        nw_all, state_all = sb("nw_all", [P, D]), sb("state_all", [P, D])
        rb_all = sb("rb_all", [P, NE2])
        w_cls_sb = sb("w_cls_sb", [NE2, D])
        w_clsT = sb("w_clsT", [P, KD, NE2])
        m_sb = sb("m_sb", [P, KD, D])
        theta = sb("theta", [P, KS, DS])
        s_br, s_bi = sb("s_br", [P, KS, DS]), sb("s_bi", [P, KS, DS])
        s_cr, s_ci = sb("s_cr", [P, KS, DS]), sb("s_ci", [P, KS, DS])
        s_t1, s_t2 = sb("s_t1", [P, KS, DS]), sb("s_t2", [P, KS, DS])
        s_cos, s_sin = sb("s_cos", [P, KS, DS]), sb("s_sin", [P, KS, DS])
        turns = sb("turns", [P, KS, DS], I32)
        gain = sb("gain", [P, KS])
        rest = sb("rest", [P, KS])
        rest_cols = sb("rest_cols", [P, KS, P])
        minus_half, var_eps = sb("minus_half", [P, 1]), sb("var_eps", [P, 1])
        ring = sb("ring", [P, RING, (KD + KI) * D])
        wgu = [ring[:, r, 0:KD * D].rearrange("p (k n) -> p k n", k=KD) for r in range(RING)]
        wdn = [ring[:, r, KD * D:(KD + KI) * D].rearrange("p (k n) -> p k n", k=KI) for r in range(RING)]
        flat = ring[:, :, :].rearrange("p r n -> p (r n)")
        w_in_sb = flat[:, 0:KS * D].rearrange("p (k n) -> p k n", k=KS)
        w_out_sb = flat[:, KS * D:2 * KS * D].rearrange("p (m k) -> p m k", m=KD)
        w_outT = flat[:, 2 * KS * D:3 * KS * D].rearrange("p (k n) -> p k n", k=KS)
        xt = [sb(f"xt{u}", [P, DIN]) for u in range(2)]
        xc = sb("xc", [P, DIN])
        x1 = [sb(f"x1_{u}", [P, DIN]) for u in range(2)]
        xT = [sb(f"xT{u}", [P, KX, R]) for u in range(2)]
        st_x, mv_x, rs_x = sb("st_x", [P, 2, 6]), sb("mv_x", [P, 2]), sb("rs_x", [P, 1])
        st_h, mv_h, rs_h = sb("st_h", [P, 6]), sb("mv_h", [P, 2]), sb("rs_h", [P, 1])
        st_o, mv_o, rs_o = sb("st_o", [P, 6]), sb("mv_o", [P, 2]), sb("rs_o", [P, 1])
        tok, hc = sb("tok", [P, D]), sb("hc", [P, D])
        h = [sb(f"h{u}", [P, D]) for u in range(2)]
        xn = [sb(f"xn{u}", [P, D]) for u in range(2)]
        hx = [sb(f"hx{u}", [P, D]) for u in range(2)]
        xnT = [sb(f"xnT{u}", [P, KD, R]) for u in range(2)]
        attn, attn_sq, attn_n = sb("attn", [P, D]), sb("attn_sq", [P, D]), sb("attn_n", [P, D])
        mean_sq = sb("mean_sq", [P, 1])
        h2 = [sb(f"h2_{u}", [P, D]) for u in range(2)]
        xf = [sb(f"xf{u}", [P, ROW]) for u in range(2)]
        xfT = [sb(f"xfT{u}", [P, KD, R]) for u in range(2)]
        exinv, nmax, ex, exsum = sb("exinv", [P, 1]), sb("nmax", [P, 1]), sb("ex", [P, NE2]), sb("exsum", [P, 1])
        score, ranked, others = sb("score", [P, NE2]), sb("ranked", [P, NE2]), sb("others", [P, NE2])
        top8 = sb("top8", [P, 8])
        mask = [sb(f"mask{u}", [P, NE2], BF16) for u in range(2)]
        mask_sum = [sb(f"mask_sum{u}", [P, E], BF16) for u in range(2)]
        wsel, wnorm = sb("wsel", [P, NE2]), sb("wnorm", [P, E])
        wsum, wden, wzero, wzn = sb("wsum", [P, 1]), sb("wden", [P, 1]), sb("wzero", [P, 1]), sb("wzn", [P, 1])
        kept, pos_i = sb("kept", [P, E]), sb("pos_i", [P, E], I32)
        hi_i = sb("hi_i", [P, E], I32)
        lo, hi1 = sb("lo", [P, E], F16), sb("hi1", [P, E], F16)
        hot_hi = [sb(f"hot_hi{u}", [P, GROUPS, HI, EG], F16) for u in range(2)]
        hot_lo = [sb(f"hot_lo{u}", [P, GROUPS, LO, EG], F16) for u in range(2)]
        id_lo = [sb(f"id_lo{u}", [P, GROUPS, LO, EG], F16) for u in range(2)]
        tmp_tbl = xc[:, 0:GROUPS * EG * LO]
        tbl_part = sb("tbl_part", [P, GROUPS, LO])
        tbl_rows = sb("tbl_rows", [E * HALVES, P])
        unused = sb("unused", [P, E * HALVES])
        slot_row = sb("slot_row", [P, E * HALVES], U32)
        over, over_sum, over_rank = sb("over", [1, E]), sb("over_sum", [1, E]), sb("over_rank", [1, E])
        over_at = sb("over_at", [1, E * E], BF16)
        over_id = sb("over_id", [1, E * E], BF16)
        over_list = sb("over_list", [1, E + 1], I32)
        row_idx = [sb(f"row_idx{r}", [P, 1], U32) for r in range(RING)]
        xe = [sb(f"xe{r}", [P, ROW]) for r in range(RING)]
        xeT = [sb(f"xeT{u}", [P, KD, P]) for u in range(2)]
        silu = [sb(f"silu{u}", [P, I]) for u in range(2)]
        act = [sb(f"act{u}", [P, I]) for u in range(2)]
        actT = [sb(f"actT{u}", [P, KI, P]) for u in range(2)]
        y = [xt[u][:, 0:D] for u in range(2)]

        x_loaded = [sem(f"x_loaded{u}") for u in range(2)]
        ln1_loaded, w_tok_loaded, rows_loaded = sem("ln1_loaded"), sem("w_tok_loaded"), sem("rows_loaded")
        state_loaded, w_in_loaded, w_out_loaded = sem("state_loaded"), sem("w_in_loaded"), sem("w_out_loaded")
        w_cls_loaded = sem("w_cls_loaded")
        h2_stored = [sem(f"h2_stored{u}") for u in range(2)]
        xf_stored = [sem(f"xf_stored{u}") for u in range(2)]
        spare_stored, tbl_stored, tbl_loaded = sem("spare_stored"), sem("tbl_stored"), sem("tbl_loaded")
        out_stored = sem("out_stored")
        stood = sem("stood")
        made, consts_made, zeros_made = sem("made"), sem("consts_made"), sem("zeros_made")
        setup_links, angles_ready, sincos_ready = sem("setup_links"), sem("angles_ready"), sem("sincos_ready")
        w_in_scaled, rest_ready = sem("w_in_scaled"), sem("rest_ready")
        w_clsT_done, w_clsT_copied = sem("w_clsT_done"), sem("w_clsT_copied")
        w_outT_done, w_outT_copied = sem("w_outT_done"), sem("w_outT_copied")
        m_done, m_copied, state_done, state_copied = sem("m_done"), sem("m_copied"), sem("state_done"), sem("state_copied")
        ln_x_links, x_normed, x_transposed, xT_copied = sem("ln_x_links"), sem("x_normed"), sem("x_transposed"), sem("xT_copied")
        tok_done, tok_read, ln_h_links, h_ready, xn_ready = sem("tok_done"), sem("tok_read"), sem("ln_h_links"), sem("h_ready"), sem("xn_ready")
        hx_ready, xn_transposed, xnT_copied = sem("hx_ready"), sem("xn_transposed"), sem("xnT_copied")
        attn_done, attn_read, sq_done, ln_o_links = sem("attn_done"), sem("attn_read"), sem("sq_done"), sem("ln_o_links")
        h2_ready, xf_ready, xf_transposed, xfT_copied = sem("h2_ready"), sem("xf_ready"), sem("xf_transposed"), sem("xfT_copied")
        var_x_ready, var_h_ready, var_o_ready = sem("var_x_ready"), sem("var_h_ready"), sem("var_o_ready")
        x_eps_added, h_eps_added, o_eps_added = sem("x_eps_added"), sem("h_eps_added"), sem("o_eps_added")
        rs_x_ready, rs_h_ready, rs_o_ready = sem("rs_x_ready"), sem("rs_h_ready"), sem("rs_o_ready")
        logits_done, nmax_ready, exp_done, route_links = sem("logits_done"), sem("nmax_ready"), sem("exp_done"), sem("route_links")
        mask_ready, wts_ready, pos_done, pos_read = sem("mask_ready"), sem("wts_ready"), sem("pos_done"), sem("pos_read")
        pos_links, id_ready, hot_links, hot_ready, table_done = sem("pos_links"), sem("id_ready"), sem("hot_links"), sem("hot_ready"), sem("table_done")
        count_done, tail_links, tbl_ready, tbl_transposed = sem("count_done"), sem("tail_links"), sem("tbl_ready"), sem("tbl_transposed")
        slots_ready, list_ready = sem("slots_ready"), sem("list_ready")
        wgu_loaded = [sem(f"wgu_loaded{r}") for r in range(RING)]
        wdn_loaded = [sem(f"wdn_loaded{r}") for r in range(RING)]
        gathered = [sem(f"gathered{r}") for r in range(RING)]
        idx_ready, xe_transposed, xeT_copied, gu_done = sem("idx_ready"), sem("xe_transposed"), sem("xeT_copied"), sem("gu_done")
        silu_done, act_ready, act_transposed, actT_copied = sem("silu_done"), sem("act_ready"), sem("act_transposed"), sem("actT_copied")
        down_done, y_ready, scattered, all_added = sem("down_done"), sem("y_ready"), sem("scattered"), sem("all_added")

        def stand(eng):
            eng.sem_inc(stood, 1)

        block = ctx.enter_context(nc.Block())

        def has(step):
            return not isinstance(step.i, int) or 0 <= step.off < TILES

        LAG = 4
        LAG_IO = 6

        def tile_steps(eng, body, between=None, lag=LAG):
            looped = (TILES - 1 - lag) // 2
            for s in range(lag):
                body(Step(0, s, 2))
                if s == 0 and between:
                    between()
            with eng.Fori(0, looped) as i:
                for u in range(2):
                    body(Step(i, lag + u, 2))
            for s in range(lag + 2 * looped, TILES + lag):
                body(Step(0, s, 2))

        LOOPED_E = (E - 2 * RING) // RING

        def expert_steps(eng, body):
            for e in range(RING):
                body(Step(0, e, RING))
            with eng.Fori(0, LOOPED_E) as i:
                for r in range(RING):
                    body(Step(i, RING + r, RING))
            for e in range(RING + RING * LOOPED_E, E + 1):
                body(Step(0, e, RING))

        def real(step):
            return not isinstance(step.i, int) or 0 <= step.off < E

        def over_steps(eng, body):
            count = eng.value_load(over_list[0:1, E:E + 1], min_val=0, max_val=E)
            with eng.Fori(0, E // RING) as i:
                for r in range(RING):
                    j = Step(i, r, RING)
                    with eng.If(j.n < count):
                        body(j + E, j)

        def over_expert(eng, j):
            return eng.value_load(over_list[0:1, bass.ds(j.n, 1)], min_val=0, max_val=E - 1)

        @block.sync
        def _(sp):
            def load_x(t):
                if not has(t):
                    return
                wait(sp, x_normed, t.n - 1)
                last = isinstance(t.i, int) and t.off == TILES - 1
                nb = BLAST if last else BPT
                sp.dma_start(xt[t.slot(2)][0:nb * NPATCH, :],
                             x_rows[bass.ds(t.n * BPT, nb), :, :]).then_inc(x_loaded[t.slot(2)], 16)

            def store(sbuf, dram, t, ready, stored):
                if not has(t):
                    return
                last = isinstance(t.i, int) and t.off == TILES - 1
                rows = RLAST if last else R
                sp.wait_ge(ready, t.n + 1)
                sp.dma_start(dram[bass.ds(t.n * R, rows), :], sbuf[t.slot(2)][0:rows, :])\
                    .then_inc(stored[t.slot(2)], 16)

            def load_expert(b, e):
                wait(sp, down_done, b.n - RING + 1)
                r = b.slot(RING)
                sp.dma_start(wgu[r], w_gate_up[bass.ds(e, 1)].rearrange("o (k p) n -> p (o k) n", p=P))\
                    .then_inc(wgu_loaded[r], 16)
                sp.dma_start(wdn[r], w_down[bass.ds(e, 1)].rearrange("o (k p) n -> p (o k) n", p=P))\
                    .then_inc(wdn_loaded[r], 16)

            load_x(Step(0, 0, 2))
            sp.dma_start(g1_all[:, :], g1.partition_broadcast(P)).then_inc(ln1_loaded, 16)
            sp.dma_start(b1_all[:, :], b1.partition_broadcast(P)).then_inc(ln1_loaded, 16)
            sp.dma_start(w_tok[:, :, :], W.rearrange("(k p) n -> p k n", p=P)).then_inc(w_tok_loaded, 16)
            load_x(Step(0, 1, 2))
            for row, vector in ((b_all, b), (g2_all, g2), (b2_all, b2), (nw_all, norm_w), (rb_all, route_bias)):
                sp.dma_start(row[:, :], vector.partition_broadcast(P)).then_inc(rows_loaded, 16)
            for tile, source in ((theta, A_theta), (s_br, B_real), (s_bi, B_imag), (s_cr, C_real), (s_ci, C_imag)):
                sp.dma_start(tile[:, :, :], source.rearrange("c d s -> (c d) s").rearrange("(p k) s -> p k s", k=KS))\
                    .then_inc(state_loaded, 16)
            sp.dma_start(w_out_sb, W_out.rearrange("(m p) k -> p m k", p=P)).then_inc(w_out_loaded, 16)
            sp.dma_start(w_in_sb, W_in.rearrange("(p k) n -> p k n", k=KS)).then_inc(w_in_loaded, 16)
            sp.dma_start(w_cls_sb[:, :], w_cls).then_inc(w_cls_loaded, 16)
            sp.wait_ge(zeros_made, 1)
            sp.dma_start(acc_d[T:T + P, :], zero_row[:, :]).then_inc(spare_stored, 16)

            def step(s):
                if not (isinstance(s.i, int) and s.off < 2):
                    load_x(s)
                store(h2, acc_d, s + -4, h2_ready, h2_stored)
                store(xf, xf_d, s + -5, wts_ready, xf_stored)
                if isinstance(s.i, int) and s.off == 4:
                    sp.wait_ge(m_done, KD)
                    sp.wait_ge(state_done, 1)
                    for e in range(RING):
                        load_expert(Step(0, e, RING), e)

            tile_steps(sp, step, lag=LAG_IO)
            sp.wait_ge(tbl_ready, 1)
            tbl_g = tbl_d.rearrange("(g e h l) -> g h e l", g=GROUPS, e=EG, l=LO)
            for g in range(GROUPS):
                sp.dma_start(tbl_g[g], tbl_part[:, g, :]).then_inc(tbl_stored, 16)
            sp.wait_ge(tbl_stored, 16 * GROUPS)
            sp.dma_start(tbl_rows[:, :], tbl_d.rearrange("(r s) -> r s", s=P)).then_inc(tbl_loaded, 16)
            with sp.Fori(0, E // RING - 1) as i:
                for r in range(RING):
                    b_ = Step(i, RING + r, RING)
                    load_expert(b_, b_.n)
            sp.wait_ge(list_ready, 1)
            over_steps(sp, lambda b_, j: load_expert(b_, over_expert(sp, j)))
            sp.wait_ge(all_added, 1)
            sp.dma_start(out_d, acc_d[0:T, :]).then_inc(out_stored, 16)
            sp.wait_ge(out_stored, 16)

        @block.gpsimd
        def _(pool):
            pool.memset(ident[:, :], 0.0).then_inc(made, 1)
            pool.memset(before[:, :], 1.0).then_inc(made, 1)
            pool.memset(ones[:, :], 1.0).then_inc(made, 1)
            pool.memset(ones_e[:, :], 1.0).then_inc(made, 1)
            pool.memset(minus_half[:, :], -0.5).then_inc(made, 1)
            pool.wait_ge(made, 5)
            pool.affine_select(out=ident[:, :], in_=ident[:, :], compare_op=ALU.not_equal, fill=1.0, base=0,
                               pattern=[[-1, P]], channel_multiplier=1).then_inc(made, 1)
            pool.affine_select(out=before[:, :], in_=before[:, :], compare_op=ALU.is_gt, fill=0.0, base=0,
                               pattern=[[1, P]], channel_multiplier=-1).then_inc(made, 1)
            fits = dict(allow_small_or_imprecise_dtypes=True)
            pool.iota(iota_lo[:, :, :, :], pattern=[[0, GROUPS], [1, LO], [0, EG]], base=0, channel_multiplier=0, **fits).then_inc(made, 1)
            pool.iota(iota_hi1[:, :, :, :], pattern=[[0, GROUPS], [1, HI], [0, EG]], base=1, channel_multiplier=0, **fits).then_inc(made, 1)
            pool.iota(iota_e[:, :], pattern=[[1, E]], base=0, channel_multiplier=0, **fits).then_inc(made, 1)
            pool.iota(iota_e1[:, :], pattern=[[1, E]], base=1, channel_multiplier=0, **fits).then_inc(made, 1)
            pool.iota(token_id[:, :], pattern=[[1, 1]], base=1, channel_multiplier=1, **fits).then_inc(made, 1)
            pool.iota(spare_row[:, :], pattern=[[1, 1]], base=T + 1, channel_multiplier=1, **fits).then_inc(made, 1)
            pool.iota(same_i[:, :], pattern=[[-1, EG]], base=0, channel_multiplier=1).then_inc(made, 1)
            pool.wait_ge(made, 14)
            pool.memset(zero_16[:, :], 0.0)
            pool.memset(zero_row[:, :], 0.0).then_inc(zeros_made, 1)
            for r in range(RING):
                last = pool.memset(xe[r][:, :], 0.0)
            last.then_inc(consts_made, 1)

            def add_hx(t):
                if not has(t):
                    return
                u = t.slot(2)
                pool.wait_ge(xn_ready, t.n + 1)
                wait(pool, h2_ready, t.n - 1)
                pool.tensor_tensor(hx[u][0:R, :], h[u][0:R, :], xn[u][0:R, :], ALU.add).then_inc(hx_ready, 1)

            def number_tokens(t):
                if not has(t):
                    return
                u = t.slot(2)
                links = Links(pool, hot_links, t.n)
                pool.wait_ge(hot_ready, t.n + 1)
                wait(pool, table_done, t.n - 1)
                stand(pool)
                pool.tensor_scalar(id_lo[u][0:R, :, :, :], hot_lo[u][0:R, :, :, :], token_id[0:R, :], None, ALU.mult).then_inc(id_ready, 1)
                pool.wait_ge(id_ready, t.n + 1)
                stand(pool)
                links(pool.tensor_scalar(token_id[:, :], token_id[:, :], float(R), None, ALU.add))

            def rstd(t, eps_added, before_it, ready, count, variance, eps, rs, done):
                if not has(t):
                    return
                pool.wait_ge(ready, count)
                stand(pool)
                pool.tensor_scalar(var_eps[0:R, :], variance[0:R, :], eps, None, ALU.add).then_inc(eps_added, 1)
                pool.wait_ge(eps_added, before_it + 1)
                pool.tensor_tensor(rs[0:R, :], var_eps[0:R, :], minus_half[0:R, :], ALU.pow).then_inc(done, 1)

            def step(s):
                o, x_, h_ = s + -2, s + 1, s
                rstd(o, o_eps_added, o.n * 2, sq_done, o.n + 1, mean_sq, 1.1920928955078125e-07, rs_o, rs_o_ready)
                rstd(o, o_eps_added, o.n * 2 + 1, var_o_ready, o.n + 1, mv_o[:, 1:2], 1e-5, rs_o, rs_o_ready)
                rstd(x_, x_eps_added, x_.n, var_x_ready, x_.n + 1, mv_x[:, 1:2], 1e-6, rs_x, rs_x_ready)
                number_tokens(s + -3)
                rstd(h_, h_eps_added, h_.n * 2, var_h_ready, h_.n * 2 + 1, mv_h[:, 1:2], 1e-6, rs_h, rs_h_ready)
                rstd(h_, h_eps_added, h_.n * 2 + 1, var_h_ready, h_.n * 2 + 2, mv_h[:, 1:2], 1e-5, rs_h, rs_h_ready)
                add_hx(s)

            rstd(Step(0, 0, 2), x_eps_added, 0, var_x_ready, 1, mv_x[:, 1:2], 1e-6, rs_x, rs_x_ready)
            tile_steps(pool, step)

            def gather(b_, column):
                r = b_.slot(RING)
                wait(pool, scattered, (b_.n - RING + 1) * 16)
                pool.tensor_copy(row_idx[r][:, :], slot_row[:, bass.ds(column, 1)]).then_inc(idx_ready, 1)
                pool.wait_ge(idx_ready, b_.n + 1)
                wait(pool, y_ready, b_.n - RING + 1)
                stand(pool)
                pool.indirect_dma_start(xe[r][:, :], None, xf_d, bass.IndirectOffsetOnAxis(ap=row_idx[r][:, :], axis=0),
                                        bounds_check=T - 1, oob_is_err=False).then_inc(gathered[r], 16)

            def scatter(b_):
                pool.wait_ge(y_ready, b_.n + 1)
                wait(pool, scattered, b_.n * 16)
                stand(pool)
                pool.indirect_dma_start(acc_d, bass.IndirectOffsetOnAxis(ap=row_idx[b_.slot(RING)][:, :], axis=0),
                                        y[b_.slot(2)], None, bounds_check=T + P - 1, oob_is_err=True,
                                        compute_op=ALU.add).then_inc(scattered, 16)

            pool.wait_ge(slots_ready, 1)
            pool.wait_ge(spare_stored, 16)
            for u in range(2):
                pool.wait_ge(xf_stored[u], 16 * ((TILES - u + 1) // 2))
                pool.wait_ge(h2_stored[u], 16 * ((TILES - u + 1) // 2))
            for e in range(2):
                gather(Step(0, e, RING), HALVES * e)

            def expert_step(e):
                ahead = e + 2
                if real(ahead):
                    gather(ahead, ahead.n * HALVES)
                if real(e + -1):
                    scatter(e + -1)

            expert_steps(pool, expert_step)
            pool.wait_ge(list_ready, 1)

            def over_block(b_, j):
                gather(b_, over_expert(pool, j) * HALVES + 1)
                scatter(b_)
                pool.wait_ge(scattered, (b_.n + 1) * 16)

            pool.wait_ge(scattered, E * 16)
            over_steps(pool, over_block)
            pool.sem_inc(all_added, 1)

        @block.scalar
        def _(act_e):
            def copy_xT(t):
                if not has(t):
                    return
                u = t.slot(2)
                act_e.wait_ge(x_transposed, t.n + 1)
                wait(act_e, tok_done, t.n - 1)
                half = KX // 2
                for k in range(2):
                    last = act_e.copy(xT[u][:, k * half:(k + 1) * half, :],
                                      p_xT[k][:, 0:half * R].rearrange("p (k r) -> p k r", r=R))
                last.then_inc(xT_copied, 1)

            def copy_T(t, transposed, psum, to, used, copied):
                if not has(t):
                    return
                act_e.wait_ge(transposed, t.n + 1)
                wait(act_e, used, t.n - 1)
                act_e.copy(to[t.slot(2)][:, :, :], psum[:, 0:KD * R].rearrange("p (k r) -> p k r", r=R)).then_inc(copied, 1)

            def square(t):
                if not has(t):
                    return
                act_e.wait_ge(attn_read, t.n + 1)
                act_e.activation(attn_sq[0:R, :], attn[0:R, :], ACT.Square, scale=float(D) ** -0.5,
                                 accum_out=mean_sq[0:R, :]).then_inc(sq_done, 1)

            def exp(t):
                if not has(t):
                    return
                act_e.wait_ge(nmax_ready, t.n + 1)
                act_e.activation(ex[0:R, :], p_logits[0:R, 0:NE2], ACT.Exp, bias=nmax[0:R, :],
                                 accum_out=exsum[0:R, :]).then_inc(exp_done, 1)

            def step(s):
                square(s + -2)
                exp(s + -3)
                copy_T(s + -2, xf_transposed, p_xfT, xfT, logits_done, xfT_copied)
                copy_xT(s + 1)
                copy_T(s, xn_transposed, p_xnT, xnT, attn_done, xnT_copied)

            def set_up():
                act_e.wait_ge(angles_ready, 1)
                act_e.activation(s_cos[:, :, :], s_t1[:, :, :], ACT.Sin)
                act_e.activation(s_sin[:, :, :], s_t2[:, :, :], ACT.Sin).then_inc(sincos_ready, 1)
                act_e.wait_ge(w_clsT_done, 1)
                act_e.copy(w_clsT[:, :, :], p_logits[:, 0:KD * NE2].rearrange("p (k n) -> p k n", k=KD)).then_inc(w_clsT_copied, 1)
                for k in range(KS):
                    act_e.wait_ge(w_outT_done, k + 1)
                    act_e.copy(w_outT[:, k, :], p_woT[k % 2][:, :]).then_inc(w_outT_copied, 1)
                for m in range(KD):
                    act_e.wait_ge(m_done, m + 1)
                    act_e.copy(m_sb[:, m, :], p_m[m % 2][:, :]).then_inc(m_copied, 1)
                act_e.wait_ge(state_done, 1)
                act_e.copy(state_all[:, :], p_m[0][:, :]).then_inc(state_copied, 1)

            copy_xT(Step(0, 0, 2))
            tile_steps(act_e, step, set_up)

            def copy_xeT(b_):
                u = b_.slot(2)
                act_e.wait_ge(xe_transposed, b_.n + 1)
                wait(act_e, gu_done, b_.n - 1)
                act_e.copy(xeT[u][:, :, :], p_xeT[u][:, :].rearrange("p (k s) -> p k s", k=KD)).then_inc(xeT_copied, 1)

            def silu_gate(b_):
                u = b_.slot(2)
                act_e.wait_ge(gu_done, b_.n + 1)
                wait(act_e, act_ready, b_.n - 1)
                act_e.activation(silu[u][:, :], p_gu[u][:, 0:I], ACT.Silu).then_inc(silu_done, 1)

            copy_xeT(Step(0, 0, RING))

            def expert_step(e):
                if real(e):
                    silu_gate(e)
                if real(e + 1):
                    copy_xeT(e + 1)

            expert_steps(act_e, expert_step)
            act_e.wait_ge(list_ready, 1)

            def over_block(b_, j):
                copy_xeT(b_)
                silu_gate(b_)

            over_steps(act_e, over_block)

        @block.vector
        def _(dve):
            def ln_x(t):
                if not has(t):
                    return
                u = t.slot(2)
                links = Links(dve, ln_x_links, t.n * 3)
                dve.wait_ge(x_loaded[u], t.turn(2) * 16 + 16)
                links(dve.bn_stats(st_x[0:R, 0, :], xt[u][0:R, 0:DIN // 2]))
                links(dve.bn_stats(st_x[0:R, 1, :], xt[u][0:R, DIN // 2:DIN]))
                stand(dve)
                dve.bn_aggr(mv_x[0:R, :], st_x[0:R, :, :].rearrange("p a b -> p (a b)")).then_inc(var_x_ready, 1)
                dve.wait_ge(var_x_ready, t.n + 1)
                links(dve.scalar_tensor_tensor(xc[0:R, :], xt[u][0:R, :], mv_x[0:R, 0:1], g1_all[0:R, :], ALU.subtract, ALU.mult))
                dve.wait_ge(rs_x_ready, t.n + 1)
                wait(dve, x_transposed, t.n - 1)
                dve.scalar_tensor_tensor(x1[u][0:R, :], xc[0:R, :], rs_x[0:R, :], b1_all[0:R, :], ALU.mult, ALU.add).then_inc(x_normed, 1)

            def ln_h(t):
                if not has(t):
                    return
                u = t.slot(2)
                links = Links(dve, ln_h_links, t.n * 3)
                dve.wait_ge(tok_done, t.n + 1)
                dve.tensor_tensor(tok[0:R, :], p_tok[0:R, :], b_all[0:R, :], ALU.add).then_inc(tok_read, 1)
                dve.wait_ge(tok_read, t.n + 1)
                links(dve.bn_stats(st_h[0:R, :], tok[0:R, :]))
                stand(dve)
                dve.bn_aggr(mv_h[0:R, :], st_h[0:R, :]).then_inc(var_h_ready, 1)
                dve.wait_ge(var_h_ready, t.n * 2 + 1)
                links(dve.scalar_tensor_tensor(hc[0:R, :], tok[0:R, :], mv_h[0:R, 0:1], g2_all[0:R, :], ALU.subtract, ALU.mult))
                dve.wait_ge(rs_h_ready, t.n * 2 + 1)
                wait(dve, hx_ready, t.n - 1)
                dve.scalar_tensor_tensor(h[u][0:R, :], hc[0:R, :], rs_h[0:R, :], b2_all[0:R, :], ALU.mult, ALU.add).then_inc(h_ready, 1)
                dve.wait_ge(h_ready, t.n + 1)
                links(dve.bn_stats(st_h[0:R, :], h[u][0:R, :]))
                stand(dve)
                dve.bn_aggr(mv_h[0:R, :], st_h[0:R, :]).then_inc(var_h_ready, 1)
                dve.wait_ge(rs_h_ready, t.n * 2 + 2)
                wait(dve, xn_transposed, t.n - 1)
                dve.tensor_scalar(xn[u][0:R, :], h[u][0:R, :], mv_h[0:R, 0:1], rs_h[0:R, :], ALU.subtract, ALU.mult).then_inc(xn_ready, 1)

            def read_attn(t):
                if not has(t):
                    return
                dve.wait_ge(attn_done, t.n + 1)
                dve.tensor_tensor(attn[0:R, :], p_attn[0:R, :], state_all[0:R, :], ALU.add).then_inc(attn_read, 1)

            def ln_o(t):
                if not has(t):
                    return
                u = t.slot(2)
                links = Links(dve, ln_o_links, t.n * 2)
                dve.wait_ge(rs_o_ready, t.n * 2 + 1)
                links(dve.scalar_tensor_tensor(attn_n[0:R, :], attn[0:R, :], rs_o[0:R, :], nw_all[0:R, :], ALU.mult, ALU.mult))
                dve.wait_ge(hx_ready, t.n + 1)
                wait(dve, h2_stored[u], t.turn(2) * 16)
                dve.tensor_tensor(h2[u][0:R, :], attn_n[0:R, :], hx[u][0:R, :], ALU.add).then_inc(h2_ready, 1)
                dve.wait_ge(h2_ready, t.n + 1)
                links(dve.bn_stats(st_o[0:R, :], h2[u][0:R, :]))
                stand(dve)
                dve.bn_aggr(mv_o[0:R, :], st_o[0:R, :]).then_inc(var_o_ready, 1)
                dve.wait_ge(rs_o_ready, t.n * 2 + 2)
                wait(dve, xf_stored[u], t.turn(2) * 16)
                dve.tensor_scalar(xf[u][0:R, 0:D], h2[u][0:R, :], mv_o[0:R, 0:1], rs_o[0:R, :], ALU.subtract, ALU.mult).then_inc(xf_ready, 1)

            def route(t):
                if not has(t):
                    return
                u = t.slot(2)
                links = Links(dve, route_links, t.n * 12)
                dve.wait_ge(logits_done, t.n + 1)
                dve.tensor_reduce(nmax[0:R, :], p_logits[0:R, 0:NE2], AX.X, ALU.max, negate=True).then_inc(nmax_ready, 1)
                dve.wait_ge(exp_done, t.n + 1)
                links(dve.reciprocal(exinv[0:R, :], exsum[0:R, :]))
                links(dve.tensor_scalar(score[0:R, :], ex[0:R, :], exinv[0:R, :], None, ALU.mult))
                links(dve.tensor_tensor(ranked[0:R, :], score[0:R, :], rb_all[0:R, :], ALU.add))
                stand(dve)
                links(dve.max(top8[0:R, :], ranked[0:R, :]))
                stand(dve)
                links(dve.match_replace(others[0:R, :], top8[0:R, :], ranked[0:R, :], -3.0e38))
                wait(dve, pos_done, t.n)
                dve.tensor_tensor(mask[u][0:R, :], others[0:R, :], ranked[0:R, :], ALU.not_equal).then_inc(mask_ready, 1)
                dve.wait_ge(mask_ready, t.n + 1)
                if isinstance(t.i, int) and t.off == 0:
                    links(dve.tensor_copy(mask_sum[u][0:R, :], mask[u][0:R, 0:E]))
                else:
                    links(dve.tensor_tensor(mask_sum[u][0:R, :], mask_sum[1 - u][0:R, :], mask[u][0:R, 0:E], ALU.add))
                links(dve.scalar_tensor_tensor(wsel[0:R, :], mask[u][0:R, :], 1.0, score[0:R, :], ALU.mult, ALU.mult, accum_out=wsum[0:R, :]))
                links(dve.tensor_scalar(wden[0:R, :], wsum[0:R, :], 1e-20, None, ALU.add))
                links(dve.reciprocal(wden[0:R, :], wden[0:R, :]))
                links(dve.tensor_reduce(wzero[0:R, :], wsel[0:R, E:NE2], AX.X, ALU.add))
                links(dve.tensor_scalar(wzn[0:R, :], wzero[0:R, :], wden[0:R, :], SCALE, ALU.mult, ALU.mult))
                links(dve.tensor_scalar(wnorm[0:R, :], wsel[0:R, 0:E], wden[0:R, :], SCALE, ALU.mult, ALU.mult))
                dve.scalar_tensor_tensor(xf[u][0:R, D:ROW], wnorm[0:R, :], wzn[0:R, :], wnorm[0:R, :], ALU.mult, ALU.add).then_inc(wts_ready, 1)

            def one_hots(t):
                if not has(t):
                    return
                u = t.slot(2)
                links = Links(dve, pos_links, t.n * 3)
                dve.wait_ge(pos_done, t.n + 1)
                links(dve.scalar_tensor_tensor(kept[0:R, :], p_pos[0:R, :], float(CAP), mask[u][0:R, 0:E], ALU.is_lt, ALU.mult))
                dve.tensor_copy(pos_i[0:R, :], p_pos[0:R, :]).then_inc(pos_read, 1)
                dve.wait_ge(pos_read, t.n + 1)
                links(dve.tensor_scalar(hi_i[0:R, :], pos_i[0:R, :], LO.bit_length() - 1, None, ALU.arith_shift_right))
                dve.scalar_tensor_tensor(lo[0:R, :], hi_i[0:R, :], float(-LO), pos_i[0:R, :], ALU.mult, ALU.add)
                links(dve.scalar_tensor_tensor(hi1[0:R, :], hi_i[0:R, :], 1.0, kept[0:R, :], ALU.add, ALU.mult))
                wait(dve, table_done, t.n - 1)
                wait(dve, id_ready, t.n - 1)
                grid = [R, GROUPS, LO, EG]
                dve.tensor_tensor(hot_lo[u][0:R, :, :, :], iota_lo[0:R, :, :, :], lo[0:R, :].rearrange("p (g e) -> p g e", e=EG).unsqueeze(2).to_broadcast(grid), ALU.is_equal)
                dve.tensor_tensor(hot_hi[u][0:R, :, :, :], iota_hi1[0:R, :, :, :], hi1[0:R, :].rearrange("p (g e) -> p g e", e=EG).unsqueeze(2).to_broadcast(grid), ALU.is_equal).then_inc(hot_ready, 1)

            def step(s):
                read_attn(s + -2)
                route(s + -3)
                ln_o(s + -2)
                ln_x(s + 1)
                one_hots(s + -3)
                ln_h(s)

            def set_up():
                links = Links(dve, setup_links, 0)
                dve.wait_ge(state_loaded, 16 * 5)
                dve.wait_ge(consts_made, 1)
                links(dve.tensor_scalar(same_i[:, :], same_i[:, :], EG - 1, None, ALU.bitwise_and))
                links(dve.tensor_scalar(same_expert[:, :], same_i[:, :], 0.0, None, ALU.is_equal))
                links(dve.tensor_scalar(turns[:, :, :], theta[:, :, :], 0.5 / PI, None, ALU.mult))
                links(dve.scalar_tensor_tensor(s_t2[:, :, :], turns[:, :, :], -2 * PI, theta[:, :, :], ALU.mult, ALU.add))
                links(dve.tensor_scalar(s_t2[:, :, :], s_t2[:, :, :], -PI, PI, ALU.max, ALU.min))
                links(dve.scalar_tensor_tensor(s_t1[:, :, :], s_t2[:, :, :], -1.0, s_t2[:, :, :], ALU.mult, ALU.max))
                dve.tensor_scalar(s_t1[:, :, :], s_t1[:, :, :], -1.0, PI / 2, ALU.mult, ALU.add).then_inc(angles_ready, 1)
                dve.wait_ge(sincos_ready, 1)
                links(dve.tensor_scalar(s_t1[:, :, :], s_sin[:, :, :], 0.0, None, ALU.mult))
                links(dve.scalar_tensor_tensor(s_t2[:, :, :], s_cos[:, :, :], 0.0, s_t1[:, :, :], ALU.mult, ALU.subtract))
                links(dve.scalar_tensor_tensor(s_t1[:, :, :], s_cos[:, :, :], 0.0, s_t1[:, :, :], ALU.mult, ALU.add))
                links(dve.tensor_tensor(s_t2[:, :, :], s_t2[:, :, :], s_cr[:, :, :], ALU.mult))
                links(dve.tensor_tensor(s_t1[:, :, :], s_t1[:, :, :], s_ci[:, :, :], ALU.mult))
                links(dve.tensor_tensor(s_t2[:, :, :], s_t2[:, :, :], s_t1[:, :, :], ALU.subtract))
                links(dve.tensor_reduce(rest[:, :], s_t2[:, :, :], AX.X, ALU.add))
                dve.tensor_copy(rest_cols[:, :, :], rest[:, :].unsqueeze(2).to_broadcast([P, KS, P])).then_inc(rest_ready, 1)
                links(dve.tensor_tensor(s_br[:, :, :], s_br[:, :, :], s_cr[:, :, :], ALU.mult))
                links(dve.tensor_tensor(s_bi[:, :, :], s_bi[:, :, :], s_ci[:, :, :], ALU.mult))
                links(dve.tensor_tensor(s_br[:, :, :], s_br[:, :, :], s_bi[:, :, :], ALU.subtract))
                links(dve.tensor_reduce(gain[:, :], s_br[:, :, :], AX.X, ALU.add))
                dve.wait_ge(w_in_loaded, 16)
                for k in range(KS):
                    last = dve.tensor_scalar(w_in_sb[:, k, :], w_in_sb[:, k, :], gain[:, k:k + 1], None, ALU.mult)
                last.then_inc(w_in_scaled, 1)
                dve.wait_ge(state_copied, 1)

            dve.wait_ge(ln1_loaded, 32)
            ln_x(Step(0, 0, 2))
            dve.wait_ge(rows_loaded, 16 * 5)
            tile_steps(dve, step, set_up)

            links = Links(dve, tail_links, 0)
            dve.wait_ge(count_done, 1)
            links(dve.tensor_scalar(over[:, :], p_tok[0:1, 0:E], float(P), None, ALU.is_gt))
            links(dve.tensor_tensor_scan(over_sum[:, :], ones_e[:, :], over[:, :], 0.0, ALU.mult, ALU.add))
            links(dve.tensor_tensor(over_rank[:, :], over_sum[:, :], over[:, :], ALU.mult))
            links(dve.tensor_copy(over_list[:, E:E + 1], over_sum[:, E - 1:E]))
            dve.wait_ge(table_done, TILES)
            links(dve.tensor_tensor(tmp_tbl.rearrange("p (a e) -> p a e", e=EG), p_table[:, :].rearrange("p (a e) -> p a e", e=EG),
                                    same_expert[:, :].unsqueeze(1).to_broadcast([P, GROUPS * LO, EG]), ALU.mult))
            dve.tensor_reduce(tbl_part[:, :, :], tmp_tbl.rearrange("p (g l e) -> p g l e", g=GROUPS, e=EG),
                              AX.X, ALU.add).then_inc(tbl_ready, 1)
            grid = [1, E, E]
            links(dve.tensor_tensor(over_at[:, :].rearrange("o (r e) -> o r e", e=E), iota_e1[:, :].unsqueeze(2).to_broadcast(grid),
                                    over_rank[:, :].unsqueeze(1).to_broadcast(grid), ALU.is_equal))
            links(dve.tensor_tensor(over_id[:, :].rearrange("o (r e) -> o r e", e=E), over_at[:, :].rearrange("o (r e) -> o r e", e=E),
                                    iota_e[:, :].unsqueeze(1).to_broadcast(grid), ALU.mult))
            links(dve.tensor_reduce(over[:, :], over_id[:, :].rearrange("o (r e) -> o r e", e=E), AX.X, ALU.add))
            links(dve.tensor_copy(over_list[:, 0:E], over[:, :]))
            dve.wait_ge(tbl_transposed, 1)
            links(dve.tensor_scalar(unused[:, :], p_logits[:, 0:E * HALVES], 0.0, spare_row[:, :], ALU.is_equal, ALU.mult))
            dve.scalar_tensor_tensor(slot_row[:, :], p_logits[:, 0:E * HALVES], -1.0, unused[:, :], ALU.add, ALU.add).then_inc(slots_ready, 1)
            dve.sem_inc(list_ready, 1)

            def gate_times_up(b_):
                u = b_.slot(2)
                dve.wait_ge(silu_done, b_.n + 1)
                wait(dve, act_transposed, b_.n - 1)
                dve.tensor_tensor(act[u][:, :], silu[u][:, :], p_gu[u][:, I:2 * I], ALU.mult).then_inc(act_ready, 1)

            def weigh(b_, e):
                u = b_.slot(2)
                dve.wait_ge(down_done, b_.n + 1)
                wait(dve, scattered, (b_.n - 1) * 16)
                dve.tensor_scalar(y[u], p_y[u][:, :], xe[b_.slot(RING)][:, bass.ds(e + D, 1)], None, ALU.mult).then_inc(y_ready, 1)

            def copy_actT(b_):
                u = b_.slot(2)
                dve.wait_ge(act_transposed, b_.n + 1)
                wait(dve, down_done, b_.n - 1)
                dve.tensor_copy(actT[u][:, :, :], p_actT[u][:, 0:KI * P].rearrange("p (k s) -> p k s", k=KI)).then_inc(actT_copied, 1)

            def expert_step(e):
                if real(e):
                    gate_times_up(e)
                if real(e + -1):
                    weigh(e + -1, (e + -1).n)
                if real(e):
                    copy_actT(e)

            expert_steps(dve, expert_step)

            def over_block(b_, j):
                gate_times_up(b_)
                copy_actT(b_)
                weigh(b_, over_expert(dve, j))

            over_steps(dve, over_block)

        @block.tensor
        def _(pe):
            def transpose_x(t):
                if not has(t):
                    return
                pe.wait_ge(x_normed, t.n + 1)
                wait(pe, xT_copied, t.n)
                half = KX // 2
                for k in range(KX):
                    last = pe.transpose(p_xT[k // half][:, (k % half) * R:(k % half + 1) * R],
                                        x1[t.slot(2)][0:R, k * P:(k + 1) * P], ident[0:R, 0:R])
                last.then_inc(x_transposed, 1)

            def transpose_d(t, ready, source, psum, copied, done):
                if not has(t):
                    return
                pe.wait_ge(ready, t.n + 1)
                wait(pe, copied, t.n)
                for k in range(KD):
                    last = pe.transpose(psum[:, k * R:(k + 1) * R], source[t.slot(2)][0:R, k * P:(k + 1) * P], ident[0:R, 0:R])
                last.then_inc(done, 1)

            def embed(t, blocks):
                if not has(t):
                    return
                if blocks[0] == 0:
                    pe.wait_ge(xT_copied, t.n + 1)
                    wait(pe, tok_read, t.n)
                for k in blocks:
                    last = pe.matmul(p_tok[0:R, :], xT[t.slot(2)][:, k, :], w_tok[:, k, :], start=(k == 0), stop=(k == KX - 1))
                if blocks[-1] == KX - 1:
                    last.then_inc(tok_done, 1)

            def mix(t):
                if not has(t):
                    return
                pe.wait_ge(xnT_copied, t.n + 1)
                wait(pe, attn_read, t.n)
                for k in range(KD):
                    last = pe.matmul(p_attn[0:R, :], xnT[t.slot(2)][:, k, :], m_sb[:, k, :], start=(k == 0), stop=(k == KD - 1))
                last.then_inc(attn_done, 1)

            def logits(t):
                if not has(t):
                    return
                pe.wait_ge(xfT_copied, t.n + 1)
                wait(pe, exp_done, t.n)
                for k in range(KD):
                    last = pe.matmul(p_logits[0:R, 0:NE2], xfT[t.slot(2)][:, k, :], w_clsT[:, k, :], start=(k == 0), stop=(k == KD - 1))
                last.then_inc(logits_done, 1)

            def positions(t):
                if not has(t):
                    return
                first = isinstance(t.i, int) and t.off == 0
                pe.wait_ge(mask_ready, t.n + 1)
                last = pe.matmul(p_pos[0:R, :], before[0:R, 0:R], mask[t.slot(2)][0:R, 0:E], start=True, stop=first)
                if not first:
                    last = pe.matmul(p_pos[0:R, :], ones[0:R, 0:R], mask_sum[1 - t.slot(2)][0:R, :], start=False, stop=True)
                last.then_inc(pos_done, 1)

            def table(t):
                if not has(t):
                    return
                final = isinstance(t.i, int) and t.off == TILES - 1
                rows, u = RLAST if final else R, t.slot(2)
                pe.wait_ge(id_ready, t.n + 1)
                for g in range(GROUPS):
                    last = pe.matmul(p_table[:, g * P:(g + 1) * P], hot_hi[u][0:rows, g, :, :].rearrange("p l e -> p (l e)"),
                                     id_lo[u][0:rows, g, :, :].rearrange("p l e -> p (l e)"),
                                     start=False, stop=final, skip_group_check=True)
                last.then_inc(table_done, 1)

            def step(s):
                embed(s, list(range(6)))
                if has(s + -3):
                    wait(pe, pos_read, (s + -3).n)
                transpose_d(s + -2, xf_ready, xf, p_xfT, xfT_copied, xf_transposed)
                embed(s, list(range(6, KX)))
                logits(s + -2)
                positions(s + -3)
                table(s + -4)
                mix(s + -1)
                transpose_x(s + 1)
                transpose_d(s, xn_ready, xn, p_xnT, xnT_copied, xn_transposed)

            def set_up():
                pe.wait_ge(w_cls_loaded, 16)
                for k in range(KD):
                    last = pe.transpose(p_logits[:, k * NE2:(k + 1) * NE2], w_cls_sb[:, k * P:(k + 1) * P], ident[0:NE2, 0:NE2])
                last.then_inc(w_clsT_done, 1)
                pe.wait_ge(w_out_loaded, 16)
                for k in range(KS):
                    if k == 0:
                        pe.wait_ge(w_clsT_copied, 1)
                    if k >= 2:
                        pe.wait_ge(w_outT_copied, k - 1)
                    for m in range(KD):
                        last = pe.transpose(p_woT[k % 2][:, m * P:(m + 1) * P], w_out_sb[:, m, k:NS:KS], ident[:, :])
                    last.then_inc(w_outT_done, 1)
                pe.wait_ge(w_outT_copied, KS)
                pe.wait_ge(w_in_scaled, 1)
                for m in range(KD):
                    if m >= 2:
                        pe.wait_ge(m_copied, m - 1)
                    for k in range(KS):
                        last = pe.matmul(p_m[m % 2][:, :], w_in_sb[:, k, m * P:(m + 1) * P], w_outT[:, k, :],
                                         start=(k == 0), stop=(k == KS - 1))
                    last.then_inc(m_done, 1)
                pe.wait_ge(rest_ready, 1)
                pe.wait_ge(m_copied, KD)
                for k in range(KS):
                    last = pe.matmul(p_m[0][:, :], rest_cols[:, k, :], w_outT[:, k, :], start=(k == 0), stop=(k == KS - 1))
                last.then_inc(state_done, 1)
                pe.wait_ge(state_copied, 1)
                pe.matmul(p_table[:, :], zero_16[:, 0:P], zero_16[:, 0:GROUPS * P], start=True, stop=False, skip_group_check=True)

            pe.wait_ge(consts_made, 1)
            transpose_x(Step(0, 0, 2))
            pe.wait_ge(w_tok_loaded, 16)
            tile_steps(pe, step, set_up)
            last_u = (TILES - 1) % 2
            pe.matmul(p_tok[0:32, 0:E], ones[0:R, 0:32], mask_sum[1 - last_u][0:R, :], start=True, stop=False)
            pe.matmul(p_tok[0:32, 0:E], ones[0:RLAST, 0:32], mask[last_u][0:RLAST, 0:E], start=False, stop=True).then_inc(count_done, 1)
            pe.wait_ge(tbl_loaded, 16)
            pe.transpose(p_logits[:, 0:E * HALVES], tbl_rows[:, :], ident[0:E * HALVES, 0:E * HALVES]).then_inc(tbl_transposed, 1)

            def transpose_xe(b_):
                u, r = b_.slot(2), b_.slot(RING)
                pe.wait_ge(gathered[r], b_.turn(RING) * 16 + 16)
                wait(pe, xeT_copied, b_.n - 1)
                for k in range(KD):
                    last = pe.transpose(p_xeT[u][:, k * P:(k + 1) * P], xe[r][:, k * P:(k + 1) * P], ident[:, :])
                last.then_inc(xe_transposed, 1)

            def gate_up(b_):
                u, r = b_.slot(2), b_.slot(RING)
                pe.wait_ge(xeT_copied, b_.n + 1)
                pe.wait_ge(wgu_loaded[r], b_.turn(RING) * 16 + 16)
                wait(pe, act_ready, b_.n - 1)
                for k in range(KD):
                    last = pe.matmul(p_gu[u][:, :], xeT[u][:, k, :], wgu[r][:, k, :], start=(k == 0), stop=(k == KD - 1))
                last.then_inc(gu_done, 1)

            def transpose_act(b_):
                u = b_.slot(2)
                pe.wait_ge(act_ready, b_.n + 1)
                wait(pe, actT_copied, b_.n - 1)
                for k in range(KI):
                    last = pe.transpose(p_actT[u][:, k * P:(k + 1) * P], act[u][:, k * P:(k + 1) * P], ident[:, :])
                last.then_inc(act_transposed, 1)

            def down(b_):
                u, r = b_.slot(2), b_.slot(RING)
                pe.wait_ge(actT_copied, b_.n + 1)
                pe.wait_ge(wdn_loaded[r], b_.turn(RING) * 16 + 16)
                wait(pe, y_ready, b_.n - 1)
                for k in range(KI):
                    last = pe.matmul(p_y[u][:, :], actT[u][:, k, :], wdn[r][:, k, :], start=(k == 0), stop=(k == KI - 1))
                last.then_inc(down_done, 1)

            transpose_xe(Step(0, 0, RING))

            def expert_step(e):
                if real(e):
                    gate_up(e)
                if real(e + 1):
                    transpose_xe(e + 1)
                if real(e + -1):
                    down(e + -1)
                if real(e):
                    transpose_act(e)

            expert_steps(pe, expert_step)
            pe.wait_ge(list_ready, 1)

            def over_block(b_, j):
                transpose_xe(b_)
                gate_up(b_)
                transpose_act(b_)
                down(b_)

            over_steps(pe, over_block)


_INS = ['x', 'L0_tok_W', 'L0_tok_b', 'L0_tok_g1', 'L0_tok_b1', 'L0_tok_g2', 'L0_tok_b2', 'L0_attn_W_in',
        'L0_attn_W_out', 'L0_attn_A_theta', 'L0_attn_B_real', 'L0_attn_B_imag', 'L0_attn_C_real',
        'L0_attn_C_imag', 'L0_attn_norm_w', 'L0_ffn_w_cls', 'L0_ffn_bias', 'L0_ffn_w_gate_up', 'L0_ffn_w_down']
_OUTS = [((64, 23, 512), 'float32')]


def kernel(**inputs):
    import numpy as _np
    import concourse.bacc as _bacc
    from concourse import mybir as _mybir
    from concourse.bass_utils import run_bass_kernel_spmd as _run

    nc = _bacc.Bacc("TRN2", target_bir_lowering=False, num_devices=1)
    arrays, args = {}, []
    for name in _INS:
        a = _np.ascontiguousarray(inputs[name])
        arrays[f"in_{name}_dram"] = a
        args.append(nc.dram_tensor(f"in_{name}_dram", a.shape, _mybir.dt.from_np(a.dtype), kind="ExternalInput").ap())
    for i, (shape, dtype) in enumerate(_OUTS):
        dt = _mybir.dt.from_np(_np.dtype(dtype))
        args.append(nc.dram_tensor(f"out_{i}_dram", shape, dt, kind="ExternalOutput").ap())
    audio_tower(nc, *args)
    r = _run(nc, [arrays], core_ids=[0])
    return r.results[0]["out_0_dram"]
```

```python
from contextlib import ExitStack

import concourse.bass as bass
from concourse import mybir

F32 = mybir.dt.float32
BF16 = mybir.dt.bfloat16
F16 = mybir.dt.float16
I32 = mybir.dt.int32
U32 = mybir.dt.uint32
ALU = mybir.AluOpType
ACT = mybir.ActivationFunctionType
AX = mybir.AxisListType

P = 128
PI = 3.1415925


class Step:

    def __init__(self, i, off, unroll):
        self.i, self.off, self.unroll = i, off, unroll

    def __add__(self, k):
        return Step(self.i, self.off + k, self.unroll)

    @property
    def n(self):
        return self.off if isinstance(self.i, int) else self.i * self.unroll + self.off

    def slot(self, ring):
        return self.off % ring

    def turn(self, ring):
        here = self.off // ring
        return here if isinstance(self.i, int) else self.i * (self.unroll // ring) + here


def wait(eng, sem, value):
    if not isinstance(value, int) or value > 0:
        eng.wait_ge(sem, value)


class Links:

    def __init__(self, eng, sem, before):
        self.eng, self.sem, self.before, self.n = eng, sem, before, 0

    def __call__(self, instruction):
        self.n += 1
        instruction.then_inc(self.sem, 1)
        return self.n

    def after(self, number):
        self.eng.wait_ge(self.sem, self.before + number)

    def chain(self, instruction):
        self.after(self(instruction))


def audio_tower(nc, x, W, b, g1, b1, g2, b2, W_in, W_out, A_theta, B_real, B_imag, C_real, C_imag,
                norm_w, w_cls, route_bias, w_gate_up, w_down, out):
    BATCH, TIME, FEAT = x.shape
    DIN, D = W.shape
    TIN = DIN // FEAT
    NPATCH = TIME // TIN
    T = BATCH * NPATCH
    R = P
    TILES = -(-T // R)
    RLAST = T - (TILES - 1) * R
    KX = DIN // P
    KD = D // P
    NS = W_in.shape[0]
    KS = NS // P
    DS = A_theta.shape[2]
    NE2 = w_cls.shape[0]
    E = w_gate_up.shape[0]
    I = w_down.shape[1]
    KI = I // P
    CAP = 256
    HALVES = CAP // P
    LO = 16
    HI = CAP // LO
    EG = P // HI
    GROUPS = E // EG
    SCALE = 1.5
    ROW = D + E
    RING = 8

    x_rows = x[:, 0:NPATCH * TIN, :].rearrange("b (n t) f -> b n (t f)", t=TIN)
    xf_d = nc.dram_tensor("token_rows", (T, ROW), F32).ap()
    acc_d = nc.dram_tensor("sums", (T + P, D), F32).ap()
    tbl_d = nc.dram_tensor("slot_table", (E * CAP,), F32).ap()
    out_d = out.rearrange("b n d -> (b n) d")

    ctx = ExitStack()
    with ctx:
        def sb(name, shape, dt=F32):
            return ctx.enter_context(nc.sbuf_tensor(name, shape, dt))

        def sem(name):
            return ctx.enter_context(nc.semaphore(name))

        bank = [ctx.enter_context(nc.psum_tensor(f"bank{i}", [P, 512], F32)) for i in range(8)]
        p_xT = [bank[0], bank[1]]
        p_tok, p_xnT, p_attn, p_xfT, p_logits, p_table = bank[2:8]
        p_pos = p_logits[:, NE2:NE2 + E]
        p_woT = [p_logits, p_table]
        p_m = [p_attn, p_xfT]
        p_gu, p_xeT, p_y, p_actT = [bank[0], bank[1]], [bank[2], bank[3]], [bank[4], bank[6]], [bank[5], bank[7]]

        ident = sb("ident", [P, P])
        before = sb("before", [P, P], BF16)
        ones = sb("ones", [P, P], BF16)
        same_i, same_expert = sb("same_i", [P, EG], I32), sb("same_expert", [P, EG])
        iota_lo = sb("iota_lo", [P, GROUPS, LO, EG], F16)
        iota_hi1 = sb("iota_hi1", [P, GROUPS, HI, EG], F16)
        iota_e = sb("iota_e", [1, E])
        iota_e1 = sb("iota_e1", [1, E])
        ones_e = sb("ones_e", [1, E])
        token_id = sb("token_id", [P, 1])
        spare_row = sb("spare_row", [P, 1])
        w_tok = sb("w_tok", [P, KX, D])
        g1_col, b1_col = sb("g1_col", [P, KX]), sb("b1_col", [P, KX])
        b_all, g2_all, b2_all = sb("b_all", [P, D]), sb("g2_all", [P, D]), sb("b2_all", [P, D])
        nw_all, state_all = sb("nw_all", [P, D]), sb("state_all", [P, D])
        rb_all = sb("rb_all", [P, NE2])
        w_clsT = sb("w_clsT", [P, KD, NE2])
        m_sb = sb("m_sb", [P, KD, D])
        turns = sb("turns", [P, KS, DS], I32)
        gain = sb("gain", [P, KS])
        rest = sb("rest", [P, KS])
        minus_half = sb("minus_half", [P, 1])
        ring = sb("ring", [P, RING, (KD + KI) * D])
        wgu = [ring[:, r, 0:KD * D].rearrange("p (k n) -> p k n", k=KD) for r in range(RING)]
        wdn = [ring[:, r, KD * D:(KD + KI) * D].rearrange("p (k n) -> p k n", k=KI) for r in range(RING)]
        flat = ring[:, :, :].rearrange("p r n -> p (r n)")
        w_in_sb = flat[:, 0:KS * D].rearrange("p (k n) -> p k n", k=KS)
        w_out_sb = flat[:, KS * D:2 * KS * D].rearrange("p (m k) -> p m k", m=KD)
        w_outT = flat[:, 2 * KS * D:3 * KS * D].rearrange("p (k n) -> p k n", k=KS)
        w_raw = flat[:, 3 * KS * D:(3 * KS + KX) * D].rearrange("p (k n) -> p k n", k=KX)
        after_w = (3 * KS + KX) * D
        b1_part, rest_part = flat[:, after_w:after_w + D], flat[:, after_w + D:after_w + 2 * D]
        ones_f = flat[:, after_w + 2 * D:after_w + 2 * D + P]
        after_cols = after_w + 2 * D + P
        w_cls_sb = flat[0:NE2, after_cols:after_cols + D]
        zero_row = flat[:, RING * (KD + KI) * D - D:RING * (KD + KI) * D]
        theta, s_br, s_bi, s_cr, s_ci, s_t1, s_t2, s_cos, s_sin = (
            flat[:, after_cols + D + n * KS * DS:after_cols + D + (n + 1) * KS * DS].rearrange("p (k s) -> p k s", k=KS) for n in range(9))
        xt = [sb(f"xt{u}", [P, DIN]) for u in range(2)]
        x1 = [sb(f"x1_{u}", [P, DIN]) for u in range(2)]
        xT = [sb(f"xT{u}", [P, KX, R]) for u in range(2)]
        st_x, mv_x, ve_x, rs_x, nm_x = sb("st_x", [P, 2, 6]), sb("mv_x", [P, 2]), sb("ve_x", [P, 1]), sb("rs_x", [P, 1]), sb("nm_x", [P, 1])
        st_t, mv_t, ve_t, rs_t = sb("st_t", [P, 6]), sb("mv_t", [P, 2]), sb("ve_t", [P, 1]), sb("rs_t", [P, 1])
        st_h, mv_h, ve_h, rs_h, nm_h = sb("st_h", [P, 6]), sb("mv_h", [P, 2]), sb("ve_h", [P, 1]), sb("rs_h", [P, 1]), sb("nm_h", [P, 1])
        st_o, mv_o, ve_o, rs_o, nm_o = sb("st_o", [P, 6]), sb("mv_o", [P, 2]), sb("ve_o", [P, 1]), sb("rs_o", [P, 1]), sb("nm_o", [P, 1])
        ve_a, rs_a = sb("ve_a", [P, 1]), sb("rs_a", [P, 1])
        tok, hc = sb("tok", [P, D]), sb("hc", [P, D])
        h = [sb(f"h{u}", [P, D]) for u in range(2)]
        xn = [sb(f"xn{u}", [P, D]) for u in range(2)]
        hx = [sb(f"hx{u}", [P, D]) for u in range(2)]
        xnT = [sb(f"xnT{u}", [P, KD, R]) for u in range(2)]
        attn, attn_sq, attn_n = sb("attn", [P, D]), sb("attn_sq", [P, D]), sb("attn_n", [P, D])
        mean_sq = sb("mean_sq", [P, 1])
        h2 = [sb(f"h2_{u}", [P, D]) for u in range(2)]
        xf = [sb(f"xf{u}", [P, ROW]) for u in range(2)]
        xfT = [sb(f"xfT{u}", [P, KD, R]) for u in range(2)]
        exinv, nmax, ex, exsum = sb("exinv", [P, 1]), sb("nmax", [P, 1]), sb("ex", [P, NE2]), sb("exsum", [P, 1])
        ranked, others = sb("ranked", [P, NE2]), sb("others", [P, NE2])
        top8 = sb("top8", [P, 8])
        mask = [sb(f"mask{u}", [P, NE2], BF16) for u in range(2)]
        mask_sum = [sb(f"mask_sum{u}", [P, E], BF16) for u in range(2)]
        wsel = sb("wsel", [P, NE2])
        wreal, wzero, wsum, winv = sb("wreal", [P, 1]), sb("wzero", [P, 1]), sb("wsum", [P, 1]), sb("winv", [P, 1])
        wzn, wfac = sb("wzn", [P, 1]), sb("wfac", [P, 1])
        kept, pos_i = sb("kept", [P, E]), sb("pos_i", [P, E], I32)
        hi_i = sb("hi_i", [P, E], I32)
        lo, hi1 = sb("lo", [P, E], F16), sb("hi1", [P, E], F16)
        hot_hi = [sb(f"hot_hi{u}", [P, GROUPS, HI, EG], F16) for u in range(2)]
        hot_lo = [sb(f"hot_lo{u}", [P, GROUPS, LO, EG], F16) for u in range(2)]
        id_lo = [sb(f"id_lo{u}", [P, GROUPS, LO, EG], F16) for u in range(2)]
        tmp_tbl = x1[0][:, 0:GROUPS * EG * LO]
        tbl_part = sb("tbl_part", [P, GROUPS, LO])
        tbl_rows, unused = attn_n[0:E * HALVES, 0:P], hc[:, 0:E * HALVES]
        slot_row = sb("slot_row", [P, E * HALVES], U32)
        over, over_sum, over_rank = sb("over", [1, E]), sb("over_sum", [1, E]), sb("over_rank", [1, E])
        over_at, over_id = x1[1][0:1, 0:E * E], xt[0][0:1, 0:E * E]
        over_list = sb("over_list", [1, E + RING + 1], I32)
        row_idx_all = sb("row_idx", [P, RING], U32)
        row_idx = [row_idx_all[:, r:r + 1] for r in range(RING)]
        in_w = KX * D // ROW
        xe = [w_tok[:, :, :].rearrange("p k n -> p (k n)")[:, r * ROW:(r + 1) * ROW] for r in range(in_w)] + \
             [m_sb[:, :, :].rearrange("p k n -> p (k n)")[:, r * ROW:(r + 1) * ROW] for r in range(RING - in_w)]

        def part_of(tile, k, n):
            return tile.rearrange("p k n -> p (k n)")[:, 0:k * n].rearrange("p (k n) -> p k n", k=k)

        xeT = [part_of(xT[u][:, :, :], KD, P) for u in range(2)]
        silu = [part_of(xnT[u][:, :, :], 1, I)[:, 0, :] for u in range(2)]
        act = [part_of(xfT[u][:, :, :], 1, I)[:, 0, :] for u in range(2)]
        actT = [h[u][:, 0:KI * P].rearrange("p (k n) -> p k n", k=KI) for u in range(2)]
        YRING = 4
        y = [z[:, 0:D] for z in (xt[0], xt[1], x1[0], x1[1])]

        x_loaded = [sem(f"x_loaded{u}") for u in range(2)]
        ln1_loaded, w_tok_loaded, rows_loaded = sem("ln1_loaded"), sem("w_tok_loaded"), sem("rows_loaded")
        w_tok_scaled, b1_part_ready, b1_done, b_ready = sem("w_tok_scaled"), sem("b1_part_ready"), sem("b1_done"), sem("b_ready")
        state_loaded, w_in_loaded, w_out_loaded = sem("state_loaded"), sem("w_in_loaded"), sem("w_out_loaded")
        w_cls_loaded = sem("w_cls_loaded")
        h2_stored = [sem(f"h2_stored{u}") for u in range(2)]
        xf_stored = [sem(f"xf_stored{u}") for u in range(2)]
        spare_stored, tbl_stored, tbl_loaded = sem("spare_stored"), sem("tbl_stored"), sem("tbl_loaded")
        out_stored = sem("out_stored")
        stood = sem("stood")
        made, consts_made, zeros_made = sem("made"), sem("consts_made"), sem("zeros_made")
        setup_links, angles_ready, sincos_ready = sem("setup_links"), sem("angles_ready"), sem("sincos_ready")
        w_in_scaled, rest_ready, part_links = sem("w_in_scaled"), sem("rest_ready"), sem("part_links")
        w_clsT_done, w_clsT_copied = sem("w_clsT_done"), sem("w_clsT_copied")
        w_outT_done, w_outT_copied = sem("w_outT_done"), sem("w_outT_copied")
        m_done, m_copied, state_done, state_copied = sem("m_done"), sem("m_copied"), sem("state_done"), sem("state_copied")
        stats_x_links, x_normed, x_transposed, xT_copied = sem("stats_x_links"), sem("x_normed"), sem("x_transposed"), sem("xT_copied")
        tok_done, tok_read, ln_h_links, h_ready, xn_ready = sem("tok_done"), sem("tok_read"), sem("ln_h_links"), sem("h_ready"), sem("xn_ready")
        hx_ready, xn_transposed, xnT_copied = sem("hx_ready"), sem("xn_transposed"), sem("xnT_copied")
        attn_done, attn_read, sq_done, ln_o_links = sem("attn_done"), sem("attn_read"), sem("sq_done"), sem("ln_o_links")
        h2_ready, xf_ready, xf_transposed, xfT_copied = sem("h2_ready"), sem("xf_ready"), sem("xf_transposed"), sem("xfT_copied")
        var_x_ready, var_t_ready, var_h_ready, var_o_ready = sem("var_x_ready"), sem("var_t_ready"), sem("var_h_ready"), sem("var_o_ready")
        x_links, t_links, h_links, o_links, a_links = sem("x_links"), sem("t_links"), sem("h_links"), sem("o_links"), sem("a_links")
        rs_x_ready, rs_t_ready, rs_h_ready = sem("rs_x_ready"), sem("rs_t_ready"), sem("rs_h_ready")
        rs_o_ready, rs_a_ready = sem("rs_o_ready"), sem("rs_a_ready")
        logits_done, nmax_ready, exp_done, route_links = sem("logits_done"), sem("nmax_ready"), sem("exp_done"), sem("route_links")
        mask_ready, wts_ready, pos_done, pos_read = sem("mask_ready"), sem("wts_ready"), sem("pos_done"), sem("pos_read")
        pos_links, id_ready, numbers_moved, hot_ready, table_done = sem("pos_links"), sem("id_ready"), sem("numbers_moved"), sem("hot_ready"), sem("table_done")
        count_done, tail_links, tbl_ready, tbl_transposed = sem("count_done"), sem("tail_links"), sem("tbl_ready"), sem("tbl_transposed")
        slots_ready, list_ready = sem("slots_ready"), sem("list_ready")
        wgu_loaded = [sem(f"wgu_loaded{r}") for r in range(RING)]
        wdn_loaded = [sem(f"wdn_loaded{r}") for r in range(RING)]
        gathered = [sem(f"gathered{r}") for r in range(RING)]
        idx_ready, xe_transposed, xeT_copied, gu_done = sem("idx_ready"), sem("xe_transposed"), sem("xeT_copied"), sem("gu_done")
        silu_done, act_ready, act_transposed, actT_copied = sem("silu_done"), sem("act_ready"), sem("act_transposed"), sem("actT_copied")
        down_done, y_ready, scattered, all_added = sem("down_done"), sem("y_ready"), sem("scattered"), sem("all_added")

        def stand(eng):
            eng.sem_inc(stood, 1)

        block = ctx.enter_context(nc.Block())

        def has(step):
            return not isinstance(step.i, int) or 0 <= step.off < TILES

        LAG = 4
        LAG_IO = 6
        PEELED = 6

        def tile_steps(eng, body, between=None, lag=LAG):
            looped = (TILES - 1 - PEELED) // 2
            for s in range(PEELED):
                body(Step(0, s, 2))
                if s == 0 and between:
                    between()
            with eng.Fori(0, looped) as i:
                for u in range(2):
                    body(Step(i, PEELED + u, 2))
            for s in range(PEELED + 2 * looped, TILES + lag):
                body(Step(0, s, 2))

        LOOPED_E = (E - 2 * RING) // RING

        def expert_steps(eng, body):
            for e in range(RING):
                body(Step(0, e, RING))
            with eng.Fori(0, LOOPED_E) as i:
                for r in range(RING):
                    body(Step(i, RING + r, RING))
            for e in range(RING + RING * LOOPED_E, E + 1):
                body(Step(0, e, RING))

        def real(step):
            return not isinstance(step.i, int) or 0 <= step.off < E

        def over_steps(eng, body, count):
            with eng.Fori(0, E // RING) as i:
                with eng.If(i * RING < count):
                    for r in range(RING):
                        j = Step(i, r, RING)
                        with eng.If(j.n < count):
                            body(j + E, j)
                        stand(eng)

        def over_count(eng):
            return eng.value_load(over_list[0:1, E + RING:E + RING + 1], min_val=0, max_val=E)

        def over_expert(eng, j):
            return eng.value_load(over_list[0:1, bass.ds(j.n, 1)], min_val=0, max_val=E - 1)

        @block.sync
        def _(sp):
            def load_x(t):
                if not has(t):
                    return
                wait(sp, x_normed, t.n - 1)
                first, rows = t.n * R, (RLAST if t.n == TILES - 1 else R)
                cuts = [n for n in range(1, rows) if (first + n) % NPATCH == 0]
                cuts = [cuts[0], cuts[-1]]
                for a, z in zip([0] + cuts, cuts + [rows]):
                    batch, patch = divmod(first + a, NPATCH)
                    batches = max(1, (z - a) // NPATCH)
                    sp.dma_start(xt[t.slot(2)][a:z, :],
                                 x_rows[batch:batch + batches, patch:patch + (z - a) // batches, :]).then_inc(x_loaded[t.slot(2)], 16)

            def store(sbuf, dram, t, ready, stored):
                if not has(t):
                    return
                last = isinstance(t.i, int) and t.off == TILES - 1
                rows = RLAST if last else R
                sp.wait_ge(ready, t.n + 1)
                sp.dma_start(dram[bass.ds(t.n * R, rows), :], sbuf[t.slot(2)][0:rows, :])\
                    .then_inc(stored[t.slot(2)], 16)

            def load_expert(b, e):
                wait(sp, down_done, b.n - RING + 1)
                r = b.slot(RING)
                sp.dma_start(wgu[r], w_gate_up[bass.ds(e, 1)].rearrange("o (k p) n -> p (o k) n", p=P))\
                    .then_inc(wgu_loaded[r], 16)
                sp.dma_start(wdn[r], w_down[bass.ds(e, 1)].rearrange("o (k p) n -> p (o k) n", p=P))\
                    .then_inc(wdn_loaded[r], 16)

            load_x(Step(0, 0, 2))
            for column, vector in ((g1_col, g1), (b1_col, b1)):
                sp.dma_start(column[:, :], vector.rearrange("(p k) -> p k", k=KX)).then_inc(ln1_loaded, 16)
            sp.dma_start(w_raw, W.rearrange("(p k) n -> p k n", k=KX)).then_inc(w_tok_loaded, 16)
            load_x(Step(0, 1, 2))
            for tile, source in ((theta, A_theta), (s_br, B_real), (s_bi, B_imag), (s_cr, C_real), (s_ci, C_imag)):
                sp.dma_start(tile, source.rearrange("c d s -> (c d) s").rearrange("(p k) s -> p k s", k=KS))\
                    .then_inc(state_loaded, 16)
            sp.dma_start(w_cls_sb, w_cls).then_inc(w_cls_loaded, 16)
            sp.dma_start(w_out_sb, W_out.rearrange("(m p) k -> p m k", p=P)).then_inc(w_out_loaded, 16)
            sp.dma_start(b_all[:, :], b.partition_broadcast(P)).then_inc(rows_loaded, 16)
            sp.dma_start(w_in_sb, W_in.rearrange("(p k) n -> p k n", k=KS)).then_inc(w_in_loaded, 16)
            for row, vector in ((g2_all, g2), (b2_all, b2), (nw_all, norm_w), (rb_all, route_bias)):
                sp.dma_start(row[:, :], vector.partition_broadcast(P)).then_inc(rows_loaded, 16)
            sp.wait_ge(zeros_made, 1)
            sp.dma_start(acc_d[T:T + P, :], zero_row).then_inc(spare_stored, 16)

            def step(s):
                if s.off >= 2:
                    load_x(s)
                store(h2, acc_d, s + -4, h2_ready, h2_stored)
                if has(s + -5):
                    sp.wait_ge(xf_ready, (s + -5).n + 1)
                store(xf, xf_d, s + -5, wts_ready, xf_stored)
                if s.off == 4:
                    sp.wait_ge(b1_done, 1)
                    sp.wait_ge(m_done, KD)
                    sp.wait_ge(spare_stored, 16)
                    sp.wait_ge(state_done, 1)
                if 0 <= s.off - 4 < RING:
                    load_expert(Step(0, s.off - 4, RING), s.off - 4)

            for s in range(TILES + LAG_IO):
                step(Step(0, s, 2))
            sp.wait_ge(tbl_ready, 1)
            tbl_g = tbl_d.rearrange("(g e h l) -> g h e l", g=GROUPS, e=EG, l=LO)
            for g in range(GROUPS):
                sp.dma_start(tbl_g[g], tbl_part[:, g, :]).then_inc(tbl_stored, 16)
            sp.wait_ge(tbl_stored, 16 * GROUPS)
            sp.dma_start(tbl_rows, tbl_d.rearrange("(r s) -> r s", s=P)).then_inc(tbl_loaded, 16)
            with sp.Fori(0, E // RING - 1) as i:
                for r in range(RING):
                    b_ = Step(i, RING + r, RING)
                    load_expert(b_, b_.n)
            sp.wait_ge(list_ready, 1)
            over_steps(sp, lambda b_, j: load_expert(b_, over_expert(sp, j)), over_count(sp))
            sp.wait_ge(all_added, 1)
            sp.dma_start(out_d, acc_d[0:T, :]).then_inc(out_stored, 16)
            sp.wait_ge(out_stored, 16)

        @block.gpsimd
        def _(pool):
            pool.memset(ident[:, :], 0.0).then_inc(made, 1)
            pool.memset(before[:, :], 1.0).then_inc(made, 1)
            pool.memset(ones[:, :], 1.0).then_inc(made, 1)
            pool.memset(ones_e[:, :], 1.0).then_inc(made, 1)
            pool.memset(minus_half[:, :], -0.5).then_inc(made, 1)
            pool.wait_ge(made, 5)
            pool.affine_select(out=ident[:, :], in_=ident[:, :], compare_op=ALU.not_equal, fill=1.0, base=0,
                               pattern=[[-1, P]], channel_multiplier=1).then_inc(made, 1)
            pool.affine_select(out=before[:, :], in_=before[:, :], compare_op=ALU.is_gt, fill=0.0, base=0,
                               pattern=[[1, P]], channel_multiplier=-1).then_inc(made, 1)
            fits = dict(allow_small_or_imprecise_dtypes=True)
            pool.iota(iota_lo[:, :, :, :], pattern=[[0, GROUPS], [1, LO], [0, EG]], base=0, channel_multiplier=0, **fits).then_inc(made, 1)
            pool.iota(iota_hi1[:, :, :, :], pattern=[[0, GROUPS], [1, HI], [0, EG]], base=1, channel_multiplier=0, **fits).then_inc(made, 1)
            pool.iota(iota_e[:, :], pattern=[[1, E]], base=0, channel_multiplier=0, **fits).then_inc(made, 1)
            pool.iota(iota_e1[:, :], pattern=[[1, E]], base=1, channel_multiplier=0, **fits).then_inc(made, 1)
            pool.iota(token_id[:, :], pattern=[[1, 1]], base=1, channel_multiplier=1, **fits).then_inc(made, 1)
            pool.iota(spare_row[:, :], pattern=[[1, 1]], base=T + 1, channel_multiplier=1, **fits).then_inc(made, 1)
            pool.iota(same_i[:, :], pattern=[[-1, EG]], base=0, channel_multiplier=1).then_inc(made, 1)
            pool.wait_ge(made, 14)
            pool.memset(ones_f, 1.0)
            pool.memset(zero_row, 0.0).then_inc(zeros_made, 1)
            pool.sem_inc(consts_made, 1)

            def add_hx(t):
                if not has(t):
                    return
                u = t.slot(2)
                pool.wait_ge(xn_ready, t.n + 1)
                wait(pool, h2_ready, t.n - 1)
                pool.tensor_tensor(hx[u][0:R, :], h[u][0:R, :], xn[u][0:R, :], ALU.add).then_inc(hx_ready, 1)

            def move_numbers(t):
                if not has(t):
                    return
                pool.wait_ge(id_ready, t.n + 1)
                stand(pool)
                pool.tensor_scalar(token_id[:, :], token_id[:, :], float(R), None, ALU.add).then_inc(numbers_moved, 1)

            def rstd(t, sem_, ready, variance, eps, with_eps, rs, done, mean=None, minus_mean=None, used=None):
                if not has(t):
                    return
                links = Links(pool, sem_, t.n * (1 if mean is None else 2))
                pool.wait_ge(ready, t.n + 1)
                stand(pool)
                links.chain(pool.tensor_scalar(with_eps[0:R, :], variance[0:R, :], eps, None, ALU.add))
                if used:
                    wait(pool, used, t.n)
                power = pool.tensor_tensor(rs[0:R, :], with_eps[0:R, :], minus_half[0:R, :], ALU.pow)
                if mean is None:
                    power.then_inc(done, 1)
                else:
                    links.chain(power)
                    stand(pool)
                    pool.tensor_scalar(minus_mean[0:R, :], mean[0:R, :], rs[0:R, :], -1.0, ALU.mult, ALU.mult).then_inc(done, 1)

            def rstd_x(t):
                rstd(t, x_links, var_x_ready, mv_x[:, 1:2], 1e-6, ve_x, rs_x, rs_x_ready, mv_x[:, 0:1], nm_x, x_normed)

            def step(s):
                move_numbers(s + -4)
                rstd(s + -2, a_links, sq_done, mean_sq, 1.1920928955078125e-07, ve_a, rs_a, rs_a_ready)
                rstd_x(s + 1)
                rstd(s + -2, o_links, var_o_ready, mv_o[:, 1:2], 1e-5, ve_o, rs_o, rs_o_ready, mv_o[:, 0:1], nm_o, xf_ready)
                add_hx(s + -1)
                rstd(s, t_links, var_t_ready, mv_t[:, 1:2], 1e-6, ve_t, rs_t, rs_t_ready)
                rstd(s, h_links, var_h_ready, mv_h[:, 1:2], 1e-5, ve_h, rs_h, rs_h_ready, mv_h[:, 0:1], nm_h, xn_ready)

            rstd_x(Step(0, 0, 2))
            tile_steps(pool, step)

            def gather(b_, column):
                r = b_.slot(RING)
                wait(pool, scattered, (b_.n - RING + 1) * 16)
                pool.tensor_copy(row_idx[r], slot_row[:, bass.ds(column, 1)]).then_inc(idx_ready, 1)
                pool.wait_ge(idx_ready, b_.n + 1)
                wait(pool, y_ready, b_.n - RING + 1)
                stand(pool)
                pool.indirect_dma_start(xe[r], None, xf_d, bass.IndirectOffsetOnAxis(ap=row_idx[r], axis=0),
                                        bounds_check=T - 1, oob_is_err=False).then_inc(gathered[r], 16)

            def scatter(b_):
                pool.wait_ge(y_ready, b_.n + 1)
                wait(pool, scattered, b_.n * 16)
                stand(pool)
                pool.indirect_dma_start(acc_d, bass.IndirectOffsetOnAxis(ap=row_idx[b_.slot(RING)], axis=0),
                                        y[b_.slot(YRING)], None, bounds_check=T + P - 1, oob_is_err=True,
                                        compute_op=ALU.add).then_inc(scattered, 16)

            pool.wait_ge(slots_ready, 1)
            pool.wait_ge(spare_stored, 16)
            for u in range(2):
                pool.wait_ge(xf_stored[u], 16 * ((TILES - u + 1) // 2))
                pool.wait_ge(h2_stored[u], 16 * ((TILES - u + 1) // 2))
            AHEAD = 4
            for e in range(AHEAD):
                gather(Step(0, e, RING), HALVES * e)

            pool.wait_ge(list_ready, 1)
            count = over_count(pool)

            def gather_over(b_, j):
                with pool.If(j.n < count):
                    gather(b_, over_expert(pool, j) * HALVES + 1)

            def expert_step(e):
                ahead = e + AHEAD
                if real(ahead):
                    gather(ahead, ahead.n * HALVES)
                elif e.off < E:
                    gather_over(ahead, Step(0, ahead.off - E, RING))
                if real(e + -1):
                    scatter(e + -1)

            expert_steps(pool, expert_step)

            def over_block(b_, j):
                gather_over(b_ + AHEAD, j + AHEAD)
                scatter(b_)

            over_steps(pool, over_block, count)
            pool.wait_ge(scattered, (count + E) * 16)
            pool.sem_inc(all_added, 1)

        @block.scalar
        def _(act_e):
            def copy_xT(t):
                if not has(t):
                    return
                u = t.slot(2)
                act_e.wait_ge(x_transposed, t.n + 1)
                wait(act_e, tok_done, t.n - 1)
                half = KX // 2
                for k in range(2):
                    last = act_e.copy(xT[u][:, k * half:(k + 1) * half, :],
                                      p_xT[k][:, 0:half * R].rearrange("p (k r) -> p k r", r=R))
                last.then_inc(xT_copied, 1)

            def copy_T(t, transposed, psum, to, used, copied):
                if not has(t):
                    return
                act_e.wait_ge(transposed, t.n + 1)
                wait(act_e, used, t.n - 1)
                act_e.copy(to[t.slot(2)][:, :, :], psum[:, 0:KD * R].rearrange("p (k r) -> p k r", r=R)).then_inc(copied, 1)

            def square(t):
                if not has(t):
                    return
                act_e.wait_ge(attn_read, t.n + 1)
                act_e.activation(attn_sq[0:R, :], attn[0:R, :], ACT.Square, scale=float(D) ** -0.5,
                                 accum_out=mean_sq[0:R, :]).then_inc(sq_done, 1)

            def exp(t):
                if not has(t):
                    return
                act_e.wait_ge(nmax_ready, t.n + 1)
                act_e.activation(ex[0:R, :], p_logits[0:R, 0:NE2], ACT.Exp, bias=nmax[0:R, :],
                                 accum_out=exsum[0:R, :]).then_inc(exp_done, 1)

            def normalise(t, used, ready, out_, in_, rs, nm, done, stored=None):
                if not has(t):
                    return
                act_e.wait_ge(ready, t.n + 1)
                wait(act_e, used, t.n - 1)
                if stored:
                    wait(act_e, stored[t.slot(2)], t.turn(2) * 16)
                act_e.activation(out_, in_, ACT.Identity, bias=nm[0:R, :], scale=rs[0:R, :]).then_inc(done, 1)

            def norm_x(t):
                u = t.slot(2)
                normalise(t, x_transposed, rs_x_ready, x1[u][0:R, :], xt[u][0:R, :], rs_x, nm_x, x_normed)

            def norm_h(t):
                u = t.slot(2)
                if has(t):
                    wait(act_e, hx_ready, t.n - 1)
                normalise(t, xn_transposed, rs_h_ready, xn[u][0:R, :], h[u][0:R, :], rs_h, nm_h, xn_ready)

            def norm_o(t):
                u = t.slot(2)
                normalise(t, xf_transposed, rs_o_ready, xf[u][0:R, 0:D], h2[u][0:R, :], rs_o, nm_o, xf_ready, xf_stored)

            def number_tokens(t):
                if not has(t):
                    return
                u = t.slot(2)
                act_e.wait_ge(hot_ready, t.n + 1)
                wait(act_e, numbers_moved, t.n)
                wait(act_e, table_done, t.n - 1)
                act_e.activation(id_lo[u][0:R, :, :, :], hot_lo[u][0:R, :, :, :], ACT.Copy, scale=token_id[0:R, :]).then_inc(id_ready, 1)

            def step(s):
                exp(s + -3)
                square(s + -2)
                norm_x(s + 1)
                if isinstance(s.i, int) and s.off == 0:
                    angles()
                copy_T(s + -1, xn_transposed, p_xnT, xnT, attn_done, xnT_copied)
                norm_o(s + -2)
                copy_T(s + -2, xf_transposed, p_xfT, xfT, logits_done, xfT_copied)
                copy_xT(s + 1)
                if isinstance(s.i, int) and s.off == 0:
                    set_up()
                number_tokens(s + -3)
                norm_h(s)

            def angles():
                act_e.wait_ge(angles_ready, 1)
                act_e.activation(s_cos, s_t1, ACT.Sin)
                act_e.activation(s_sin, s_t2, ACT.Sin).then_inc(sincos_ready, 1)

            def set_up():
                act_e.wait_ge(w_clsT_done, 1)
                act_e.copy(w_clsT[:, :, :], p_logits[:, 0:KD * NE2].rearrange("p (k n) -> p k n", k=KD)).then_inc(w_clsT_copied, 1)
                for k in range(KS):
                    act_e.wait_ge(w_outT_done, k + 1)
                    act_e.copy(w_outT[:, k, :], p_woT[k % 2][:, :]).then_inc(w_outT_copied, 1)
                for m in range(KD):
                    act_e.wait_ge(m_done, m + 1)
                    act_e.copy(m_sb[:, m, :], p_m[m % 2][:, :]).then_inc(m_copied, 1)
                act_e.wait_ge(state_done, 1)
                act_e.copy(state_all[:, :], p_m[0][:, :]).then_inc(state_copied, 1)

            norm_x(Step(0, 0, 2))
            act_e.wait_ge(ln1_loaded, 32)
            act_e.wait_ge(w_tok_loaded, 16)
            for k in range(1, KX, 2):
                act_e.activation(w_tok[:, k, :], w_raw[:, k, :], ACT.Copy, scale=g1_col[:, k:k + 1]).then_inc(w_tok_scaled, 1)
            copy_xT(Step(0, 0, 2))
            tile_steps(act_e, step)

            def copy_xeT(b_):
                u = b_.slot(2)
                act_e.wait_ge(xe_transposed, b_.n + 1)
                wait(act_e, gu_done, b_.n - 1)
                act_e.copy(xeT[u], p_xeT[u][:, :].rearrange("p (k s) -> p k s", k=KD)).then_inc(xeT_copied, 1)

            def silu_gate(b_):
                u = b_.slot(2)
                act_e.wait_ge(gu_done, b_.n + 1)
                wait(act_e, act_ready, b_.n - 1)
                act_e.activation(silu[u], p_gu[u][:, 0:I], ACT.Silu).then_inc(silu_done, 1)

            copy_xeT(Step(0, 0, RING))

            def expert_step(e):
                if real(e):
                    silu_gate(e)
                if real(e + 1):
                    copy_xeT(e + 1)

            expert_steps(act_e, expert_step)
            act_e.wait_ge(list_ready, 1)

            count = over_count(act_e)
            first, second = Step(0, E, RING), Step(0, E + 1, RING)
            with act_e.If(count > 0):
                copy_xeT(first)
                silu_gate(first)
            with act_e.If(count > 1):
                copy_xeT(second)

            def over_block(b_, j):
                with act_e.If((j + 1).n < count):
                    silu_gate(b_ + 1)
                with act_e.If((j + 2).n < count):
                    copy_xeT(b_ + 2)
                stand(act_e)

            over_steps(act_e, over_block, count)

        @block.vector
        def _(dve):
            def stats_x(t):
                if not has(t):
                    return
                u = t.slot(2)
                links = Links(dve, stats_x_links, t.n * 2)
                wait(dve, var_x_ready, t.n)
                dve.wait_ge(x_loaded[u], (t.turn(2) + 1) * 16 * 3)
                links(dve.bn_stats(st_x[0:R, 0, :], xt[u][0:R, 0:DIN // 2]))
                links(dve.bn_stats(st_x[0:R, 1, :], xt[u][0:R, DIN // 2:DIN]))

            def aggr_x(t):
                if not has(t):
                    return
                dve.wait_ge(stats_x_links, t.n * 2 + 2)
                wait(dve, rs_x_ready, t.n)
                stand(dve)
                dve.bn_aggr(mv_x[0:R, :], st_x[0:R, :, :].rearrange("p a b -> p (a b)")).then_inc(var_x_ready, 1)

            class NormH:

                def __init__(self, t):
                    self.t, self.u, self.links = t, t.slot(2), Links(dve, ln_h_links, t.n * 3)

                def read(self):
                    dve.wait_ge(tok_done, self.t.n + 1)
                    dve.tensor_tensor(tok[0:R, :], p_tok[0:R, :], b_all[0:R, :], ALU.add).then_inc(tok_read, 1)

                def stats(self):
                    dve.wait_ge(tok_read, self.t.n + 1)
                    self.links(dve.bn_stats(st_t[0:R, :], tok[0:R, :]))

                def aggregate(self):
                    self.links.after(1)
                    stand(dve)
                    dve.bn_aggr(mv_t[0:R, :], st_t[0:R, :]).then_inc(var_t_ready, 1)

                def centre(self):
                    dve.wait_ge(var_t_ready, self.t.n + 1)
                    self.links(dve.scalar_tensor_tensor(hc[0:R, :], tok[0:R, :], mv_t[0:R, 0:1], g2_all[0:R, :], ALU.subtract, ALU.mult))

                def scale(self):
                    dve.wait_ge(rs_t_ready, self.t.n + 1)
                    self.links.after(2)
                    wait(dve, hx_ready, self.t.n - 1)
                    dve.scalar_tensor_tensor(h[self.u][0:R, :], hc[0:R, :], rs_t[0:R, :], b2_all[0:R, :], ALU.mult, ALU.add).then_inc(h_ready, 1)

                def stats_of_h(self):
                    dve.wait_ge(h_ready, self.t.n + 1)
                    wait(dve, var_h_ready, self.t.n)
                    self.links(dve.bn_stats(st_h[0:R, :], h[self.u][0:R, :]))

                def aggregate_h(self):
                    self.links.after(3)
                    wait(dve, rs_h_ready, self.t.n)
                    stand(dve)
                    dve.bn_aggr(mv_h[0:R, :], st_h[0:R, :]).then_inc(var_h_ready, 1)

            class NormO:

                def __init__(self, t):
                    self.t, self.u, self.links = t, t.slot(2), Links(dve, ln_o_links, t.n * 2)

                def read(self):
                    if isinstance(self.t.i, int) and self.t.off == 0:
                        dve.wait_ge(state_copied, 1)
                    dve.wait_ge(attn_done, self.t.n + 1)
                    dve.tensor_tensor(attn[0:R, :], p_attn[0:R, :], state_all[0:R, :], ALU.add).then_inc(attn_read, 1)

                def scale(self):
                    dve.wait_ge(rs_a_ready, self.t.n + 1)
                    self.links(dve.scalar_tensor_tensor(attn_n[0:R, :], attn[0:R, :], rs_a[0:R, :], nw_all[0:R, :], ALU.mult, ALU.mult))

                def add(self):
                    self.links.after(1)
                    dve.wait_ge(hx_ready, self.t.n + 1)
                    wait(dve, h2_stored[self.u], self.t.turn(2) * 16)
                    wait(dve, xf_ready, self.t.n - 1)
                    dve.tensor_tensor(h2[self.u][0:R, :], attn_n[0:R, :], hx[self.u][0:R, :], ALU.add).then_inc(h2_ready, 1)

                def stats(self):
                    dve.wait_ge(h2_ready, self.t.n + 1)
                    wait(dve, var_o_ready, self.t.n)
                    self.links(dve.bn_stats(st_o[0:R, :], h2[self.u][0:R, :]))

                def aggregate(self):
                    self.links.after(2)
                    wait(dve, rs_o_ready, self.t.n)
                    stand(dve)
                    dve.bn_aggr(mv_o[0:R, :], st_o[0:R, :]).then_inc(var_o_ready, 1)

            class Route:

                def __init__(self, t):
                    self.t, self.u, self.links = t, t.slot(2), Links(dve, route_links, t.n * 11)

                def maximum(self):
                    dve.wait_ge(logits_done, self.t.n + 1)
                    dve.tensor_reduce(nmax[0:R, :], p_logits[0:R, 0:NE2], AX.X, ALU.max, negate=True).then_inc(nmax_ready, 1)

                def invert(self):
                    dve.wait_ge(exp_done, self.t.n + 1)
                    self.links(dve.reciprocal(exinv[0:R, :], exsum[0:R, :]))

                def bias(self):
                    self.links.after(1)
                    self.links(dve.scalar_tensor_tensor(ranked[0:R, :], ex[0:R, :], exinv[0:R, :], rb_all[0:R, :], ALU.mult, ALU.add))

                def best(self):
                    self.links.after(2)
                    stand(dve)
                    self.links(dve.max(top8[0:R, :], ranked[0:R, :]))

                def strike(self):
                    self.links.after(3)
                    stand(dve)
                    self.links(dve.match_replace(others[0:R, :], top8[0:R, :], ranked[0:R, :], -3.0e38))

                def choose(self):
                    self.links.after(4)
                    wait(dve, pos_done, self.t.n)
                    dve.tensor_tensor(mask[self.u][0:R, :], others[0:R, :], ranked[0:R, :], ALU.not_equal).then_inc(mask_ready, 1)

                def weights(self):
                    u = self.u
                    dve.wait_ge(mask_ready, self.t.n + 1)
                    if isinstance(self.t.i, int) and self.t.off == 0:
                        self.links(dve.tensor_copy(mask_sum[u][0:R, :], mask[u][0:R, 0:E]))
                    else:
                        self.links(dve.tensor_tensor(mask_sum[u][0:R, :], mask_sum[1 - u][0:R, :], mask[u][0:R, 0:E], ALU.add))
                    wait(dve, wts_ready, self.t.n)
                    self.links(dve.scalar_tensor_tensor(wsel[0:R, 0:E], ex[0:R, 0:E], exinv[0:R, :], mask[u][0:R, 0:E], ALU.mult, ALU.mult,
                                                        accum_out=wreal[0:R, :]))
                    self.links(dve.scalar_tensor_tensor(wsel[0:R, E:NE2], ex[0:R, E:NE2], exinv[0:R, :], mask[u][0:R, E:NE2], ALU.mult, ALU.mult,
                                                        accum_out=wzero[0:R, :]))

                def total(self):
                    self.links.after(7)
                    self.links(dve.tensor_scalar(wsum[0:R, :], wreal[0:R, :], wzero[0:R, :], 1e-20, ALU.add, ALU.add))

                def invert_total(self):
                    self.links.after(8)
                    self.links(dve.reciprocal(winv[0:R, :], wsum[0:R, :]))

                def zero_weight(self):
                    self.links.after(9)
                    self.links(dve.tensor_scalar(wzn[0:R, :], wzero[0:R, :], winv[0:R, :], SCALE, ALU.mult, ALU.mult))

                def factor(self):
                    self.links.after(10)
                    self.links(dve.tensor_scalar(wfac[0:R, :], wzn[0:R, :], 1.0, winv[0:R, :], ALU.add, ALU.mult))

                def write(self):
                    self.links.after(11)
                    wait(dve, xf_stored[self.u], self.t.turn(2) * 16)
                    dve.tensor_scalar(xf[self.u][0:R, D:ROW], wsel[0:R, 0:E], wfac[0:R, :], SCALE, ALU.mult, ALU.mult).then_inc(wts_ready, 1)

            class Slots:

                def __init__(self, t):
                    self.t, self.u, self.links = t, t.slot(2), Links(dve, pos_links, t.n * 4)

                def read(self):
                    dve.wait_ge(pos_done, self.t.n + 1)
                    self.links(dve.scalar_tensor_tensor(kept[0:R, :], p_pos[0:R, :], float(CAP), mask[self.u][0:R, 0:E], ALU.is_lt, ALU.mult))
                    dve.tensor_copy(pos_i[0:R, :], p_pos[0:R, :]).then_inc(pos_read, 1)

                def high(self):
                    dve.wait_ge(pos_read, self.t.n + 1)
                    self.links(dve.tensor_scalar(hi_i[0:R, :], pos_i[0:R, :], LO.bit_length() - 1, None, ALU.arith_shift_right))

                def low(self):
                    self.links.after(2)
                    wait(dve, hot_ready, self.t.n)
                    self.links(dve.scalar_tensor_tensor(lo[0:R, :], hi_i[0:R, :], float(-LO), pos_i[0:R, :], ALU.mult, ALU.add))
                    self.links(dve.scalar_tensor_tensor(hi1[0:R, :], hi_i[0:R, :], 1.0, kept[0:R, :], ALU.add, ALU.mult))

                def hot(self, out_, iota, part):
                    wide = part[0:R, :].rearrange("p (g e) -> p g e", e=EG).unsqueeze(2).to_broadcast([R, GROUPS, LO, EG])
                    return dve.tensor_tensor(out_[self.u][0:R, :, :, :], iota[0:R, :, :, :], wide, ALU.is_equal)

                def hot_low(self):
                    self.links.after(4)
                    wait(dve, table_done, self.t.n - 1)
                    wait(dve, id_ready, self.t.n - 1)
                    self.hot(hot_lo, iota_lo, lo)

                def hot_high(self):
                    self.hot(hot_hi, iota_hi1, hi1).then_inc(hot_ready, 1)

            def step(s):
                norm_h, norm_o = has(s) and NormH(s), has(s + -2) and NormO(s + -2)
                route, slots = has(s + -3) and Route(s + -3), has(s + -3) and Slots(s + -3)
                if route:
                    route.maximum()
                if norm_o:
                    norm_o.read()
                stats_x(s + 1)
                if route:
                    route.invert()
                aggr_x(s + 1)
                if route:
                    route.bias()
                if norm_o:
                    norm_o.scale()
                if route:
                    route.best()
                if norm_o:
                    norm_o.add()
                if route:
                    route.strike()
                if norm_o:
                    norm_o.stats()
                if route:
                    route.choose()
                if norm_o:
                    norm_o.aggregate()
                if route:
                    route.weights()
                    route.total()
                if isinstance(s.i, int) and s.off == 0:
                    set_up()
                if norm_h:
                    norm_h.read()
                if route:
                    route.invert_total()
                if norm_h:
                    norm_h.stats()
                if route:
                    route.zero_weight()
                    slots.read()
                if norm_h:
                    norm_h.aggregate()
                if route:
                    route.factor()
                    slots.high()
                if norm_h:
                    norm_h.centre()
                if route:
                    route.write()
                    slots.low()
                if norm_h:
                    norm_h.scale()
                if route:
                    slots.hot_low()
                if norm_h:
                    norm_h.stats_of_h()
                if route:
                    slots.hot_high()
                if norm_h:
                    norm_h.aggregate_h()

            def weighted_sum(out_, blocks, column, count, ready, before_it):
                links = Links(dve, part_links, before_it)
                links.chain(dve.tensor_scalar(out_, blocks[:, 0, :], column[:, 0:1], None, ALU.mult))
                for k in range(1, count):
                    last = dve.scalar_tensor_tensor(out_, blocks[:, k, :], column[:, k:k + 1], out_, ALU.mult, ALU.add)
                    if k < count - 1:
                        links.chain(last)
                last.then_inc(ready, 1)

            def set_up():
                links = Links(dve, setup_links, 0)
                dve.wait_ge(state_loaded, 16 * 5)
                dve.wait_ge(consts_made, 1)
                links.chain(dve.tensor_scalar(same_i[:, :], same_i[:, :], EG - 1, None, ALU.bitwise_and))
                links.chain(dve.tensor_scalar(same_expert[:, :], same_i[:, :], 0.0, None, ALU.is_equal))
                links.chain(dve.tensor_scalar(turns[:, :, :], theta, 0.5 / PI, None, ALU.mult))
                links.chain(dve.scalar_tensor_tensor(s_t2, turns[:, :, :], -2 * PI, theta, ALU.mult, ALU.add))
                links.chain(dve.tensor_scalar(s_t2, s_t2, -PI, PI, ALU.max, ALU.min))
                links.chain(dve.scalar_tensor_tensor(s_t1, s_t2, -1.0, s_t2, ALU.mult, ALU.max))
                dve.tensor_scalar(s_t1, s_t1, -1.0, PI / 2, ALU.mult, ALU.add).then_inc(angles_ready, 1)
                links.chain(dve.tensor_tensor(s_br, s_br, s_cr, ALU.mult))
                links.chain(dve.tensor_tensor(s_bi, s_bi, s_ci, ALU.mult))
                links.chain(dve.tensor_tensor(s_br, s_br, s_bi, ALU.subtract))
                links.chain(dve.tensor_reduce(gain[:, :], s_br, AX.X, ALU.add))
                dve.wait_ge(w_in_loaded, 16)
                for k in range(KS):
                    last = dve.tensor_scalar(w_in_sb[:, k, :], w_in_sb[:, k, :], gain[:, k:k + 1], None, ALU.mult)
                last.then_inc(w_in_scaled, 1)
                dve.wait_ge(rows_loaded, 16 * 5)
                dve.wait_ge(b1_done, 1)
                links.chain(dve.tensor_tensor(b_all[:, :], p_attn[:, :], b_all[:, :], ALU.add))
                dve.sem_inc(b_ready, 1)
                dve.wait_ge(sincos_ready, 1)
                links.chain(dve.tensor_scalar(s_t1, s_sin, 0.0, None, ALU.mult))
                links.chain(dve.scalar_tensor_tensor(s_t2, s_cos, 0.0, s_t1, ALU.mult, ALU.subtract))
                links.chain(dve.scalar_tensor_tensor(s_t1, s_cos, 0.0, s_t1, ALU.mult, ALU.add))
                links.chain(dve.tensor_tensor(s_t2, s_t2, s_cr, ALU.mult))
                links.chain(dve.tensor_tensor(s_t1, s_t1, s_ci, ALU.mult))
                links.chain(dve.tensor_tensor(s_t2, s_t2, s_t1, ALU.subtract))
                links.chain(dve.tensor_reduce(rest[:, :], s_t2, AX.X, ALU.add))
                dve.wait_ge(w_outT_copied, KS)
                weighted_sum(rest_part, w_outT, rest, KS, rest_ready, 0 + KX - 1)

            stats_x(Step(0, 0, 2))
            aggr_x(Step(0, 0, 2))
            dve.wait_ge(ln1_loaded, 32)
            dve.wait_ge(w_tok_loaded, 16)
            for k in range(0, KX, 2):
                dve.tensor_scalar(w_tok[:, k, :], w_raw[:, k, :], g1_col[:, k:k + 1], None, ALU.mult).then_inc(w_tok_scaled, 1)
            weighted_sum(b1_part, w_raw, b1_col, KX, b1_part_ready, 0)
            tile_steps(dve, step)

            links = Links(dve, tail_links, 0)
            dve.wait_ge(count_done, 1)
            links.chain(dve.tensor_scalar(over[:, :], p_tok[0:1, 0:E], float(P), None, ALU.is_gt))
            links.chain(dve.tensor_tensor_scan(over_sum[:, :], ones_e[:, :], over[:, :], 0.0, ALU.mult, ALU.add))
            links.chain(dve.tensor_tensor(over_rank[:, :], over_sum[:, :], over[:, :], ALU.mult))
            links.chain(dve.tensor_copy(over_list[:, E + RING:E + RING + 1], over_sum[:, E - 1:E]))
            dve.wait_ge(table_done, TILES)
            links.chain(dve.tensor_tensor(tmp_tbl.rearrange("p (a e) -> p a e", e=EG), p_table[:, :].rearrange("p (a e) -> p a e", e=EG),
                                    same_expert[:, :].unsqueeze(1).to_broadcast([P, GROUPS * LO, EG]), ALU.mult))
            dve.tensor_reduce(tbl_part[:, :, :], tmp_tbl.rearrange("p (g l e) -> p g l e", g=GROUPS, e=EG),
                              AX.X, ALU.add).then_inc(tbl_ready, 1)
            grid = [1, E, E]
            links.chain(dve.tensor_tensor(over_at.rearrange("o (r e) -> o r e", e=E), iota_e1[:, :].unsqueeze(2).to_broadcast(grid),
                                    over_rank[:, :].unsqueeze(1).to_broadcast(grid), ALU.is_equal))
            links.chain(dve.tensor_tensor(over_id.rearrange("o (r e) -> o r e", e=E), over_at.rearrange("o (r e) -> o r e", e=E),
                                    iota_e[:, :].unsqueeze(1).to_broadcast(grid), ALU.mult))
            links.chain(dve.tensor_reduce(over[:, :], over_id.rearrange("o (r e) -> o r e", e=E), AX.X, ALU.add))
            links.chain(dve.tensor_copy(over_list[:, 0:E], over[:, :]))
            dve.wait_ge(tbl_transposed, 1)
            links.chain(dve.tensor_scalar(unused, p_logits[:, 0:E * HALVES], 0.0, spare_row[:, :], ALU.is_equal, ALU.mult))
            dve.scalar_tensor_tensor(slot_row[:, :], p_logits[:, 0:E * HALVES], -1.0, unused, ALU.add, ALU.add).then_inc(slots_ready, 1)
            dve.sem_inc(list_ready, 1)

            def gate_times_up(b_):
                u = b_.slot(2)
                dve.wait_ge(silu_done, b_.n + 1)
                wait(dve, act_transposed, b_.n - 1)
                dve.tensor_tensor(act[u], silu[u], p_gu[u][:, I:2 * I], ALU.mult).then_inc(act_ready, 1)

            def weigh(b_, e):
                u = b_.slot(2)
                dve.wait_ge(down_done, b_.n + 1)
                wait(dve, scattered, (b_.n - YRING + 1) * 16)
                dve.tensor_scalar(y[b_.slot(YRING)], p_y[u][:, :], xe[b_.slot(RING)][:, bass.ds(e + D, 1)], None, ALU.mult).then_inc(y_ready, 1)

            def copy_actT(b_):
                u = b_.slot(2)
                dve.wait_ge(act_transposed, b_.n + 1)
                wait(dve, down_done, b_.n - 1)
                dve.tensor_copy(actT[u], p_actT[u][:, 0:KI * P].rearrange("p (k s) -> p k s", k=KI)).then_inc(actT_copied, 1)

            def expert_step(e):
                if real(e):
                    gate_times_up(e)
                if real(e + -1):
                    weigh(e + -1, (e + -1).n)
                if real(e):
                    copy_actT(e)

            expert_steps(dve, expert_step)

            count = over_count(dve)
            with dve.If(count > 0):
                gate_times_up(Step(0, E, RING))

            def over_block(b_, j):
                copy_actT(b_)
                with dve.If((j + 1).n < count):
                    gate_times_up(b_ + 1)
                weigh(b_, over_expert(dve, j))

            over_steps(dve, over_block, count)

        @block.tensor
        def _(pe):
            def transpose_x(t):
                if not has(t):
                    return
                pe.wait_ge(x_normed, t.n + 1)
                wait(pe, xT_copied, t.n)
                half = KX // 2
                for k in range(KX):
                    last = pe.transpose(p_xT[k // half][:, (k % half) * R:(k % half + 1) * R],
                                        x1[t.slot(2)][0:R, k:DIN:KX], ident[0:R, 0:R])
                last.then_inc(x_transposed, 1)

            def transpose_d(t, ready, source, psum, copied, done):
                if not has(t):
                    return
                pe.wait_ge(ready, t.n + 1)
                wait(pe, copied, t.n)
                for k in range(KD):
                    last = pe.transpose(psum[:, k * R:(k + 1) * R], source[t.slot(2)][0:R, k * P:(k + 1) * P], ident[0:R, 0:R])
                last.then_inc(done, 1)

            def embed(t, blocks):
                if not has(t):
                    return
                if blocks[0] == 0:
                    pe.wait_ge(xT_copied, t.n + 1)
                    wait(pe, tok_read, t.n)
                for k in blocks:
                    last = pe.matmul(p_tok[0:R, :], xT[t.slot(2)][:, k, :], w_tok[:, k, :], start=(k == 0), stop=(k == KX - 1))
                if blocks[-1] == KX - 1:
                    last.then_inc(tok_done, 1)

            def mix(t):
                if not has(t):
                    return
                pe.wait_ge(xnT_copied, t.n + 1)
                wait(pe, attn_read, t.n)
                for k in range(KD):
                    last = pe.matmul(p_attn[0:R, :], xnT[t.slot(2)][:, k, :], m_sb[:, k, :], start=(k == 0), stop=(k == KD - 1))
                last.then_inc(attn_done, 1)

            def logits(t):
                if not has(t):
                    return
                pe.wait_ge(xfT_copied, t.n + 1)
                wait(pe, exp_done, t.n)
                for k in range(KD):
                    last = pe.matmul(p_logits[0:R, 0:NE2], xfT[t.slot(2)][:, k, :], w_clsT[:, k, :], start=(k == 0), stop=(k == KD - 1))
                last.then_inc(logits_done, 1)

            def positions(t):
                if not has(t):
                    return
                first = isinstance(t.i, int) and t.off == 0
                pe.wait_ge(mask_ready, t.n + 1)
                last = pe.matmul(p_pos[0:R, :], before[0:R, 0:R], mask[t.slot(2)][0:R, 0:E], start=True, stop=first)
                if not first:
                    last = pe.matmul(p_pos[0:R, :], ones[0:R, 0:R], mask_sum[1 - t.slot(2)][0:R, :], start=False, stop=True)
                last.then_inc(pos_done, 1)

            def table(t):
                if not has(t):
                    return
                final = isinstance(t.i, int) and t.off == TILES - 1
                rows, u = RLAST if final else R, t.slot(2)
                pe.wait_ge(id_ready, t.n + 1)
                for g in range(GROUPS):
                    last = pe.matmul(p_table[:, g * P:(g + 1) * P], hot_hi[u][0:rows, g, :, :].rearrange("p l e -> p (l e)"),
                                     id_lo[u][0:rows, g, :, :].rearrange("p l e -> p (l e)"),
                                     start=False, stop=final, skip_group_check=True)
                last.then_inc(table_done, 1)

            def step(s):
                embed(s, list(range(KX // 2)))
                transpose_d(s + -1, xn_ready, xn, p_xnT, xnT_copied, xn_transposed)
                embed(s, list(range(KX // 2, KX)))
                positions(s + -3)
                table(s + -4)
                mix(s + -1)
                transpose_d(s + -2, xf_ready, xf, p_xfT, xfT_copied, xf_transposed)
                transpose_x(s + 1)
                if has(s + -3):
                    pe.wait_ge(pos_read, (s + -3).n + 1)
                logits(s + -2)

            def set_up():
                pe.wait_ge(b1_part_ready, 1)
                pe.matmul(p_attn[:, :], ones_f, b1_part, start=True, stop=True).then_inc(b1_done, 1)
                pe.wait_ge(w_cls_loaded, 16)
                for k in range(KD):
                    last = pe.transpose(p_logits[:, k * NE2:(k + 1) * NE2], w_cls_sb[:, k * P:(k + 1) * P], ident[0:NE2, 0:NE2])
                last.then_inc(w_clsT_done, 1)
                pe.wait_ge(w_out_loaded, 16)
                for k in range(KS):
                    if k == 0:
                        pe.wait_ge(w_clsT_copied, 1)
                    if k >= 2:
                        pe.wait_ge(w_outT_copied, k - 1)
                    for m in range(KD):
                        last = pe.transpose(p_woT[k % 2][:, m * P:(m + 1) * P], w_out_sb[:, m, k:NS:KS], ident[:, :])
                    last.then_inc(w_outT_done, 1)
                pe.wait_ge(w_outT_copied, KS)
                pe.wait_ge(w_in_scaled, 1)
                for m in range(KD):
                    if m == 0:
                        pe.wait_ge(b_ready, 1)
                    if m >= 2:
                        pe.wait_ge(m_copied, m - 1)
                    for k in range(KS):
                        last = pe.matmul(p_m[m % 2][:, :], w_in_sb[:, k, m * P:(m + 1) * P], w_outT[:, k, :],
                                         start=(k == 0), stop=(k == KS - 1))
                    last.then_inc(m_done, 1)
                pe.wait_ge(rest_ready, 1)
                pe.wait_ge(m_copied, KD)
                pe.wait_ge(zeros_made, 1)
                pe.matmul(p_table[:, :], zero_row[:, 0:P], zero_row[:, 0:GROUPS * P], start=True, stop=False, skip_group_check=True)
                pe.matmul(p_m[0][:, :], ones_f, rest_part, start=True, stop=True).then_inc(state_done, 1)
                pe.wait_ge(state_copied, 1)

            pe.wait_ge(consts_made, 1)
            transpose_x(Step(0, 0, 2))
            pe.wait_ge(w_tok_scaled, KX)
            tile_steps(pe, step, set_up)
            last_u = (TILES - 1) % 2
            pe.matmul(p_tok[0:32, 0:E], ones[0:R, 0:32], mask_sum[1 - last_u][0:R, :], start=True, stop=False)
            pe.matmul(p_tok[0:32, 0:E], ones[0:RLAST, 0:32], mask[last_u][0:RLAST, 0:E], start=False, stop=True).then_inc(count_done, 1)
            pe.wait_ge(tbl_loaded, 16)
            pe.transpose(p_logits[:, 0:E * HALVES], tbl_rows, ident[0:E * HALVES, 0:E * HALVES]).then_inc(tbl_transposed, 1)

            def transpose_xe(b_):
                u, r = b_.slot(2), b_.slot(RING)
                pe.wait_ge(gathered[r], b_.turn(RING) * 16 + 16)
                wait(pe, xeT_copied, b_.n - 1)
                for k in range(KD):
                    last = pe.transpose(p_xeT[u][:, k * P:(k + 1) * P], xe[r][:, k * P:(k + 1) * P], ident[:, :])
                last.then_inc(xe_transposed, 1)

            def gate_up(b_):
                u, r = b_.slot(2), b_.slot(RING)
                pe.wait_ge(xeT_copied, b_.n + 1)
                pe.wait_ge(wgu_loaded[r], b_.turn(RING) * 16 + 16)
                wait(pe, act_ready, b_.n - 1)
                for k in range(KD):
                    last = pe.matmul(p_gu[u][:, :], xeT[u][:, k, :], wgu[r][:, k, :], start=(k == 0), stop=(k == KD - 1))
                last.then_inc(gu_done, 1)

            def transpose_act(b_):
                u = b_.slot(2)
                pe.wait_ge(act_ready, b_.n + 1)
                wait(pe, actT_copied, b_.n - 1)
                for k in range(KI):
                    last = pe.transpose(p_actT[u][:, k * P:(k + 1) * P], act[u][:, k * P:(k + 1) * P], ident[:, :])
                last.then_inc(act_transposed, 1)

            def down(b_):
                u, r = b_.slot(2), b_.slot(RING)
                pe.wait_ge(actT_copied, b_.n + 1)
                pe.wait_ge(wdn_loaded[r], b_.turn(RING) * 16 + 16)
                wait(pe, y_ready, b_.n - 1)
                for k in range(KI):
                    last = pe.matmul(p_y[u][:, :], actT[u][:, k, :], wdn[r][:, k, :], start=(k == 0), stop=(k == KI - 1))
                last.then_inc(down_done, 1)

            transpose_xe(Step(0, 0, RING))

            def expert_step(e):
                if real(e):
                    gate_up(e)
                if real(e + 1):
                    transpose_xe(e + 1)
                if real(e + -1):
                    down(e + -1)
                if real(e):
                    transpose_act(e)

            expert_steps(pe, expert_step)
            pe.wait_ge(list_ready, 1)

            count = over_count(pe)
            first, second = Step(0, E, RING), Step(0, E + 1, RING)
            with pe.If(count > 0):
                transpose_xe(first)
                gate_up(first)
            with pe.If(count > 1):
                transpose_xe(second)

            def over_block(b_, j):
                with pe.If((j + 1).n < count):
                    gate_up(b_ + 1)
                transpose_act(b_)
                with pe.If((j + 2).n < count):
                    transpose_xe(b_ + 2)
                down(b_)

            over_steps(pe, over_block, count)


_INS = ['x', 'L0_tok_W', 'L0_tok_b', 'L0_tok_g1', 'L0_tok_b1', 'L0_tok_g2', 'L0_tok_b2', 'L0_attn_W_in',
        'L0_attn_W_out', 'L0_attn_A_theta', 'L0_attn_B_real', 'L0_attn_B_imag', 'L0_attn_C_real',
        'L0_attn_C_imag', 'L0_attn_norm_w', 'L0_ffn_w_cls', 'L0_ffn_bias', 'L0_ffn_w_gate_up', 'L0_ffn_w_down']
_OUTS = [((64, 23, 512), 'float32')]


def kernel(**inputs):
    import numpy as _np
    import concourse.bacc as _bacc
    from concourse import mybir as _mybir
    from concourse.bass_utils import run_bass_kernel_spmd as _run

    nc = _bacc.Bacc("TRN2", target_bir_lowering=False, num_devices=1)
    arrays, args = {}, []
    for name in _INS:
        a = _np.ascontiguousarray(inputs[name])
        arrays[f"in_{name}_dram"] = a
        args.append(nc.dram_tensor(f"in_{name}_dram", a.shape, _mybir.dt.from_np(a.dtype), kind="ExternalInput").ap())
    for i, (shape, dtype) in enumerate(_OUTS):
        dt = _mybir.dt.from_np(_np.dtype(dtype))
        args.append(nc.dram_tensor(f"out_{i}_dram", shape, dt, kind="ExternalOutput").ap())
    audio_tower(nc, *args)
    r = _run(nc, [arrays], core_ids=[0])
    return r.results[0]["out_0_dram"]
```

```python
from contextlib import ExitStack

import concourse.bass as bass
from concourse import mybir

F32 = mybir.dt.float32
F32R = mybir.dt.float32r
BF16 = mybir.dt.bfloat16
F16 = mybir.dt.float16
I32 = mybir.dt.int32
U32 = mybir.dt.uint32
ALU = mybir.AluOpType
ACT = mybir.ActivationFunctionType
AX = mybir.AxisListType

P = 128
PI = 3.1415925


class Step:

    def __init__(self, i, off, unroll):
        self.i, self.off, self.unroll = i, off, unroll

    def __add__(self, k):
        return Step(self.i, self.off + k, self.unroll)

    @property
    def n(self):
        return self.off if isinstance(self.i, int) else self.i * self.unroll + self.off

    def slot(self, ring):
        return self.off % ring

    def turn(self, ring):
        here = self.off // ring
        return here if isinstance(self.i, int) else self.i * (self.unroll // ring) + here


def wait(eng, sem, value):
    if not isinstance(value, int) or value > 0:
        eng.wait_ge(sem, value)


class Links:

    def __init__(self, eng, sem, before):
        self.eng, self.sem, self.before, self.n = eng, sem, before, 0

    def __call__(self, instruction):
        self.n += 1
        instruction.then_inc(self.sem, 1)
        return self.n

    def after(self, number):
        self.eng.wait_ge(self.sem, self.before + number)

    def chain(self, instruction):
        self.after(self(instruction))


def audio_tower(nc, x, W, b, g1, b1, g2, b2, W_in, W_out, A_theta, B_real, B_imag, C_real, C_imag,
                norm_w, w_cls, route_bias, w_gate_up, w_down, out):
    BATCH, TIME, FEAT = x.shape
    DIN, D = W.shape
    TIN = DIN // FEAT
    NPATCH = TIME // TIN
    T = BATCH * NPATCH
    R = P
    TILES = -(-T // R)
    RLAST = T - (TILES - 1) * R
    KX = DIN // P
    KD = D // P
    NS = W_in.shape[0]
    KS = NS // P
    DS = A_theta.shape[2]
    NE2 = w_cls.shape[0]
    E = w_gate_up.shape[0]
    I = w_down.shape[1]
    KI = I // P
    CAP = 256
    HALVES = CAP // P
    FEW = P // 2
    LO = 16
    HI = CAP // LO
    EG = P // HI
    GROUPS = E // EG
    SCALE = 1.5
    ROW = D + E
    RING = 8
    WRING = 4

    x_rows = x[:, 0:NPATCH * TIN, :].rearrange("b (n t) f -> b n (t f)", t=TIN)
    xf_d = nc.dram_tensor("token_rows", (T, ROW), F32).ap()
    acc_d = nc.dram_tensor("sums", (T + P, D), F32).ap()
    tbl_d = nc.dram_tensor("slot_table", (E * CAP,), F32).ap()
    out_d = out.rearrange("b n d -> (b n) d")

    ctx = ExitStack()
    with ctx:
        def sb(name, shape, dt=F32):
            return ctx.enter_context(nc.sbuf_tensor(name, shape, dt))

        def sem(name):
            return ctx.enter_context(nc.semaphore(name))

        bank = [ctx.enter_context(nc.psum_tensor(f"bank{i}", [P, 512], F32)) for i in range(8)]
        p_xT = [bank[0], bank[1]]
        p_tok, p_xnT, p_attn, p_xfT, p_logits, p_table = bank[2:8]
        p_pos = p_logits[:, NE2:NE2 + E]
        p_woT = [p_logits, p_table]
        p_m = [p_attn, p_xfT]
        p_gu, p_xeT, p_y, p_actT = [bank[0], bank[1]], [bank[2], bank[3]], [bank[4], bank[6]], [bank[5], bank[7]]

        ident = sb("ident", [P, P])
        before = sb("before", [P, P], BF16)
        ones = sb("ones", [P, P], BF16)
        same_i, same_expert = sb("same_i", [P, EG], I32), sb("same_expert", [P, EG])
        iota_lo = sb("iota_lo", [P, GROUPS, LO, EG], F16)
        iota_hi1 = sb("iota_hi1", [P, GROUPS, EG, HI], F16)
        iota_e = sb("iota_e", [1, E])
        iota_e1 = sb("iota_e1", [1, E])
        ones_e = sb("ones_e", [1, E])
        token_id = sb("token_id", [P, 1])
        spare_row = sb("spare_row", [P, 1])
        w_hi, w_lo = sb("w_hi", [P, KX, D], F32R), sb("w_lo", [P, KX, D], F32R)
        g1_col, b1_col = sb("g1_col", [P, KX]), sb("b1_col", [P, KX])
        g2_all, b2_all, nw_all = sb("g2_all", [P, D]), sb("b2_all", [P, D]), sb("nw_all", [P, D])
        b_rows, state_rows = sb("b_rows", [P, D], F32R), sb("state_rows", [P, D], F32R)
        halves = sb("halves", [P, P], F32R)
        rb_all = sb("rb_all", [P, NE2])
        w_clsT = sb("w_clsT", [P, KD, NE2])
        m_hi, m_lo = sb("m_hi", [P, KD, D], F32R), sb("m_lo", [P, KD, D], F32R)
        turns = sb("turns", [P, KS, DS], I32)
        gain = sb("gain", [P, KS])
        rest = sb("rest", [P, KS])
        minus_half = sb("minus_half", [P, 1])
        ring = sb("ring", [P, WRING, (KD + KI) * D])
        wgu = [ring[:, r, 0:KD * D].rearrange("p (k n) -> p k n", k=KD) for r in range(WRING)]
        wdn = [ring[:, r, KD * D:(KD + KI) * D].rearrange("p (k n) -> p k n", k=KI) for r in range(WRING)]
        flat = ring[:, :, :].rearrange("p r n -> p (r n)")
        w_in_sb = flat[:, 0:KS * D].rearrange("p (k n) -> p k n", k=KS)
        w_out_sb = flat[:, KS * D:2 * KS * D].rearrange("p (m k) -> p m k", m=KD)
        w_outT = flat[:, 2 * KS * D:3 * KS * D].rearrange("p (k n) -> p k n", k=KS)
        w_raw = flat[:, 2 * KS * D:(2 * KS + KX) * D].rearrange("p (k n) -> p k n", k=KX)
        small = sb("small", [P, 4 * D + P + 9 * KS * DS])
        b1_part, rest_part, b_all = (small[:, n * D:(n + 1) * D] for n in range(3))
        w_cls_sb = small[0:NE2, 3 * D:4 * D]
        ones_f = small[:, 4 * D:4 * D + P]
        theta, s_br, s_bi, s_cr, s_ci, s_t1, s_t2, s_cos, s_sin = (
            small[:, 4 * D + P + n * KS * DS:4 * D + P + (n + 1) * KS * DS].rearrange("p (k s) -> p k s", k=KS) for n in range(9))
        xt = [sb(f"xt{u}", [P, DIN]) for u in range(2)]
        x1 = [sb(f"x1_{u}", [P, DIN]) for u in range(2)]
        xT = [sb(f"xT{u}", [P, KX, R], F32R) for u in range(2)]
        xT_lo, xnT_lo = sb("xT_lo", [P, KX, R], F32R), sb("xnT_lo", [P, KD, R], F32R)
        st_x, mv_x, ve_x, rs_x, nm_x = sb("st_x", [P, 2, 6]), sb("mv_x", [P, 2]), sb("ve_x", [P, 1]), sb("rs_x", [P, 1]), sb("nm_x", [P, 1])
        st_t, mv_t, ve_t, rs_t = sb("st_t", [P, 6]), sb("mv_t", [P, 2]), sb("ve_t", [P, 1]), sb("rs_t", [P, 1])
        st_h, mv_h, ve_h, rs_h, nm_h = sb("st_h", [P, 6]), sb("mv_h", [P, 2]), sb("ve_h", [P, 1]), sb("rs_h", [P, 1]), sb("nm_h", [P, 1])
        st_o, mv_o, ve_o, rs_o, nm_o = sb("st_o", [P, 6]), sb("mv_o", [P, 2]), sb("ve_o", [P, 1]), sb("rs_o", [P, 1]), sb("nm_o", [P, 1])
        ve_a, rs_a = sb("ve_a", [P, 1]), sb("rs_a", [P, 1])
        hc = sb("hc", [P, D])
        h = [sb(f"h{u}", [P, D]) for u in range(2)]
        xn = [sb(f"xn{u}", [P, D]) for u in range(2)]
        hx = [sb(f"hx{u}", [P, D]) for u in range(2)]
        xnT = [sb(f"xnT{u}", [P, KD, R], F32R) for u in range(2)]
        attn_sq, attn_n = sb("attn_sq", [P, D]), sb("attn_n", [P, D])
        mean_sq = sb("mean_sq", [P, 1])
        h2 = [sb(f"h2_{u}", [P, D]) for u in range(2)]
        zero_row = h2[1][:, :]
        xf = [sb(f"xf{u}", [P, ROW]) for u in range(2)]
        xfT = [sb(f"xfT{u}", [P, KD, R]) for u in range(2)]
        exinv, nmax, ex, exsum = sb("exinv", [P, 1]), sb("nmax", [P, 1]), sb("ex", [P, NE2]), sb("exsum", [P, 1])
        ranked, others = sb("ranked", [P, NE2]), sb("others", [P, NE2])
        top8 = sb("top8", [P, 8])
        mask = [sb(f"mask{u}", [P, NE2], BF16) for u in range(2)]
        mask_sum = [sb(f"mask_sum{u}", [P, E], BF16) for u in range(2)]
        wsel = sb("wsel", [P, NE2])
        wreal, wzero, wsum, winv = sb("wreal", [P, 1]), sb("wzero", [P, 1]), sb("wsum", [P, 1]), sb("winv", [P, 1])
        wzn, wfac = sb("wzn", [P, 1]), sb("wfac", [P, 1])
        kept, pos_i = sb("kept", [P, E]), sb("pos_i", [P, E], I32)
        hi_i = sb("hi_i", [P, E], I32)
        lo, hi1 = sb("lo", [P, E], F16), sb("hi1", [P, E], F16)
        hot_hi = [sb(f"hot_hi{u}", [P, GROUPS, EG, HI], F16) for u in range(2)]
        hot_lo = [sb(f"hot_lo{u}", [P, GROUPS, LO, EG], F16) for u in range(2)]
        id_lo = [sb(f"id_lo{u}", [P, GROUPS, LO, EG], F16) for u in range(2)]
        tmp_tbl = x1[0][:, 0:GROUPS * EG * LO]
        tbl_part = sb("tbl_part", [P, GROUPS, LO])
        tbl_rows, unused = attn_n[0:E * HALVES, 0:P], hc[:, 0:E * HALVES]
        slot_row = sb("slot_row", [P, E * HALVES], U32)
        many = sb("many", [1, E], I32)
        over, over_sum, over_rank = sb("over", [1, E]), sb("over_sum", [1, E]), sb("over_rank", [1, E])
        over_at, over_id = x1[1][0:1, 0:E * E], xt[0][0:1, 0:E * E]
        over_list = sb("over_list", [1, E + RING + 2], I32)
        row_idx_all = sb("row_idx", [P, RING], U32)
        row_idx = [row_idx_all[:, r:r + 1] for r in range(RING)]
        in_small = small.shape[1] // ROW
        xe = [small[:, r * ROW:(r + 1) * ROW] for r in range(in_small)] + [xf[u][:, :] for u in range(RING - in_small)]
        silu = [xn[u][:, 0:I] for u in range(2)]
        act = [xn[u][:, I:2 * I] for u in range(2)]

        def pieces(tile, k, n, at=0):
            flat_ = tile.rearrange("p a b -> p (a b)")
            return flat_[:, at:at + k * n].rearrange("p (k n) -> p k n", k=k)

        xeT = [pieces(xT[u][:, :, :], KD, P) for u in range(2)]
        xeT_lo = [pieces(xT_lo[:, :, :], KD, P, u * KD * P) for u in range(2)]
        actT = [pieces(xnT[u][:, :, :], KI, P) for u in range(2)]
        actT_lo = [pieces(xnT_lo[:, :, :], KI, P, u * KI * P) for u in range(2)]
        wgu_hi, wgu_lo = ([pieces(w[:, :, :], KD, D), m[:, :, :]] for w, m in ((w_hi, m_hi), (w_lo, m_lo)))
        wdn_hi, wdn_lo = ([pieces(w[:, :, :], KI, D, (KD + u * KI) * D) for u in range(2)] for w in (w_hi, w_lo))
        YRING = 4
        y = [z[:, 0:D] for z in (xt[0], xt[1], x1[0], x1[1])]

        x_loaded = [sem(f"x_loaded{u}") for u in range(2)]
        ln1_loaded, w_tok_loaded, rows_loaded = sem("ln1_loaded"), sem("w_tok_loaded"), sem("rows_loaded")
        w_hi_ready, w_lo_ready = sem("w_hi_ready"), sem("w_lo_ready")
        halves_ready = sem("halves_ready")
        b1_part_ready, b1_done, b_ready = sem("b1_part_ready"), sem("b1_done"), sem("b_ready")
        state_loaded, w_in_loaded, w_out_loaded = sem("state_loaded"), sem("w_in_loaded"), sem("w_out_loaded")
        w_cls_loaded = sem("w_cls_loaded")
        h2_stored = [sem(f"h2_stored{u}") for u in range(2)]
        xf_stored = [sem(f"xf_stored{u}") for u in range(2)]
        spare_stored, tbl_stored, tbl_loaded = sem("spare_stored"), sem("tbl_stored"), sem("tbl_loaded")
        out_stored = sem("out_stored")
        stood = sem("stood")
        made, consts_made, zeros_made = sem("made"), sem("consts_made"), sem("zeros_made")
        setup_links, angles_ready, sincos_ready = sem("setup_links"), sem("angles_ready"), sem("sincos_ready")
        w_in_scaled, rest_ready, part_links = sem("w_in_scaled"), sem("rest_ready"), sem("part_links")
        w_clsT_done, w_clsT_copied = sem("w_clsT_done"), sem("w_clsT_copied")
        w_outT_done, w_outT_copied = sem("w_outT_done"), sem("w_outT_copied")
        m_done, m_hi_ready, m_lo_ready, state_done, state_ready = sem("m_done"), sem("m_hi_ready"), sem("m_lo_ready"), sem("state_done"), sem("state_ready")
        stats_x_links, x_normed, x_transposed, xT_copied = sem("stats_x_links"), sem("x_normed"), sem("x_transposed"), sem("xT_copied")
        xT_lo_ready, xnT_lo_ready = sem("xT_lo_ready"), sem("xnT_lo_ready")
        tok_done, tok_read, ln_h_links, h_ready, xn_ready = sem("tok_done"), sem("tok_read"), sem("ln_h_links"), sem("h_ready"), sem("xn_ready")
        hx_ready, xn_transposed, xnT_copied = sem("hx_ready"), sem("xn_transposed"), sem("xnT_copied")
        attn_done, attn_read, sq_done, ln_o_links = sem("attn_done"), sem("attn_read"), sem("sq_done"), sem("ln_o_links")
        h2_ready, xf_ready, xf_transposed, xfT_copied = sem("h2_ready"), sem("xf_ready"), sem("xf_transposed"), sem("xfT_copied")
        var_x_ready, var_t_ready, var_h_ready, var_o_ready = sem("var_x_ready"), sem("var_t_ready"), sem("var_h_ready"), sem("var_o_ready")
        x_links, t_links, h_links, o_links, a_links = sem("x_links"), sem("t_links"), sem("h_links"), sem("o_links"), sem("a_links")
        rs_x_ready, rs_t_ready, rs_h_ready = sem("rs_x_ready"), sem("rs_t_ready"), sem("rs_h_ready")
        rs_o_ready, rs_a_ready = sem("rs_o_ready"), sem("rs_a_ready")
        logits_done, nmax_ready, exp_done, route_links = sem("logits_done"), sem("nmax_ready"), sem("exp_done"), sem("route_links")
        mask_ready, wts_ready, pos_done, pos_read = sem("mask_ready"), sem("wts_ready"), sem("pos_done"), sem("pos_read")
        pos_links, id_ready, numbers_moved, hot_ready, table_done = sem("pos_links"), sem("id_ready"), sem("numbers_moved"), sem("hot_ready"), sem("table_done")
        count_done, tail_links, tbl_ready, tbl_transposed = sem("count_done"), sem("tail_links"), sem("tbl_ready"), sem("tbl_transposed")
        slots_ready, list_ready = sem("slots_ready"), sem("list_ready")
        wgu_loaded = [sem(f"wgu_loaded{r}") for r in range(WRING)]
        wdn_loaded = [sem(f"wdn_loaded{r}") for r in range(WRING)]
        gathered = [sem(f"gathered{r}") for r in range(RING)]
        wgu_hi_ready, wgu_lo_ready = sem("wgu_hi_ready"), sem("wgu_lo_ready")
        wdn_hi_ready, wdn_lo_ready = sem("wdn_hi_ready"), sem("wdn_lo_ready")
        xeT_lo_ready, actT_lo_ready = sem("xeT_lo_ready"), sem("actT_lo_ready")
        idx_ready, xe_transposed, xeT_copied, gu_done = sem("idx_ready"), sem("xe_transposed"), sem("xeT_copied"), sem("gu_done")
        silu_done, act_ready, act_transposed, actT_copied = sem("silu_done"), sem("act_ready"), sem("act_transposed"), sem("actT_copied")
        down_done, y_ready, scattered, all_added = sem("down_done"), sem("y_ready"), sem("scattered"), sem("all_added")

        def stand(eng):
            eng.sem_inc(stood, 1)

        block = ctx.enter_context(nc.Block())

        def has(step):
            return not isinstance(step.i, int) or 0 <= step.off < TILES

        LAG = 4
        LAG_IO = 7
        PEELED = 6

        def tile_steps(eng, body, between=None, lag=LAG):
            looped = (TILES - 1 - PEELED) // 2
            for s in range(PEELED):
                body(Step(0, s, 2))
                if s == 0 and between:
                    between()
            with eng.Fori(0, looped) as i:
                for u in range(2):
                    body(Step(i, PEELED + u, 2))
            for s in range(PEELED + 2 * looped, TILES + lag):
                body(Step(0, s, 2))

        LOOPED_E = (E - 2 * RING) // RING

        def expert_steps(eng, body):
            for e in range(RING):
                body(Step(0, e, RING))
            with eng.Fori(0, LOOPED_E) as i:
                for r in range(RING):
                    body(Step(i, RING + r, RING))
            for e in range(RING + RING * LOOPED_E, E):
                body(Step(0, e, RING))

        def if_real(eng, count, step, body):
            if isinstance(step.i, int) and step.off >= E:
                with eng.If(count > step.off - E):
                    body(step)
            elif not isinstance(step.i, int) or step.off >= 0:
                body(step)

        def over_steps(eng, body, count, extra=1, finish=None):
            with eng.Fori(0, E // RING) as i:
                with eng.If(i * RING < count + extra):
                    for r in range(RING):
                        j = Step(i, r, RING)
                        with eng.If(j.n < count + extra):
                            body(j + E, j)
                        stand(eng)
            if finish:
                with eng.If(count > E - 1):
                    finish(Step(0, 2 * E - 1, RING))

        def over_count(eng):
            return eng.value_load(over_list[0:1, E + RING + 1:E + RING + 2], min_val=0, max_val=E)

        def over_expert(eng, j):
            return eng.value_load(over_list[0:1, bass.ds(j.n + 1, 1)], min_val=0, max_val=E - 1)

        @block.sync
        def _(sp):
            def load_x(t):
                if not has(t):
                    return
                wait(sp, x_normed, t.n - 1)
                first, rows = t.n * R, (RLAST if t.n == TILES - 1 else R)
                cuts = [n for n in range(1, rows) if (first + n) % NPATCH == 0]
                cuts = [cuts[0], cuts[-1]]
                for a, z in zip([0] + cuts, cuts + [rows]):
                    batch, patch = divmod(first + a, NPATCH)
                    batches = max(1, (z - a) // NPATCH)
                    sp.dma_start(xt[t.slot(2)][a:z, :],
                                 x_rows[batch:batch + batches, patch:patch + (z - a) // batches, :]).then_inc(x_loaded[t.slot(2)], 16)

            def store(sbuf, dram, t, ready, stored):
                if not has(t):
                    return
                last = isinstance(t.i, int) and t.off == TILES - 1
                rows = RLAST if last else R
                sp.wait_ge(ready, t.n + 1)
                sp.dma_start(dram[bass.ds(t.n * R, rows), :], sbuf[t.slot(2)][0:rows, :])\
                    .then_inc(stored[t.slot(2)], 16)

            def load_expert(b, e):
                wait(sp, wgu_lo_ready, (b.n - WRING + 1) * 2)
                wait(sp, wdn_lo_ready, b.n - WRING + 1)
                r = b.slot(WRING)
                sp.dma_start(wgu[r], w_gate_up[bass.ds(e, 1)].rearrange("o (k p) n -> p (o k) n", p=P))\
                    .then_inc(wgu_loaded[r], 16)
                sp.dma_start(wdn[r], w_down[bass.ds(e, 1)].rearrange("o (k p) n -> p (o k) n", p=P))\
                    .then_inc(wdn_loaded[r], 16)

            load_x(Step(0, 0, 2))
            for column, vector in ((g1_col, g1), (b1_col, b1)):
                sp.dma_start(column[:, :], vector.rearrange("(p k) -> p k", k=KX)).then_inc(ln1_loaded, 16)
            load_x(Step(0, 1, 2))
            sp.dma_start(w_raw, W.rearrange("(p k) n -> p k n", k=KX)).then_inc(w_tok_loaded, 16)
            for tile, source in ((theta, A_theta), (s_br, B_real), (s_bi, B_imag), (s_cr, C_real), (s_ci, C_imag)):
                sp.dma_start(tile, source.rearrange("c d s -> (c d) s").rearrange("(p k) s -> p k s", k=KS))\
                    .then_inc(state_loaded, 16)
            sp.dma_start(w_cls_sb, w_cls).then_inc(w_cls_loaded, 16)
            sp.dma_start(w_out_sb, W_out.rearrange("(m p) k -> p m k", p=P)).then_inc(w_out_loaded, 16)
            sp.dma_start(b_all[:, :], b.partition_broadcast(P)).then_inc(rows_loaded, 16)
            sp.dma_start(w_in_sb, W_in.rearrange("(p k) n -> p k n", k=KS)).then_inc(w_in_loaded, 16)
            for row, vector in ((g2_all, g2), (b2_all, b2), (nw_all, norm_w), (rb_all, route_bias)):
                sp.dma_start(row[:, :], vector.partition_broadcast(P)).then_inc(rows_loaded, 16)
            sp.wait_ge(zeros_made, 1)
            sp.dma_start(acc_d[T:T + P, :], zero_row).then_inc(spare_stored, 16)

            def step(s):
                if s.off >= 2:
                    load_x(s)
                store(h2, acc_d, s + -5, h2_ready, h2_stored)
                if has(s + -6):
                    sp.wait_ge(xf_ready, (s + -6).n + 1)
                store(xf, xf_d, s + -6, wts_ready, xf_stored)
                if s.off == 4:
                    sp.wait_ge(b1_done, 1)
                    sp.wait_ge(m_done, KD)
                    sp.wait_ge(state_done, 1)
                if 0 <= s.off - 4 < WRING:
                    load_expert(Step(0, s.off - 4, RING), s.off - 4)

            for s in range(TILES + LAG_IO):
                step(Step(0, s, 2))
            sp.wait_ge(tbl_ready, 1)
            sp.dma_start(tbl_d.rearrange("(g p l) -> p g l", g=GROUPS, l=LO), tbl_part[:, :, :]).then_inc(tbl_stored, 16)
            sp.wait_ge(tbl_stored, 16)
            sp.dma_start(tbl_rows, tbl_d.rearrange("(r s) -> r s", s=P)).then_inc(tbl_loaded, 16)
            for e in range(WRING, RING):
                load_expert(Step(0, e, RING), e)
            with sp.Fori(0, E // RING - 1) as i:
                for r in range(RING):
                    b_ = Step(i, RING + r, RING)
                    load_expert(b_, b_.n)
            sp.wait_ge(list_ready, 1)
            over_steps(sp, lambda b_, j: load_expert(b_, over_expert(sp, j)), over_count(sp), 0)
            sp.wait_ge(all_added, 1)
            sp.dma_start(out_d, acc_d[0:T, :]).then_inc(out_stored, 16)
            sp.wait_ge(out_stored, 16)

        @block.gpsimd
        def _(pool):
            pool.memset(ident[:, :], 0.0).then_inc(made, 1)
            pool.memset(before[:, :], 1.0).then_inc(made, 1)
            pool.memset(ones[:, :], 1.0).then_inc(made, 1)
            pool.memset(ones_e[:, :], 1.0).then_inc(made, 1)
            pool.memset(minus_half[:, :], -0.5).then_inc(made, 1)
            pool.wait_ge(made, 5)
            pool.affine_select(out=ident[:, :], in_=ident[:, :], compare_op=ALU.not_equal, fill=1.0, base=0,
                               pattern=[[-1, P]], channel_multiplier=1).then_inc(made, 1)
            pool.affine_select(out=before[:, :], in_=before[:, :], compare_op=ALU.is_gt, fill=0.0, base=0,
                               pattern=[[1, P]], channel_multiplier=-1).then_inc(made, 1)
            fits = dict(allow_small_or_imprecise_dtypes=True)
            pool.iota(iota_lo[:, :, :, :], pattern=[[0, GROUPS], [1, LO], [0, EG]], base=0, channel_multiplier=0, **fits).then_inc(made, 1)
            pool.iota(iota_hi1[:, :, :, :], pattern=[[0, GROUPS], [0, EG], [1, HI]], base=1, channel_multiplier=0, **fits).then_inc(made, 1)
            pool.iota(iota_e[:, :], pattern=[[1, E]], base=0, channel_multiplier=0, **fits).then_inc(made, 1)
            pool.iota(iota_e1[:, :], pattern=[[1, E]], base=1, channel_multiplier=0, **fits).then_inc(made, 1)
            pool.iota(token_id[:, :], pattern=[[1, 1]], base=1, channel_multiplier=1, **fits).then_inc(made, 1)
            pool.iota(spare_row[:, :], pattern=[[1, 1]], base=T + 1, channel_multiplier=1, **fits).then_inc(made, 1)
            pool.iota(same_i[:, :], pattern=[[-HI, EG]], base=0, channel_multiplier=1).then_inc(made, 1)
            pool.wait_ge(made, 14)
            pool.memset(ones_f, 1.0).then_inc(made, 1)
            pool.wait_ge(made, 15)
            pool.memset(small[NE2:P, 3 * D:4 * D], 0.0).then_inc(made, 1)
            pool.wait_ge(made, 16)
            pool.iota(over_list[:, 0:1], pattern=[[0, 1]], base=E - 1, channel_multiplier=0)
            pool.memset(zero_row, 0.0).then_inc(zeros_made, 1)
            pool.sem_inc(consts_made, 1)

            def add_hx(t):
                if not has(t):
                    return
                u = t.slot(2)
                pool.wait_ge(xn_ready, t.n + 1)
                wait(pool, h2_ready, t.n - 1)
                pool.tensor_tensor(hx[u][0:R, :], h[u][0:R, :], xn[u][0:R, :], ALU.add).then_inc(hx_ready, 1)

            def add_h2(t):
                if not has(t):
                    return
                u = t.slot(2)
                pool.wait_ge(attn_read, t.n + 1)
                pool.wait_ge(hx_ready, t.n + 1)
                wait(pool, h2_stored[u], t.turn(2) * 16)
                wait(pool, xf_ready, t.n - 1)
                pool.tensor_tensor(h2[u][0:R, :], attn_n[0:R, :], hx[u][0:R, :], ALU.add).then_inc(h2_ready, 1)

            def move_numbers(t):
                if not has(t):
                    return
                pool.wait_ge(id_ready, t.n + 1)
                stand(pool)
                pool.tensor_scalar(token_id[:, :], token_id[:, :], float(R), None, ALU.add).then_inc(numbers_moved, 1)

            def rstd(t, sem_, ready, variance, eps, with_eps, rs, done, mean=None, minus_mean=None, used=None):
                if not has(t):
                    return
                links = Links(pool, sem_, t.n * (1 if mean is None else 2))
                pool.wait_ge(ready, t.n + 1)
                stand(pool)
                links.chain(pool.tensor_scalar(with_eps[0:R, :], variance[0:R, :], eps, None, ALU.add))
                if used:
                    wait(pool, used, t.n)
                power = pool.tensor_tensor(rs[0:R, :], with_eps[0:R, :], minus_half[0:R, :], ALU.pow)
                if mean is None:
                    power.then_inc(done, 1)
                else:
                    links.chain(power)
                    stand(pool)
                    pool.tensor_scalar(minus_mean[0:R, :], mean[0:R, :], rs[0:R, :], -1.0, ALU.mult, ALU.mult).then_inc(done, 1)

            def rstd_x(t):
                rstd(t, x_links, var_x_ready, mv_x[:, 1:2], 1e-6, ve_x, rs_x, rs_x_ready, mv_x[:, 0:1], nm_x, x_normed)

            def step(s):
                first = isinstance(s.i, int) and s.off == 0
                rstd(s + -2, a_links, sq_done, mean_sq, 1.1920928955078125e-07, ve_a, rs_a, rs_a_ready)
                if not first:
                    rstd_x(s + 2)
                add_h2(s + -2)
                move_numbers(s + -4)
                add_hx(s + -1)
                rstd(s, t_links, var_t_ready, mv_t[:, 1:2], 1e-6, ve_t, rs_t, rs_t_ready)
                rstd(s + -2, o_links, var_o_ready, mv_o[:, 1:2], 1e-5, ve_o, rs_o, rs_o_ready, mv_o[:, 0:1], nm_o, xf_ready)
                rstd(s, h_links, var_h_ready, mv_h[:, 1:2], 1e-5, ve_h, rs_h, rs_h_ready, mv_h[:, 0:1], nm_h, xn_ready)
                if first:
                    rstd_x(s + 2)

            rstd_x(Step(0, 0, 2))
            rstd_x(Step(0, 1, 2))
            tile_steps(pool, step)

            def gather(b_, column):
                r = b_.slot(RING)
                wait(pool, scattered, (b_.n - RING + 1) * 16)
                pool.tensor_copy(row_idx[r], slot_row[:, bass.ds(column, 1)]).then_inc(idx_ready, 1)
                pool.wait_ge(idx_ready, b_.n + 1)
                wait(pool, y_ready, b_.n - RING + 1)
                stand(pool)

                def start(n):
                    pool.indirect_dma_start(xe[r][0:n, :], None, xf_d, bass.IndirectOffsetOnAxis(ap=row_idx[r][0:n, :], axis=0),
                                            bounds_check=T - 1, oob_is_err=False).then_inc(gathered[r], 16)
                return start

            def scatter(b_):
                pool.wait_ge(y_ready, b_.n + 1)
                wait(pool, scattered, b_.n * 16)
                stand(pool)

                def start(n):
                    pool.indirect_dma_start(acc_d, bass.IndirectOffsetOnAxis(ap=row_idx[b_.slot(RING)][0:n, :], axis=0),
                                            y[b_.slot(YRING)][0:n, :], None, bounds_check=T + P - 1, oob_is_err=True,
                                            compute_op=ALU.add).then_inc(scattered, 16)
                return start

            def sized(e, start):
                above = pool.value_load(many[0:1, bass.ds(e, 1)], min_val=0, max_val=1)
                with pool.If(above > 0):
                    start(P)
                with pool.If(above < 1):
                    start(FEW)

            pool.wait_ge(slots_ready, 1)
            pool.wait_ge(spare_stored, 16)
            for u in range(2):
                pool.wait_ge(xf_stored[u], 16 * ((TILES - u + 1) // 2))
                pool.wait_ge(h2_stored[u], 16 * ((TILES - u + 1) // 2))
            AHEAD = 4
            for e in range(AHEAD):
                sized(e, gather(Step(0, e, RING), HALVES * e))

            pool.wait_ge(list_ready, 1)
            count = over_count(pool)

            def gather_over(b_, j):
                with pool.If(j.n < count):
                    gather(b_, over_expert(pool, j) * HALVES + 1)(P)

            def expert_step(e):
                ahead = e + AHEAD
                if isinstance(ahead.i, int) and ahead.off >= E:
                    gather_over(ahead, Step(0, ahead.off - E, RING))
                else:
                    sized(ahead.n, gather(ahead, ahead.n * HALVES))
                if not isinstance(e.i, int) or e.off > 0:
                    sized((e + -1).n, scatter(e + -1))

            expert_steps(pool, expert_step)

            def over_block(b_, j):
                gather_over(b_ + AHEAD, j + AHEAD)
                scatter(b_ + -1)(P)

            over_steps(pool, over_block, count, finish=lambda b_: scatter(b_)(P))
            pool.wait_ge(scattered, (count + E) * 16)
            pool.sem_inc(all_added, 1)

        @block.scalar
        def _(act_e):
            def copy_xT(t):
                if not has(t):
                    return
                u = t.slot(2)
                act_e.wait_ge(x_transposed, t.n + 1)
                wait(act_e, tok_done, t.n - 1)
                half = KX // 2
                for k in range(2):
                    act_e.copy(xT[u][:, k * half:(k + 1) * half, :],
                               p_xT[k][:, 0:half * R].rearrange("p (k r) -> p k r", r=R)).then_inc(xT_copied, 1)

            def copy_T(t, transposed, psum, to, used, copied):
                if not has(t):
                    return
                act_e.wait_ge(transposed, t.n + 1)
                wait(act_e, used, t.n - 1)
                act_e.copy(to[t.slot(2)][:, :, :], psum[:, 0:KD * R].rearrange("p (k r) -> p k r", r=R)).then_inc(copied, 1)

            def square(t):
                if not has(t):
                    return
                act_e.wait_ge(attn_done, t.n + 1)
                act_e.activation(attn_sq[0:R, :], p_attn[0:R, :], ACT.Square, scale=float(D) ** -0.5,
                                 accum_out=mean_sq[0:R, :]).then_inc(sq_done, 1)

            def exp(t):
                if not has(t):
                    return
                act_e.wait_ge(nmax_ready, t.n + 1)
                act_e.activation(ex[0:R, :], p_logits[0:R, 0:NE2], ACT.Exp, bias=nmax[0:R, :],
                                 accum_out=exsum[0:R, :]).then_inc(exp_done, 1)

            def normalise(t, used, ready, out_, in_, rs, nm, done, stored=None):
                if not has(t):
                    return
                act_e.wait_ge(ready, t.n + 1)
                wait(act_e, used, t.n - 1)
                if stored:
                    wait(act_e, stored[t.slot(2)], t.turn(2) * 16)
                act_e.activation(out_, in_, ACT.Identity, bias=nm[0:R, :], scale=rs[0:R, :]).then_inc(done, 1)

            def norm_x(t):
                u = t.slot(2)
                normalise(t, x_transposed, rs_x_ready, x1[u][0:R, :], xt[u][0:R, :], rs_x, nm_x, x_normed)

            def norm_h(t):
                u = t.slot(2)
                if has(t):
                    wait(act_e, hx_ready, t.n - 1)
                normalise(t, xn_transposed, rs_h_ready, xn[u][0:R, :], h[u][0:R, :], rs_h, nm_h, xn_ready)

            def norm_o(t):
                u = t.slot(2)
                normalise(t, xf_transposed, rs_o_ready, xf[u][0:R, 0:D], h2[u][0:R, :], rs_o, nm_o, xf_ready, xf_stored)

            def number_tokens(t):
                if not has(t):
                    return
                u = t.slot(2)
                act_e.wait_ge(hot_ready, t.n + 1)
                wait(act_e, numbers_moved, t.n)
                wait(act_e, table_done, t.n - 1)
                act_e.activation(id_lo[u][0:R, :, :, :], hot_lo[u][0:R, :, :, :], ACT.Copy, scale=token_id[0:R, :]).then_inc(id_ready, 1)

            def step(s):
                first = isinstance(s.i, int) and s.off == 0
                square(s + -2)
                number_tokens(s + -4)
                exp(s + -3)
                norm_h(s + -1)
                if not first:
                    norm_x(s + 2)
                copy_T(s + -1, xn_transposed, p_xnT, xnT, attn_done, xnT_copied)
                copy_xT(s + 1)
                norm_o(s + -2)
                copy_T(s + -2, xf_transposed, p_xfT, xfT, logits_done, xfT_copied)
                if first:
                    set_up()
                    norm_x(s + 2)

            def angles():
                act_e.wait_ge(angles_ready, 1)
                act_e.activation(s_cos, s_t1, ACT.Sin)
                act_e.activation(s_sin, s_t2, ACT.Sin).then_inc(sincos_ready, 1)

            def set_up():
                act_e.wait_ge(w_clsT_done, 1)
                act_e.copy(w_clsT[:, :, :], p_logits[:, 0:KD * NE2].rearrange("p (k n) -> p k n", k=KD)).then_inc(w_clsT_copied, 1)
                act_e.wait_ge(b1_part_ready, 1)
                for k in range(KS):
                    act_e.wait_ge(w_outT_done, k + 1)
                    act_e.copy(w_outT[:, k, :], p_woT[k % 2][:, :]).then_inc(w_outT_copied, 1)
                angles()
                for m in range(KD):
                    act_e.wait_ge(m_done, m + 1)
                    act_e.copy(m_hi[:, m, :], p_m[m % 2][:, :]).then_inc(m_hi_ready, 1)

            norm_x(Step(0, 0, 2))
            norm_x(Step(0, 1, 2))
            copy_xT(Step(0, 0, 2))
            act_e.wait_ge(ln1_loaded, 32)
            act_e.wait_ge(w_tok_loaded, 16)
            for k in range(KX):
                act_e.activation(w_hi[:, k, :], w_raw[:, k, :], ACT.Copy, scale=g1_col[:, k:k + 1]).then_inc(w_hi_ready, 1)
            tile_steps(act_e, step)

            def split_gate_up(b_):
                u, w, half = b_.slot(2), b_.slot(WRING), KD // 2
                act_e.wait_ge(wgu_loaded[w], b_.turn(WRING) * 16 + 16)
                wait(act_e, gu_done, b_.n - 1)
                for k in range(2):
                    act_e.copy(wgu_hi[u][:, k * half:(k + 1) * half, :], wgu[w][:, k * half:(k + 1) * half, :]).then_inc(wgu_hi_ready, 1)

            def split_down(b_):
                u, w = b_.slot(2), b_.slot(WRING)
                act_e.wait_ge(wdn_loaded[w], b_.turn(WRING) * 16 + 16)
                wait(act_e, down_done, b_.n - 1)
                act_e.copy(wdn_hi[u], wdn[w]).then_inc(wdn_hi_ready, 1)

            def copy_xeT(b_):
                u = b_.slot(2)
                act_e.wait_ge(xe_transposed, b_.n + 1)
                wait(act_e, gu_done, b_.n - 1)
                act_e.copy(xeT[u], p_xeT[u][:, :].rearrange("p (k s) -> p k s", k=KD)).then_inc(xeT_copied, 1)

            def copy_actT(b_):
                u = b_.slot(2)
                act_e.wait_ge(act_transposed, b_.n + 1)
                wait(act_e, down_done, b_.n - 1)
                act_e.copy(actT[u], p_actT[u][:, 0:KI * P].rearrange("p (k s) -> p k s", k=KI)).then_inc(actT_copied, 1)

            def silu_gate(b_):
                u = b_.slot(2)
                act_e.wait_ge(gu_done, b_.n + 1)
                wait(act_e, act_ready, b_.n - 1)
                act_e.activation(silu[u], p_gu[u][:, 0:I], ACT.Silu).then_inc(silu_done, 1)

            def weigh(b_, e):
                u = b_.slot(2)
                act_e.wait_ge(down_done, b_.n + 1)
                wait(act_e, scattered, (b_.n - YRING + 1) * 16)
                act_e.activation(y[b_.slot(YRING)], p_y[u][:, :], ACT.Copy, scale=xe[b_.slot(RING)][:, bass.ds(e + D, 1)]).then_inc(y_ready, 1)

            act_e.wait_ge(tok_done, TILES)
            act_e.wait_ge(attn_done, TILES)
            split_gate_up(Step(0, 0, RING))
            split_down(Step(0, 0, RING))
            copy_xeT(Step(0, 0, RING))

            act_e.wait_ge(list_ready, 1)
            count = over_count(act_e)

            def expert_step(e):
                if not isinstance(e.i, int) or e.off > 0:
                    copy_actT(e + -1)
                if_real(act_e, count, e + 1, split_gate_up)
                silu_gate(e)
                if_real(act_e, count, e + 1, copy_xeT)
                if not isinstance(e.i, int) or e.off > 0:
                    weigh(e + -1, (e + -1).n)
                if_real(act_e, count, e + 1, split_down)

            expert_steps(act_e, expert_step)

            def over_block(b_, j):
                copy_actT(b_ + -1)
                with act_e.If((j + 1).n < count):
                    split_gate_up(b_ + 1)
                with act_e.If(j.n < count):
                    silu_gate(b_)
                with act_e.If((j + 1).n < count):
                    copy_xeT(b_ + 1)
                weigh(b_ + -1, over_expert(act_e, j + -1))
                with act_e.If((j + 1).n < count):
                    split_down(b_ + 1)
                stand(act_e)

            def finish(b_):
                copy_actT(b_)
                weigh(b_, over_expert(act_e, Step(0, E - 1, RING)))

            over_steps(act_e, over_block, count, finish=finish)

        @block.vector
        def _(dve):
            def stats_x(t):
                if not has(t):
                    return
                u = t.slot(2)
                links = Links(dve, stats_x_links, t.n * 2)
                wait(dve, var_x_ready, t.n)
                dve.wait_ge(x_loaded[u], (t.turn(2) + 1) * 16 * 3)
                links(dve.bn_stats(st_x[0:R, 0, :], xt[u][0:R, 0:DIN // 2]))
                links(dve.bn_stats(st_x[0:R, 1, :], xt[u][0:R, DIN // 2:DIN]))

            def aggr_x(t):
                if not has(t):
                    return
                dve.wait_ge(stats_x_links, t.n * 2 + 2)
                wait(dve, rs_x_ready, t.n)
                stand(dve)
                dve.bn_aggr(mv_x[0:R, :], st_x[0:R, :, :].rearrange("p a b -> p (a b)")).then_inc(var_x_ready, 1)

            def low_x(t, k):
                if not has(t):
                    return
                dve.wait_ge(xT_copied, t.n * 2 + k + 1)
                wait(dve, tok_done, t.n)
                half = KX // 2
                dve.tensor_tensor(xT_lo[:, k * half:(k + 1) * half, :], p_xT[k][:, 0:half * R].rearrange("p (k r) -> p k r", r=R),
                                  xT[t.slot(2)][:, k * half:(k + 1) * half, :], ALU.subtract).then_inc(xT_lo_ready, 1)

            def low_xn(t):
                if not has(t):
                    return
                dve.wait_ge(xnT_copied, t.n + 1)
                wait(dve, attn_done, t.n)
                dve.tensor_tensor(xnT_lo[:, :, :], p_xnT[:, 0:KD * R].rearrange("p (k r) -> p k r", r=R),
                                  xnT[t.slot(2)][:, :, :], ALU.subtract).then_inc(xnT_lo_ready, 1)

            class NormH:

                def __init__(self, t):
                    self.t, self.u, self.links = t, t.slot(2), Links(dve, ln_h_links, t.n * 2)

                def stats(self):
                    dve.wait_ge(tok_done, self.t.n + 1)
                    self.links(dve.bn_stats(st_t[0:R, :], p_tok[0:R, :]))

                def aggregate(self):
                    self.links.after(1)
                    stand(dve)
                    dve.bn_aggr(mv_t[0:R, :], st_t[0:R, :]).then_inc(var_t_ready, 1)

                def centre(self):
                    dve.wait_ge(var_t_ready, self.t.n + 1)
                    dve.scalar_tensor_tensor(hc[0:R, :], p_tok[0:R, :], mv_t[0:R, 0:1], g2_all[0:R, :], ALU.subtract, ALU.mult).then_inc(tok_read, 1)

                def scale(self):
                    dve.wait_ge(rs_t_ready, self.t.n + 1)
                    dve.wait_ge(tok_read, self.t.n + 1)
                    wait(dve, hx_ready, self.t.n - 1)
                    dve.scalar_tensor_tensor(h[self.u][0:R, :], hc[0:R, :], rs_t[0:R, :], b2_all[0:R, :], ALU.mult, ALU.add).then_inc(h_ready, 1)

                def stats_of_h(self):
                    dve.wait_ge(h_ready, self.t.n + 1)
                    wait(dve, var_h_ready, self.t.n)
                    self.links(dve.bn_stats(st_h[0:R, :], h[self.u][0:R, :]))

                def aggregate_h(self):
                    self.links.after(2)
                    wait(dve, rs_h_ready, self.t.n)
                    stand(dve)
                    dve.bn_aggr(mv_h[0:R, :], st_h[0:R, :]).then_inc(var_h_ready, 1)

            class NormO:

                def __init__(self, t):
                    self.t, self.u, self.links = t, t.slot(2), Links(dve, ln_o_links, t.n)

                def scale(self):
                    dve.wait_ge(rs_a_ready, self.t.n + 1)
                    wait(dve, h2_ready, self.t.n)
                    dve.scalar_tensor_tensor(attn_n[0:R, :], p_attn[0:R, :], rs_a[0:R, :], nw_all[0:R, :], ALU.mult, ALU.mult).then_inc(attn_read, 1)

                def stats(self):
                    dve.wait_ge(h2_ready, self.t.n + 1)
                    wait(dve, var_o_ready, self.t.n)
                    self.links(dve.bn_stats(st_o[0:R, :], h2[self.u][0:R, :]))

                def aggregate(self):
                    self.links.after(1)
                    wait(dve, rs_o_ready, self.t.n)
                    stand(dve)
                    dve.bn_aggr(mv_o[0:R, :], st_o[0:R, :]).then_inc(var_o_ready, 1)

            class Route:

                def __init__(self, t):
                    self.t, self.u, self.links = t, t.slot(2), Links(dve, route_links, t.n * 11)

                def maximum(self):
                    dve.wait_ge(logits_done, self.t.n + 1)
                    dve.tensor_reduce(nmax[0:R, :], p_logits[0:R, 0:NE2], AX.X, ALU.max, negate=True).then_inc(nmax_ready, 1)

                def invert(self):
                    dve.wait_ge(exp_done, self.t.n + 1)
                    self.links(dve.reciprocal(exinv[0:R, :], exsum[0:R, :]))

                def bias(self):
                    self.links.after(1)
                    self.links(dve.scalar_tensor_tensor(ranked[0:R, :], ex[0:R, :], exinv[0:R, :], rb_all[0:R, :], ALU.mult, ALU.add))

                def best(self):
                    self.links.after(2)
                    stand(dve)
                    self.links(dve.max(top8[0:R, :], ranked[0:R, :]))

                def strike(self):
                    self.links.after(3)
                    stand(dve)
                    self.links(dve.match_replace(others[0:R, :], top8[0:R, :], ranked[0:R, :], -3.0e38))

                def choose(self):
                    self.links.after(4)
                    wait(dve, pos_done, self.t.n)
                    dve.tensor_tensor(mask[self.u][0:R, :], others[0:R, :], ranked[0:R, :], ALU.not_equal).then_inc(mask_ready, 1)

                def weights(self):
                    u = self.u
                    dve.wait_ge(mask_ready, self.t.n + 1)
                    if isinstance(self.t.i, int) and self.t.off == 0:
                        self.links(dve.tensor_copy(mask_sum[u][0:R, :], mask[u][0:R, 0:E]))
                    else:
                        self.links(dve.tensor_tensor(mask_sum[u][0:R, :], mask_sum[1 - u][0:R, :], mask[u][0:R, 0:E], ALU.add))
                    wait(dve, wts_ready, self.t.n)
                    self.links(dve.scalar_tensor_tensor(wsel[0:R, 0:E], ex[0:R, 0:E], exinv[0:R, :], mask[u][0:R, 0:E], ALU.mult, ALU.mult,
                                                        accum_out=wreal[0:R, :]))
                    self.links(dve.scalar_tensor_tensor(wsel[0:R, E:NE2], ex[0:R, E:NE2], exinv[0:R, :], mask[u][0:R, E:NE2], ALU.mult, ALU.mult,
                                                        accum_out=wzero[0:R, :]))

                def total(self):
                    self.links.after(7)
                    self.links(dve.tensor_scalar(wsum[0:R, :], wreal[0:R, :], wzero[0:R, :], 1e-20, ALU.add, ALU.add))

                def invert_total(self):
                    self.links.after(8)
                    self.links(dve.reciprocal(winv[0:R, :], wsum[0:R, :]))

                def zero_weight(self):
                    self.links.after(9)
                    self.links(dve.tensor_scalar(wzn[0:R, :], wzero[0:R, :], winv[0:R, :], SCALE, ALU.mult, ALU.mult))

                def factor(self):
                    self.links.after(10)
                    self.links(dve.tensor_scalar(wfac[0:R, :], wzn[0:R, :], 1.0, winv[0:R, :], ALU.add, ALU.mult))

                def write(self):
                    self.links.after(11)
                    wait(dve, xf_stored[self.u], self.t.turn(2) * 16)
                    dve.tensor_scalar(xf[self.u][0:R, D:ROW], wsel[0:R, 0:E], wfac[0:R, :], SCALE, ALU.mult, ALU.mult).then_inc(wts_ready, 1)

            class Slots:

                def __init__(self, t):
                    self.t, self.u, self.links = t, t.slot(2), Links(dve, pos_links, t.n * 4)

                def read(self):
                    dve.wait_ge(pos_done, self.t.n + 1)
                    self.links(dve.scalar_tensor_tensor(kept[0:R, :], p_pos[0:R, :], float(CAP), mask[self.u][0:R, 0:E], ALU.is_lt, ALU.mult))
                    dve.tensor_copy(pos_i[0:R, :], p_pos[0:R, :]).then_inc(pos_read, 1)

                def high(self):
                    dve.wait_ge(pos_read, self.t.n + 1)
                    self.links(dve.tensor_scalar(hi_i[0:R, :], pos_i[0:R, :], LO.bit_length() - 1, None, ALU.arith_shift_right))

                def low(self):
                    self.links.after(2)
                    wait(dve, hot_ready, self.t.n)
                    self.links(dve.scalar_tensor_tensor(lo[0:R, :], hi_i[0:R, :], float(-LO), pos_i[0:R, :], ALU.mult, ALU.add))
                    self.links(dve.scalar_tensor_tensor(hi1[0:R, :], hi_i[0:R, :], 1.0, kept[0:R, :], ALU.add, ALU.mult))

                def hot(self, out_, iota, part, axis, grid):
                    wide = part[0:R, :].rearrange("p (g e) -> p g e", e=EG).unsqueeze(axis).to_broadcast(grid)
                    return dve.tensor_tensor(out_[self.u][0:R, :, :, :], iota[0:R, :, :, :], wide, ALU.is_equal)

                def hot_low(self):
                    self.links.after(4)
                    wait(dve, table_done, self.t.n - 1)
                    wait(dve, id_ready, self.t.n - 1)
                    self.hot(hot_lo, iota_lo, lo, 2, [R, GROUPS, LO, EG])

                def hot_high(self):
                    self.hot(hot_hi, iota_hi1, hi1, 3, [R, GROUPS, EG, HI]).then_inc(hot_ready, 1)

            def step(s):
                first = isinstance(s.i, int) and s.off == 0
                norm_h, norm_o = has(s) and NormH(s), has(s + -2) and NormO(s + -2)
                route, slots = has(s + -3) and Route(s + -3), has(s + -3) and Slots(s + -3)
                if not first:
                    stats_x(s + 2)
                if route:
                    route.maximum()
                if not first:
                    aggr_x(s + 2)
                if norm_o:
                    norm_o.scale()
                if route:
                    route.invert()
                    route.bias()
                if route:
                    route.best()
                if route:
                    route.strike()
                    route.choose()
                    route.weights()
                    route.total()
                if first:
                    set_up()
                if norm_h:
                    norm_h.stats()
                if route:
                    route.invert_total()
                if norm_o:
                    norm_o.stats()
                if norm_h:
                    norm_h.aggregate()
                low_xn(s + -1)
                if norm_o:
                    norm_o.aggregate()
                if route:
                    route.zero_weight()
                low_x(s + 1, 0)
                if route:
                    route.factor()
                if norm_h:
                    norm_h.centre()
                if route:
                    slots.read()
                low_x(s + 1, 1)
                if route:
                    slots.high()
                    route.write()
                if norm_h:
                    norm_h.scale()
                if route:
                    slots.low()
                if norm_h:
                    norm_h.stats_of_h()
                if route:
                    slots.hot_low()
                if norm_h:
                    norm_h.aggregate_h()
                if route:
                    slots.hot_high()
                if first:
                    set_up_end()
                    stats_x(s + 2)
                    aggr_x(s + 2)

            def weighted_sum(out_, blocks, column, count, ready, before_it):
                links = Links(dve, part_links, before_it)
                links.chain(dve.tensor_scalar(out_, blocks[:, 0, :], column[:, 0:1], None, ALU.mult))
                for k in range(1, count):
                    last = dve.scalar_tensor_tensor(out_, blocks[:, k, :], column[:, k:k + 1], out_, ALU.mult, ALU.add)
                    if k < count - 1:
                        links.chain(last)
                last.then_inc(ready, 1)

            def set_up_end():
                for m in range(KD):
                    dve.wait_ge(m_hi_ready, m + 1)
                    dve.tensor_tensor(m_lo[:, m, :], p_m[m % 2][:, :], m_hi[:, m, :], ALU.subtract).then_inc(m_lo_ready, 1)
                    if m == 1:
                        dve.wait_ge(state_done, 1)
                        dve.tensor_copy(state_rows[:, :], p_xnT[:, :]).then_inc(state_ready, 1)
                        dve.wait_ge(state_ready, 1)
                        dve.tensor_tensor(state_rows[P // 2:P, :], p_xnT[P // 2:P, :], state_rows[P // 2:P, :], ALU.subtract).then_inc(state_ready, 1)

            def set_up():
                links = Links(dve, setup_links, 0)
                dve.wait_ge(state_loaded, 16 * 5)
                dve.wait_ge(consts_made, 1)
                links.chain(dve.tensor_scalar(same_i[:, :], same_i[:, :], HI.bit_length() - 1, None, ALU.arith_shift_right))
                links.chain(dve.tensor_scalar(same_expert[:, :], same_i[:, :], 0.0, None, ALU.is_equal))
                links.chain(dve.tensor_tensor(s_br, s_br, s_cr, ALU.mult))
                links.chain(dve.tensor_tensor(s_bi, s_bi, s_ci, ALU.mult))
                links.chain(dve.tensor_tensor(s_br, s_br, s_bi, ALU.subtract))
                links.chain(dve.tensor_reduce(gain[:, :], s_br, AX.X, ALU.add))
                dve.wait_ge(w_in_loaded, 16)
                for k in range(KS):
                    last = dve.tensor_scalar(w_in_sb[:, k, :], w_in_sb[:, k, :], gain[:, k:k + 1], None, ALU.mult)
                last.then_inc(w_in_scaled, 1)
                dve.wait_ge(rows_loaded, 16 * 5)
                dve.wait_ge(b1_done, 1)
                links.chain(dve.tensor_tensor(b_all, p_xnT[:, :], b_all, ALU.add))
                links.chain(dve.tensor_copy(b_rows[:, :], b_all))
                dve.tensor_tensor(b_rows[P // 2:P, :], b_all[P // 2:P, :], b_rows[P // 2:P, :], ALU.subtract).then_inc(b_ready, 1)
                links.chain(dve.tensor_scalar(turns[:, :, :], theta, 0.5 / PI, None, ALU.mult))
                links.chain(dve.scalar_tensor_tensor(s_t2, turns[:, :, :], -2 * PI, theta, ALU.mult, ALU.add))
                links.chain(dve.tensor_scalar(s_t2, s_t2, -PI, PI, ALU.max, ALU.min))
                links.chain(dve.scalar_tensor_tensor(s_t1, s_t2, -1.0, s_t2, ALU.mult, ALU.max))
                dve.tensor_scalar(s_t1, s_t1, -1.0, PI / 2, ALU.mult, ALU.add).then_inc(angles_ready, 1)
                dve.wait_ge(sincos_ready, 1)
                links.chain(dve.tensor_scalar(s_t1, s_sin, 0.0, None, ALU.mult))
                links.chain(dve.scalar_tensor_tensor(s_t2, s_cos, 0.0, s_t1, ALU.mult, ALU.subtract))
                links.chain(dve.scalar_tensor_tensor(s_t1, s_cos, 0.0, s_t1, ALU.mult, ALU.add))
                links.chain(dve.tensor_tensor(s_t2, s_t2, s_cr, ALU.mult))
                links.chain(dve.tensor_tensor(s_t1, s_t1, s_ci, ALU.mult))
                links.chain(dve.tensor_tensor(s_t2, s_t2, s_t1, ALU.subtract))
                links.chain(dve.tensor_reduce(rest[:, :], s_t2, AX.X, ALU.add))
                dve.wait_ge(w_outT_copied, KS)
                weighted_sum(rest_part, w_outT, rest, KS, rest_ready, 0 + KX - 1)

            stats_x(Step(0, 0, 2))
            aggr_x(Step(0, 0, 2))
            stats_x(Step(0, 1, 2))
            aggr_x(Step(0, 1, 2))
            low_x(Step(0, 0, 2), 0)
            low_x(Step(0, 0, 2), 1)
            dve.wait_ge(ln1_loaded, 32)
            for k in range(KX):
                dve.wait_ge(w_hi_ready, k + 1)
                dve.scalar_tensor_tensor(w_lo[:, k, :], w_raw[:, k, :], g1_col[:, k:k + 1], w_hi[:, k, :], ALU.mult, ALU.subtract).then_inc(w_lo_ready, 1)
            dve.wait_ge(consts_made, 1)
            dve.tensor_scalar(halves[:, :], ones_f, 2.0 / P, None, ALU.mult).then_inc(halves_ready, 1)
            weighted_sum(b1_part, w_raw, b1_col, KX, b1_part_ready, 0)
            tile_steps(dve, step)

            links = Links(dve, tail_links, 0)
            dve.wait_ge(count_done, 1)
            links.chain(dve.tensor_scalar(many[:, :], p_tok[0:1, 0:E], float(FEW), None, ALU.is_gt))
            links.chain(dve.tensor_scalar(over[:, :], p_tok[0:1, 0:E], float(P), None, ALU.is_gt))
            links.chain(dve.tensor_tensor_scan(over_sum[:, :], ones_e[:, :], over[:, :], 0.0, ALU.mult, ALU.add))
            links.chain(dve.tensor_tensor(over_rank[:, :], over_sum[:, :], over[:, :], ALU.mult))
            links.chain(dve.tensor_copy(over_list[:, E + RING + 1:E + RING + 2], over_sum[:, E - 1:E]))
            dve.wait_ge(table_done, TILES)
            links.chain(dve.tensor_tensor(tmp_tbl.rearrange("p (a e) -> p a e", e=EG), p_table[:, :].rearrange("p (a e) -> p a e", e=EG),
                                    same_expert[:, :].unsqueeze(1).to_broadcast([P, GROUPS * LO, EG]), ALU.mult))
            dve.tensor_reduce(tbl_part[:, :, :], tmp_tbl.rearrange("p (g l e) -> p g l e", g=GROUPS, e=EG),
                              AX.X, ALU.add).then_inc(tbl_ready, 1)
            grid = [1, E, E]
            links.chain(dve.tensor_tensor(over_at.rearrange("o (r e) -> o r e", e=E), iota_e1[:, :].unsqueeze(2).to_broadcast(grid),
                                    over_rank[:, :].unsqueeze(1).to_broadcast(grid), ALU.is_equal))
            links.chain(dve.tensor_tensor(over_id.rearrange("o (r e) -> o r e", e=E), over_at.rearrange("o (r e) -> o r e", e=E),
                                    iota_e[:, :].unsqueeze(1).to_broadcast(grid), ALU.mult))
            links.chain(dve.tensor_reduce(over[:, :], over_id.rearrange("o (r e) -> o r e", e=E), AX.X, ALU.add))
            links.chain(dve.tensor_copy(over_list[:, 1:E + 1], over[:, :]))
            dve.wait_ge(tbl_transposed, 1)
            links.chain(dve.tensor_scalar(unused, p_logits[:, 0:E * HALVES], 0.0, spare_row[:, :], ALU.is_equal, ALU.mult))
            dve.scalar_tensor_tensor(slot_row[:, :], p_logits[:, 0:E * HALVES], -1.0, unused, ALU.add, ALU.add).then_inc(slots_ready, 1)
            dve.sem_inc(list_ready, 1)

            def gate_times_up(b_):
                u = b_.slot(2)
                dve.wait_ge(silu_done, b_.n + 1)
                wait(dve, act_transposed, b_.n - 1)
                dve.tensor_tensor(act[u], silu[u], p_gu[u][:, I:2 * I], ALU.mult).then_inc(act_ready, 1)

            def low_gate_up(b_, k):
                u, w, half = b_.slot(2), b_.slot(WRING), slice(k * KD // 2, (k + 1) * KD // 2)
                dve.wait_ge(wgu_hi_ready, b_.n * 2 + k + 1)
                dve.tensor_tensor(wgu_lo[u][:, half, :], wgu[w][:, half, :], wgu_hi[u][:, half, :], ALU.subtract).then_inc(wgu_lo_ready, 1)

            def low_down(b_):
                u, w = b_.slot(2), b_.slot(WRING)
                dve.wait_ge(wdn_hi_ready, b_.n + 1)
                dve.tensor_tensor(wdn_lo[u], wdn[w], wdn_hi[u], ALU.subtract).then_inc(wdn_lo_ready, 1)

            def low_xeT(b_):
                u = b_.slot(2)
                dve.wait_ge(xeT_copied, b_.n + 1)
                dve.tensor_tensor(xeT_lo[u], p_xeT[u][:, :].rearrange("p (k s) -> p k s", k=KD), xeT[u], ALU.subtract).then_inc(xeT_lo_ready, 1)

            def low_actT(b_):
                u = b_.slot(2)
                dve.wait_ge(actT_copied, b_.n + 1)
                dve.tensor_tensor(actT_lo[u], p_actT[u][:, 0:KI * P].rearrange("p (k s) -> p k s", k=KI), actT[u], ALU.subtract).then_inc(actT_lo_ready, 1)

            first = Step(0, 0, RING)
            low_gate_up(first, 0)
            low_gate_up(first, 1)
            low_xeT(first)

            count = over_count(dve)

            def expert_step(e):
                if not isinstance(e.i, int) or e.off > 0:
                    low_actT(e + -1)
                low_down(e)
                if_real(dve, count, e + 1, lambda b_: low_gate_up(b_, 0))
                gate_times_up(e)
                if_real(dve, count, e + 1, lambda b_: (low_gate_up(b_, 1), low_xeT(b_)))

            expert_steps(dve, expert_step)

            def over_block(b_, j):
                low_actT(b_ + -1)
                with dve.If(j.n < count):
                    low_down(b_)
                with dve.If((j + 1).n < count):
                    low_gate_up(b_ + 1, 0)
                with dve.If(j.n < count):
                    gate_times_up(b_)
                with dve.If((j + 1).n < count):
                    low_gate_up(b_ + 1, 1)
                    low_xeT(b_ + 1)
                stand(dve)

            over_steps(dve, over_block, count, finish=low_actT)

        @block.tensor
        def _(pe):
            def transpose_x(t):
                if not has(t):
                    return
                pe.wait_ge(x_normed, t.n + 1)
                wait(pe, xT_copied, t.n * 2)
                wait(pe, xT_lo_ready, t.n * 2)
                half = KX // 2
                for k in range(KX):
                    last = pe.transpose(p_xT[k // half][:, (k % half) * R:(k % half + 1) * R],
                                        x1[t.slot(2)][0:R, k:DIN:KX], ident[0:R, 0:R])
                last.then_inc(x_transposed, 1)

            def transpose_d(t, ready, source, psum, copied, done):
                if not has(t):
                    return
                pe.wait_ge(ready, t.n + 1)
                for each in copied:
                    wait(pe, each, t.n)
                for k in range(KD):
                    last = pe.transpose(psum[:, k * R:(k + 1) * R], source[t.slot(2)][0:R, k * P:(k + 1) * P], ident[0:R, 0:R])
                last.then_inc(done, 1)

            def embed(t, first, last_):
                if not has(t):
                    return
                u, start_up = t.slot(2), isinstance(t.i, int) and t.off == 0
                for n in range(first, last_):
                    part, k = divmod(n, KX)
                    if n == 0:
                        pe.wait_ge(xT_copied, t.n * 2 + 2)
                        wait(pe, tok_read, t.n)
                    if start_up and part < 2:
                        pe.wait_ge((w_hi_ready, w_lo_ready)[part], k + 1)
                    if n == 2 * KX:
                        pe.wait_ge(xT_lo_ready, t.n * 2 + 2)
                    pe.matmul(p_tok[:, :], (xT_lo if part == 2 else xT[u])[:, k, :], (w_lo if part == 1 else w_hi)[:, k, :],
                              start=(n == 0), stop=False)

            def add_bias(t):
                if not has(t):
                    return
                pe.matmul(p_tok[:, :], halves[:, :], b_rows[:, :], start=False, stop=True).then_inc(tok_done, 1)

            def mix(t):
                if not has(t):
                    return
                u = t.slot(2)
                pe.wait_ge(xnT_copied, t.n + 1)
                wait(pe, attn_read, t.n)
                if isinstance(t.i, int) and t.off == 0:
                    pe.wait_ge(m_lo_ready, KD)
                pe.matmul(p_attn[:, :], halves[:, :], state_rows[:, :], start=True, stop=False)
                for part in range(3):
                    if part == 2:
                        pe.wait_ge(xnT_lo_ready, t.n + 1)
                    for k in range(KD):
                        last = pe.matmul(p_attn[:, :], (xnT_lo if part == 2 else xnT[u])[:, k, :], (m_lo if part == 1 else m_hi)[:, k, :],
                                         start=False, stop=(part == 2 and k == KD - 1))
                last.then_inc(attn_done, 1)

            def logits(t):
                if not has(t):
                    return
                pe.wait_ge(xfT_copied, t.n + 1)
                wait(pe, exp_done, t.n)
                for k in range(KD):
                    last = pe.matmul(p_logits[0:R, 0:NE2], xfT[t.slot(2)][:, k, :], w_clsT[:, k, :], start=(k == 0), stop=(k == KD - 1))
                last.then_inc(logits_done, 1)

            def positions(t):
                if not has(t):
                    return
                first = isinstance(t.i, int) and t.off == 0
                pe.wait_ge(mask_ready, t.n + 1)
                last = pe.matmul(p_pos[0:R, :], before[0:R, 0:R], mask[t.slot(2)][0:R, 0:E], start=True, stop=first)
                if not first:
                    last = pe.matmul(p_pos[0:R, :], ones[0:R, 0:R], mask_sum[1 - t.slot(2)][0:R, :], start=False, stop=True)
                last.then_inc(pos_done, 1)

            def table(t):
                if not has(t):
                    return
                final = isinstance(t.i, int) and t.off == TILES - 1
                rows, u = RLAST if final else R, t.slot(2)
                pe.wait_ge(id_ready, t.n + 1)
                for g in range(GROUPS):
                    last = pe.matmul(p_table[:, g * P:(g + 1) * P], hot_hi[u][0:rows, g, :, :].rearrange("p l e -> p (l e)"),
                                     id_lo[u][0:rows, g, :, :].rearrange("p l e -> p (l e)"),
                                     start=False, stop=final, skip_group_check=True)
                last.then_inc(table_done, 1)

            def step(s):
                embed(s, 0, KX)
                if has(s + -4):
                    pe.wait_ge(pos_read, (s + -4).n + 1)
                logits(s + -3)
                embed(s, KX, 3 * KX)
                if not (isinstance(s.i, int) and s.off == 0):
                    add_bias(s)
                transpose_d(s + -1, xn_ready, xn, p_xnT, (xnT_copied, xnT_lo_ready), xn_transposed)
                transpose_x(s + 1)
                positions(s + -3)
                table(s + -4)
                mix(s + -1)
                transpose_d(s + -2, xf_ready, xf, p_xfT, (xfT_copied,), xf_transposed)

            def set_up():
                pe.wait_ge(w_cls_loaded, 16)
                for k in range(KD):
                    last = pe.transpose(p_logits[:, k * NE2:(k + 1) * NE2], w_cls_sb[:, k * P:(k + 1) * P], ident[0:NE2, 0:NE2])
                last.then_inc(w_clsT_done, 1)
                pe.wait_ge(w_out_loaded, 16)
                for k in range(KS):
                    if k == 0:
                        pe.wait_ge(w_clsT_copied, 1)
                    if k >= 2:
                        pe.wait_ge(w_outT_copied, k - 1)
                    for m in range(KD):
                        last = pe.transpose(p_woT[k % 2][:, m * P:(m + 1) * P], w_out_sb[:, m, k:NS:KS], ident[:, :])
                    last.then_inc(w_outT_done, 1)
                pe.wait_ge(b1_part_ready, 1)
                pe.matmul(p_xnT[:, :], ones_f, b1_part, start=True, stop=True).then_inc(b1_done, 1)
                pe.wait_ge(b_ready, 1)
                pe.wait_ge(halves_ready, 1)
                add_bias(Step(0, 0, 2))
                pe.wait_ge(w_outT_copied, KS)
                pe.wait_ge(w_in_scaled, 1)
                for m in range(KD):
                    if m >= 2:
                        pe.wait_ge(m_lo_ready, m - 1)
                    if m == 2:
                        pe.wait_ge(rest_ready, 1)
                        pe.matmul(p_xnT[:, :], ones_f, rest_part, start=True, stop=True).then_inc(state_done, 1)
                        pe.wait_ge(zeros_made, 1)
                        pe.matmul(p_table[:, :], zero_row[:, 0:P], zero_row[:, 0:GROUPS * P], start=True, stop=False, skip_group_check=True)
                    for k in range(KS):
                        last = pe.matmul(p_m[m % 2][:, :], w_in_sb[:, k, m * P:(m + 1) * P], w_outT[:, k, :],
                                         start=(k == 0), stop=(k == KS - 1))
                    last.then_inc(m_done, 1)
                pe.wait_ge(state_ready, 2)

            pe.wait_ge(consts_made, 1)
            transpose_x(Step(0, 0, 2))
            tile_steps(pe, step, set_up)
            last_u = (TILES - 1) % 2
            pe.matmul(p_tok[0:32, 0:E], ones[0:R, 0:32], mask_sum[1 - last_u][0:R, :], start=True, stop=False)
            pe.matmul(p_tok[0:32, 0:E], ones[0:RLAST, 0:32], mask[last_u][0:RLAST, 0:E], start=False, stop=True).then_inc(count_done, 1)
            pe.wait_ge(tbl_loaded, 16)
            pe.transpose(p_logits[:, 0:E * HALVES], tbl_rows, ident[0:E * HALVES, 0:E * HALVES]).then_inc(tbl_transposed, 1)

            def transpose_xe(b_):
                u, r = b_.slot(2), b_.slot(RING)
                pe.wait_ge(gathered[r], b_.turn(RING) * 16 + 16)
                wait(pe, xeT_lo_ready, b_.n - 1)
                for k in range(KD):
                    last = pe.transpose(p_xeT[u][:, k * P:(k + 1) * P], xe[r][:, k * P:(k + 1) * P], ident[:, :])
                last.then_inc(xe_transposed, 1)

            def gate_up(b_):
                u = b_.slot(2)
                pe.wait_ge(xeT_copied, b_.n + 1)
                wait(pe, act_ready, b_.n - 1)
                for part in range(3):
                    if part == 1:
                        pe.wait_ge(xeT_lo_ready, b_.n + 1)
                    for k in range(KD):
                        if part == 0 and k % (KD // 2) == 0:
                            pe.wait_ge(wgu_hi_ready, b_.n * 2 + k // (KD // 2) + 1)
                        if part == 2 and k == 0:
                            pe.wait_ge(wgu_lo_ready, b_.n * 2 + 2)
                        last = pe.matmul(p_gu[u][:, :], (xeT_lo if part == 1 else xeT)[u][:, k, :], (wgu_lo if part == 2 else wgu_hi)[u][:, k, :],
                                         start=(part == 0 and k == 0), stop=(part == 2 and k == KD - 1))
                last.then_inc(gu_done, 1)

            def transpose_act(b_):
                u = b_.slot(2)
                pe.wait_ge(act_ready, b_.n + 1)
                wait(pe, actT_lo_ready, b_.n - 1)
                for k in range(KI):
                    last = pe.transpose(p_actT[u][:, k * P:(k + 1) * P], act[u][:, k * P:(k + 1) * P], ident[:, :])
                last.then_inc(act_transposed, 1)

            def down(b_):
                u = b_.slot(2)
                pe.wait_ge(actT_copied, b_.n + 1)
                pe.wait_ge(wdn_hi_ready, b_.n + 1)
                wait(pe, y_ready, b_.n - 1)
                for part in range(3):
                    if part == 1:
                        pe.wait_ge(actT_lo_ready, b_.n + 1)
                    if part == 2:
                        pe.wait_ge(wdn_lo_ready, b_.n + 1)
                    for k in range(KI):
                        last = pe.matmul(p_y[u][:, :], (actT_lo if part == 1 else actT)[u][:, k, :], (wdn_lo if part == 2 else wdn_hi)[u][:, k, :],
                                         start=(part == 0 and k == 0), stop=(part == 2 and k == KI - 1))
                last.then_inc(down_done, 1)

            transpose_xe(Step(0, 0, RING))

            pe.wait_ge(list_ready, 1)
            count = over_count(pe)

            def expert_step(e):
                gate_up(e)
                if_real(pe, count, e + 1, transpose_xe)
                if not isinstance(e.i, int) or e.off > 0:
                    down(e + -1)
                transpose_act(e)

            expert_steps(pe, expert_step)

            def over_block(b_, j):
                with pe.If(j.n < count):
                    gate_up(b_)
                with pe.If((j + 1).n < count):
                    transpose_xe(b_ + 1)
                down(b_ + -1)
                with pe.If(j.n < count):
                    transpose_act(b_)
                stand(pe)

            over_steps(pe, over_block, count, finish=down)


_INS = ['x', 'L0_tok_W', 'L0_tok_b', 'L0_tok_g1', 'L0_tok_b1', 'L0_tok_g2', 'L0_tok_b2', 'L0_attn_W_in',
        'L0_attn_W_out', 'L0_attn_A_theta', 'L0_attn_B_real', 'L0_attn_B_imag', 'L0_attn_C_real',
        'L0_attn_C_imag', 'L0_attn_norm_w', 'L0_ffn_w_cls', 'L0_ffn_bias', 'L0_ffn_w_gate_up', 'L0_ffn_w_down']
_OUTS = [((64, 23, 512), 'float32')]


def kernel(**inputs):
    import numpy as _np
    import concourse.bacc as _bacc
    from concourse import mybir as _mybir
    from concourse.bass_utils import run_bass_kernel_spmd as _run

    nc = _bacc.Bacc("TRN2", target_bir_lowering=False, num_devices=1)
    arrays, args = {}, []
    for name in _INS:
        a = _np.ascontiguousarray(inputs[name])
        arrays[f"in_{name}_dram"] = a
        args.append(nc.dram_tensor(f"in_{name}_dram", a.shape, _mybir.dt.from_np(a.dtype), kind="ExternalInput").ap())
    for i, (shape, dtype) in enumerate(_OUTS):
        dt = _mybir.dt.from_np(_np.dtype(dtype))
        args.append(nc.dram_tensor(f"out_{i}_dram", shape, dt, kind="ExternalOutput").ap())
    audio_tower(nc, *args)
    r = _run(nc, [arrays], core_ids=[0])
    return r.results[0]["out_0_dram"]
```
